# Optimizing a Trainium2 kernel written in Bass

```python
import numpy as np
import jax
import jax.numpy as jnp

def _softmax(x, axis=-1):
    return jax.nn.softmax(x, axis=axis)

def _gelu(x):
    return jax.nn.gelu(x, approximate=True)

def _silu(x):
    return jax.nn.silu(x)

def _sigmoid(x):
    return jax.nn.sigmoid(x)

def _layernorm(x, axis=-1, eps=1e-05):
    m = jnp.mean(x, axis=axis, keepdims=True)
    v = jnp.var(x, axis=axis, keepdims=True)
    return (x - m) / jnp.sqrt(v + eps)

def _scatter_add(tgt, idx, src, axis=0):
    return tgt.at[idx].add(src)

def _segment_sum(src, seg, n):
    return jax.ops.segment_sum(src, seg, n)
kernel_name = 'mk_macaron_d1_jaxref_r8_fdc018'

def setup_inputs(seed: int=0):
    np.random.seed(seed)
    _w = jnp.asarray

    def _L0_attn_setup():
        import jax, jax.numpy as jnp
        import numpy as np
        D_MODEL = 256
        N_HEADS = 16
        HEAD_DIM = D_MODEL // N_HEADS
        key = jax.random.key(seed)
        ks = jax.random.split(key, 5)
        b, l, d = (2, 256, D_MODEL)
        x = jax.random.normal(ks[0], (b, l, d), dtype=jnp.float32)
        s_qkv = 1.0 / np.sqrt(d)
        W_qkv = jax.random.uniform(ks[1], (3 * d, d), dtype=jnp.float32, minval=-s_qkv, maxval=s_qkv)
        b_qkv = jax.random.uniform(ks[2], (3 * d,), dtype=jnp.float32, minval=-s_qkv, maxval=s_qkv)
        W_out = jax.random.uniform(ks[3], (d, d), dtype=jnp.float32, minval=-s_qkv, maxval=s_qkv)
        b_out = jax.random.uniform(ks[4], (d,), dtype=jnp.float32, minval=-s_qkv, maxval=s_qkv)
        return {'x': x, 'W_qkv': W_qkv, 'b_qkv': b_qkv, 'W_out': W_out, 'b_out': b_out}
    _L0_attn_in = _L0_attn_setup()

    def _L0_ffn_setup():
        import jax, jax.numpy as jnp
        import numpy as np
        HIDDEN = 256
        N_EXPERTS = 8
        N_SHARED = 2
        TOP_K = 2
        MOE_FF = 176
        SHARED_FF = N_SHARED * MOE_FF
        SCALE = 2.5
        BATCH, SEQ = (2, 128)
        key = jax.random.key(seed)
        ks = jax.random.split(key, 8)
        s = 0.02
        return {'hidden_states': jax.random.normal(ks[0], (BATCH, SEQ, HIDDEN), jnp.float32), 'gate_w': jax.random.normal(ks[1], (N_EXPERTS, HIDDEN), jnp.float32) * s, 'shared_wg': jax.random.normal(ks[2], (SHARED_FF, HIDDEN), jnp.float32) * s, 'shared_wu': jax.random.normal(ks[3], (SHARED_FF, HIDDEN), jnp.float32) * s, 'shared_wd': jax.random.normal(ks[4], (HIDDEN, SHARED_FF), jnp.float32) * s, 'exp_wg': jax.random.normal(ks[5], (N_EXPERTS, MOE_FF, HIDDEN), jnp.float32) * s, 'exp_wu': jax.random.normal(ks[6], (N_EXPERTS, MOE_FF, HIDDEN), jnp.float32) * s, 'exp_wd': jax.random.normal(ks[7], (N_EXPERTS, HIDDEN, MOE_FF), jnp.float32) * s}
    _L0_ffn_in = _L0_ffn_setup()
    _d = {'L0_attn_x': _L0_attn_in['x'], 'L0_attn_W_qkv': _L0_attn_in['W_qkv'], 'L0_attn_b_qkv': _L0_attn_in['b_qkv'], 'L0_attn_W_out': _L0_attn_in['W_out'], 'L0_attn_b_out': _L0_attn_in['b_out'], 'L0_ffn_gate_w': _L0_ffn_in['gate_w'], 'L0_ffn_shared_wg': _L0_ffn_in['shared_wg'], 'L0_ffn_shared_wu': _L0_ffn_in['shared_wu'], 'L0_ffn_shared_wd': _L0_ffn_in['shared_wd'], 'L0_ffn_exp_wg': _L0_ffn_in['exp_wg'], 'L0_ffn_exp_wu': _L0_ffn_in['exp_wu'], 'L0_ffn_exp_wd': _L0_ffn_in['exp_wd']}
    _x0 = _d['L0_attn_x']
    _d['L0_attn_x'] = jax.random.normal(jax.random.fold_in(jax.random.key(seed), 1), (4, 1024, 256), dtype=_x0.dtype)
    del _x0
    return _d

def reference(L0_attn_x, L0_attn_W_qkv, L0_attn_b_qkv, L0_attn_W_out, L0_attn_b_out, L0_ffn_gate_w, L0_ffn_shared_wg, L0_ffn_shared_wu, L0_ffn_shared_wd, L0_ffn_exp_wg, L0_ffn_exp_wu, L0_ffn_exp_wd):

    def _L0_attn_ref(x, W_qkv, b_qkv, W_out, b_out):
        import jax, jax.numpy as jnp
        import numpy as np
        D_MODEL = 256
        N_HEADS = 16
        HEAD_DIM = D_MODEL // N_HEADS
        b, l, d = x.shape
        h, e = (N_HEADS, HEAD_DIM)
        qkv = x @ W_qkv.T + b_qkv
        q, k, v = jnp.split(qkv, 3, axis=-1)
        q = q.reshape(b, l, h, e)
        k = k.reshape(b, l, h, e)
        v = v.reshape(b, l, h, e)
        scale = 1.0 / jnp.sqrt(jnp.float32(e))
        scores = jnp.einsum('bqhe,bkhe->bhqk', q, k) * scale
        causal = jnp.tril(jnp.ones((l, l), dtype=bool))
        scores = jnp.where(causal[None, None], scores, -jnp.inf)
        attn = jax.nn.softmax(scores, axis=-1)
        out = jnp.einsum('bhqk,bkhe->bqhe', attn, v)
        out = out.reshape(b, l, d)
        out = out @ W_out.T + b_out
        return out

    def _L0_ffn_ref(hidden_states, gate_w, shared_wg, shared_wu, shared_wd, exp_wg, exp_wu, exp_wd):
        import jax, jax.numpy as jnp
        import numpy as np
        HIDDEN = 256
        N_EXPERTS = 8
        N_SHARED = 2
        TOP_K = 2
        MOE_FF = 176
        SHARED_FF = N_SHARED * MOE_FF
        SCALE = 2.5
        BATCH, SEQ = (2, 128)
        B, S, D = hidden_states.shape
        T = B * S
        xf = hidden_states.reshape(T, D)
        scores = jax.nn.sigmoid(xf @ gate_w.T)
        topk_w, topk_idx = jax.lax.top_k(scores, TOP_K)
        topk_w = topk_w / (topk_w.sum(axis=-1, keepdims=True) + 1e-20)
        topk_w = topk_w * SCALE
        shared_out = jax.nn.silu(xf @ shared_wg.T) * (xf @ shared_wu.T) @ shared_wd.T
        h = jax.nn.silu(jnp.einsum('td,efd->etf', xf, exp_wg)) * jnp.einsum('td,efd->etf', xf, exp_wu)
        all_out = jnp.einsum('etf,edf->etd', h, exp_wd)
        picked = all_out[topk_idx, jnp.arange(T)[:, None]]
        routed_out = (topk_w[..., None] * picked).sum(axis=1)
        return (shared_out + routed_out).reshape(B, S, D)
    x = L0_attn_x
    x = x + 0.5 * _L0_ffn_ref(_layernorm(x, axis=-1), L0_ffn_gate_w, L0_ffn_shared_wg, L0_ffn_shared_wu, L0_ffn_shared_wd, L0_ffn_exp_wg, L0_ffn_exp_wu, L0_ffn_exp_wd)
    x = x + _L0_attn_ref(_layernorm(x, axis=-1), L0_attn_W_qkv, L0_attn_b_qkv, L0_attn_W_out, L0_attn_b_out)
    x = x + 0.5 * _L0_ffn_ref(_layernorm(x, axis=-1), L0_ffn_gate_w, L0_ffn_shared_wg, L0_ffn_shared_wu, L0_ffn_shared_wd, L0_ffn_exp_wg, L0_ffn_exp_wu, L0_ffn_exp_wd)
    return x

_drawn_inputs = setup_inputs


def setup_inputs(seed=0):
    import zlib

    import numpy as np

    out = dict(_drawn_inputs(seed))
    spreads = {}
    factors = {'L0_ffn_shared_wg': 2.873,
     'L0_ffn_shared_wu': 2.839,
     'L0_ffn_shared_wd': 2.84,
     'L0_ffn_gate_w': 3.099,
     'L0_ffn_exp_wg': 2.689}
    for name, (base, spread) in spreads.items():
        noise = np.random.default_rng([zlib.crc32(name.encode()), seed]).standard_normal(out[name].shape)
        drawn = base * np.exp(spread * noise) if base else spread * noise
        out[name] = jnp.asarray(drawn.astype(out[name].dtype))
    for name, factor in factors.items():
        out[name] = (out[name] * factor).astype(out[name].dtype)
    return out
```

```python
from contextlib import ExitStack

import concourse.bass as bass
from concourse import mybir

ALU = mybir.AluOpType
ACT = mybir.ActivationFunctionType
AX = mybir.AxisListType
F32 = mybir.dt.float32
F32R = mybir.dt.float32r
BF16 = mybir.dt.bfloat16
I32 = mybir.dt.int32
U32 = mybir.dt.uint32
ds = bass.ds

P = 128
TOP_K = 2
ROUTED_SCALE = 2.5
HALF = 0.5
EPS = 1e-5


def steps(eng, total, unroll):
    for n in range(unroll):
        yield n, n
    with eng.Fori(1, total // unroll - 1) as i:
        for k in range(unroll):
            yield i * unroll + k, k
    for n in range(total - unroll, total):
        yield n, n % unroll


def since(n, k):
    return not isinstance(n, int) or n >= k


def until(n, k, total):
    return not isinstance(n, int) or n + k < total


def half(n, k):
    return n // 2 if isinstance(n, int) else (n - k % 2) // 2


def semaphores(nc, stack, tag):
    made = []

    def clear():
        nc.clear_and_free_semaphores(made)
        nc.all_engine_barrier()

    def sem(name):
        made.append(nc.alloc_semaphore(f"{tag}_{name}"))
        return made[-1]

    stack.callback(clear)
    return sem


class Shapes:
    def __init__(self, x, w_up, w_down, gate):
        self.B, self.L, self.D = x.shape
        self.T = self.B * self.L
        self.NT = self.T // P
        self.NC = self.D // P
        self.NU = w_up.shape[1]
        self.E = gate.shape[1]
        self.NS = self.NU - self.E
        self.FF = w_up.shape[2] // 2
        self.NJ = self.T * TOP_K // P + self.E
        self.TAIL = self.FF - P
        self.HD = 16
        self.HEADS = self.D // self.HD
        self.G = self.HEADS // 4
        assert self.NS == 2 and self.NC == 2 and 0 < self.TAIL < P and self.NT % 4 == 0 and self.NJ % 4 == 0


def feed_forward(nc, tag, S, X, ST, MV, ident, w_up, w_down, gate, xn_dram, y_dram, out_dram, first):
    D, NT, NU, NS, FF, E, NJ, TAIL = S.D, S.NT, S.NU, S.NS, S.FF, S.E, S.NJ, S.TAIL
    NG = NT * TOP_K
    with ExitStack() as ctx:
        def sb(name, shape, dt=F32):
            return ctx.enter_context(nc.sbuf_tensor(f"{tag}_{name}", shape, dt))

        WUh = sb("WUh", [P, 2, NU * 2 * FF], F32R)
        WUl = sb("WUl", [P, 2, NU * 2 * FF], F32R)
        WDh = [sb("WDh0", [P, NU * D], F32R), sb("WDh1", [TAIL, NU * D], F32R)]
        WDl = [sb("WDl0", [P, NU * D], F32R), sb("WDl1", [TAIL, NU * D], F32R)]
        RSTD = sb("RSTD", [P, NT])
        W12 = sb("W12", [P, TOP_K, NT])
        slots_u = sb("slots_u", [P, TOP_K, NT], U32)
        tok_u = sb("tok_u", [P, NJ], U32)
        unit_i = sb("unit_i", [P, NJ], I32)
        X2 = X[:, :, :].rearrange("p t d -> p (t d)")
        MV2 = MV[:, :, :].rearrange("p t s -> p (t s)")

        with ExitStack() as c1:
            sem = semaphores(nc, c1, f"{tag}1")

            def sb1(name, shape, dt=F32):
                return c1.enter_context(nc.sbuf_tensor(f"{tag}1_{name}", shape, dt))

            def ps1(name, shape):
                return c1.enter_context(nc.psum_tensor(f"{tag}1_{name}", shape, F32))

            XN = sb1("XN", [P, 4, D])
            xh = sb1("xh", [P, 2, D], F32R)
            xl = sb1("xl", [P, 2, D], F32R)
            GW = sb1("GW", [P, 2, E])
            GWh = sb1("GWh", [P, 2, E], F32R)
            GWl = sb1("GWl", [P, 2, E], F32R)
            stage = sb1("stage", [P, 2, 4 * FF])
            stageD = sb1("stageD", [P, 2, 2, D])
            ps_x = [ps1(f"ps_x{i}", [P, D]) for i in range(2)]
            ps_gate = ps1("ps_gate", [P, NT * E])
            ps_pre = ps1("ps_pre", [P, E * NT])
            ps_tot = ps1("ps_tot", [P, E * NT])
            ps_tok = ps1("ps_tok", [P, 2 * NJ])
            SC = sb1("SC", [P, NT, E])
            SC2 = sb1("SC2", [P, NT, E])
            EQ = sb1("EQ", [P, NT, E])
            PR = sb1("PR", [P, NT, E])
            OH = sb1("OH", [P, TOP_K, NT, E])
            SEL = sb1("SEL", [P, E, NT], BF16)
            M12 = sb1("M12", [P, TOP_K, NT])
            PMAX = sb1("PMAX", [P, NT])
            DEN = sb1("DEN", [P, NT])
            prio_i = sb1("prio_i", [P, E], I32)
            prio = sb1("prio", [P, E])
            lower_t = sb1("lower_t", [P, P], BF16)
            ones_b = sb1("ones_b", [P, P], BF16)
            ones_f = sb1("ones_f", [P, E * NT])
            CUM = sb1("CUM", [P, E, NT])
            EXC = sb1("EXC", [P, E, NT])
            SLOT = sb1("SLOT", [P, E, NT])
            CNT = sb1("CNT", [P, E])
            CNTi = sb1("CNTi", [P, E], I32)
            NTI = sb1("NTI", [P, E])
            CT = sb1("CT", [P, E])
            BASE = sb1("BASE", [P, E])
            SL = sb1("SL", [P, TOP_K, NT])
            SLi = sb1("SLi", [P, TOP_K, NT], I32)
            Ri = sb1("Ri", [P, NG], I32)
            Ti = sb1("Ti", [P, NG], I32)
            RF = sb1("RF", [P, NG])
            TF = sb1("TF", [P, NG])
            row_i = sb1("row_i", [P, P], I32)
            row_f = sb1("row_f", [P, P])
            row_b = sb1("row_b", [P, P], BF16)
            par_i = sb1("par_i", [P, 1], I32)
            par_f = sb1("par_f", [P, 1])
            GE = sb1("GE", [P, NJ, E])
            UF = sb1("UF", [P, NJ])
            tile_of = sb1("tile_of", [P, NG])
            RSEL = sb1("RSEL", [P, 4, P], BF16)
            TSEL = sb1("TSEL", [P, 4, 2 * NJ], BF16)
            tokf = sb1("tokf", [P, 2 * NJ])

            raw_in = [sem("raw_in0"), sem("raw_in1")]
            gate_in = sem("gate_in")
            consts = sem("consts")
            chain = sem("chain")
            chain_pool = sem("chain_pool")
            split_w = sem("split_w")
            rstd_in = sem("rstd_in")
            rstd_out = sem("rstd_out")
            stats_done = sem("stats_done")
            xn_ready = sem("xn_ready")
            xn_out = [sem(f"xn_out{i}") for i in range(4)]
            xT_done = sem("xT_done")
            xh_done = sem("xh_done")
            xl_done = sem("xl_done")
            gate_w = sem("gate_w")
            gate_done = sem("gate_done")
            sig_done = sem("sig_done")
            sel_done = sem("sel_done")
            pre_done = sem("pre_done")
            pre_copied = sem("pre_copied")
            onehot = sem("onehot")
            tok_done = sem("tok_done")

            PRE = sb1("PRE", [P, E * NT])
            TOT = sb1("TOT", [P, E * NT])

            block = c1.enter_context(nc.Block())

            @block.sync
            def _(sp):
                sp.dma_start(GW[:, :, :], gate.rearrange("(c p) e -> p c e", p=P)).then_inc(gate_in, 16)
                def load_unit(u):
                    b = u % 2
                    if u >= 2:
                        sp.wait_ge(split_w, u - 1)
                    sp.dma_start(stage[:, b, :].rearrange("p (c f) -> p c f", c=2),
                                 w_up[:, u, :].rearrange("(c p) f -> p c f", p=P)).then_inc(raw_in[b], 16)
                    sp.dma_start(stageD[:, b, 0, :], w_down[u, 0:P, :]).then_inc(raw_in[b], 16)
                    sp.dma_start(stageD[0:TAIL, b, 1, :], w_down[u, P:FF, :]).then_inc(raw_in[b], 16)
                load_unit(0)
                load_unit(1)
                for u in range(2, NU):
                    load_unit(u)
                for k in range(4):
                    sp.wait_ge(xn_out[k], 16 * (NT // 4))

            @block.gpsimd
            def _(pool):
                nc.gpsimd.iota(prio_i[:, :], pattern=[[-1, E]], base=E, channel_multiplier=0).then_inc(consts, 1)
                nc.gpsimd.iota(row_i[:, :], pattern=[[1, P]], base=0, channel_multiplier=0).then_inc(consts, 1)
                nc.gpsimd.iota(par_i[:, :], pattern=[[0, 1]], base=0, channel_multiplier=1).then_inc(consts, 1)
                nc.gpsimd.memset(ones_b[:, :], 1.0).then_inc(consts, 1)
                nc.gpsimd.memset(ones_f[:, :], 1.0).then_inc(consts, 1)
                pool.wait_ge(consts, 5)
                nc.gpsimd.affine_select(out=lower_t[:, :], in_=ones_b[:, :], compare_op=ALU.is_gt, fill=0.0,
                                        base=0, pattern=[[1, P]], channel_multiplier=-1).then_inc(consts, 1)
                for u in range(NU):
                    b = u % 2
                    pool.wait_ge(raw_in[b], 48 * (u // 2 + 1))
                    up = stage[:, b, :].rearrange("p (c f) -> p c f", c=2)
                    wu = slice(u * 2 * FF, (u + 1) * 2 * FF)
                    wd = slice(u * D, (u + 1) * D)
                    nc.gpsimd.tensor_copy(WUh[:, :, wu], up).then_inc(chain_pool, 1)
                    nc.gpsimd.tensor_copy(WDh[0][:, wd], stageD[:, b, 0, :]).then_inc(chain_pool, 1)
                    nc.gpsimd.tensor_copy(WDh[1][:, wd], stageD[0:TAIL, b, 1, :]).then_inc(chain_pool, 1)
                    pool.wait_ge(chain_pool, 3 * (u + 1))
                    nc.gpsimd.tensor_tensor(WUl[:, :, wu], up, WUh[:, :, wu].bitcast(F32), ALU.subtract)
                    nc.gpsimd.tensor_tensor(WDl[0][:, wd], stageD[:, b, 0, :], WDh[0][:, wd].bitcast(F32), ALU.subtract)
                    nc.gpsimd.tensor_tensor(WDl[1][:, wd], stageD[0:TAIL, b, 1, :], WDh[1][:, wd].bitcast(F32),
                                            ALU.subtract).then_inc(split_w, 1)

            @block.scalar
            def _(act):
                act.wait_ge(rstd_in, 1)
                nc.scalar.activation(RSTD[:, :], RSTD[:, :], ACT.Sqrt).then_inc(rstd_out, 1)
                for t, k in steps(act, NT, 4):
                    act.wait_ge(xT_done, t + 1)
                    if since(t, 2):
                        act.wait_ge(gate_done, t - 1)
                    nc.scalar.activation(xh[:, k % 2, :], ps_x[k % 2][:, :], ACT.Copy).then_inc(xh_done, 1)
                    act.wait_ge(xn_ready, t + 1)
                    act.dma_start(xn_dram[ds(t * P, P), :], XN[:, k, :]).then_inc(xn_out[k], 16)
                act.wait_ge(gate_done, NT)
                nc.scalar.activation(SC[:, :, :].rearrange("p t e -> p (t e)"), ps_gate[:, :],
                                     ACT.Sigmoid).then_inc(sig_done, 1)
                act.wait_ge(pre_done, 1)
                nc.scalar.activation(PRE[:, :], ps_pre[:, :], ACT.Copy).then_inc(pre_copied, 1)
                nc.scalar.activation(TOT[:, :], ps_tot[:, :], ACT.Copy).then_inc(pre_copied, 1)

            @block.vector
            def _(dve):
                count = [0]

                def link(ins):
                    count[0] += 1
                    ins.then_inc(chain, 1)
                    dve.wait_ge(chain, count[0])

                dve.wait_ge(gate_in, 16)
                link(nc.vector.tensor_copy(GWh[:, :, :], GW[:, :, :]))
                nc.vector.tensor_tensor(GWl[:, :, :], GW[:, :, :], GWh[:, :, :].bitcast(F32),
                                        ALU.subtract).then_inc(gate_w, 1)
                if first:
                    for t in range(NT):
                        last = nc.vector.bn_stats(ST[:, t, :], X[:, t, :])
                    link(last)
                for t in range(NT):
                    last = nc.vector.bn_aggr(MV[:, t, :], ST[:, t, :])
                link(last)
                nc.vector.tensor_scalar(RSTD[:, :], MV[:, :, 1], EPS, None, ALU.add).then_inc(rstd_in, 1)
                dve.wait_ge(rstd_out, 1)
                link(nc.vector.reciprocal(RSTD[:, :], RSTD[:, :]))

                def normalise(t, k):
                    if since(t, 4):
                        dve.wait_ge(xT_done, t - 3)
                        dve.wait_ge(xn_out[k], 16 * quarter(t, k))
                    nc.vector.tensor_scalar(XN[:, k, :], X2[:, ds(t * D, D)], MV2[:, ds(2 * t, 1)],
                                            RSTD[:, ds(t, 1)], ALU.subtract, ALU.mult).then_inc(xn_ready, 1)

                def quarter(t, k):
                    return t // 4 if isinstance(t, int) else (t - k) // 4

                normalise(0, 0)
                for t, k in steps(dve, NT, 4):
                    if until(t, 1, NT):
                        normalise(t + 1, (k + 1) % 4)
                    dve.wait_ge(xh_done, t + 1)
                    nc.vector.tensor_tensor(xl[:, k % 2, :], ps_x[k % 2][:, :], xh[:, k % 2, :].bitcast(F32),
                                            ALU.subtract).then_inc(xl_done, 1)

                dve.wait_ge(consts, 6)
                link(nc.vector.tensor_copy(prio[:, :], prio_i[:, :]))
                link(nc.vector.tensor_copy(row_f[:, :], row_i[:, :]))
                link(nc.vector.tensor_copy(row_b[:, :], row_i[:, :]))
                link(nc.vector.tensor_copy(par_f[:, :], par_i[:, :]))
                for k in range(TOP_K):
                    link(nc.vector.tensor_copy(tile_of[:, k * NT:(k + 1) * NT], row_i[:, 0:NT]))
                dve.wait_ge(sig_done, 1)
                src = SC
                wide = [P, NT, E]
                for k in range(TOP_K):
                    link(nc.vector.tensor_reduce(M12[:, k, :], src[:, :, :], AX.X, ALU.max))
                    link(nc.vector.tensor_tensor(EQ[:, :, :], src[:, :, :],
                                                 M12[:, k, :].unsqueeze(2).to_broadcast(wide), ALU.is_equal))
                    link(nc.vector.tensor_tensor(PR[:, :, :], EQ[:, :, :],
                                                 prio[:, :].unsqueeze(1).to_broadcast(wide), ALU.mult))
                    link(nc.vector.tensor_reduce(PMAX[:, :], PR[:, :, :], AX.X, ALU.max))
                    link(nc.vector.tensor_tensor(OH[:, k, :, :], PR[:, :, :],
                                                 PMAX[:, :].unsqueeze(2).to_broadcast(wide), ALU.is_equal))
                    if k == 0:
                        link(nc.vector.scalar_tensor_tensor(SC2[:, :, :], OH[:, 0, :, :], -4.0, SC[:, :, :],
                                                            ALU.mult, ALU.add))
                        src = SC2
                nc.vector.tensor_tensor(SEL[:, :, :].rearrange("p e t -> p t e"), OH[:, 0, :, :],
                                        OH[:, 1, :, :], ALU.add).then_inc(sel_done, 1)
                link(nc.vector.tensor_tensor(DEN[:, :], M12[:, 0, :], M12[:, 1, :], ALU.add))
                link(nc.vector.tensor_scalar(DEN[:, :], DEN[:, :], 1e-20, None, ALU.add))
                link(nc.vector.reciprocal(DEN[:, :], DEN[:, :]))
                for k in range(TOP_K):
                    link(nc.vector.scalar_tensor_tensor(W12[:, k, :], M12[:, k, :], ROUTED_SCALE * HALF, DEN[:, :],
                                                        ALU.mult, ALU.mult))

                dve.wait_ge(pre_copied, 2)
                CUMf = CUM[:, :, :].rearrange("p e t -> p (e t)")
                EXCf = EXC[:, :, :].rearrange("p e t -> p (e t)")
                SLOTf = SLOT[:, :, :].rearrange("p e t -> p (e t)")
                link(nc.vector.tensor_tensor_scan(CUMf, ones_f[:, :], TOT[:, :], 0.0, ALU.mult, ALU.add))
                link(nc.vector.tensor_tensor(EXCf, CUMf, TOT[:, :], ALU.subtract))
                link(nc.vector.tensor_tensor(CNT[:, :], CUM[:, :, NT - 1], EXC[:, :, 0], ALU.subtract))
                link(nc.vector.tensor_scalar(CNTi[:, :], CNT[:, :], float(P - 1), None, ALU.add))
                link(nc.vector.tensor_scalar(CNTi[:, :], CNTi[:, :], P.bit_length() - 1, None,
                                             ALU.arith_shift_right))
                link(nc.vector.tensor_copy(NTI[:, :], CNTi[:, :]))
                link(nc.vector.tensor_tensor_scan(CT[:, :], ones_f[:, 0:E], NTI[:, :], 0.0, ALU.mult, ALU.add))
                link(nc.vector.tensor_tensor(BASE[:, :], CT[:, :], NTI[:, :], ALU.subtract))
                link(nc.vector.scalar_tensor_tensor(BASE[:, :], BASE[:, :], float(P), EXC[:, :, 0],
                                                    ALU.mult, ALU.subtract))
                link(nc.vector.tensor_tensor(SLOTf, EXCf, PRE[:, :], ALU.add))
                link(nc.vector.tensor_tensor(SLOT[:, :, :], SLOT[:, :, :],
                                             BASE[:, :].unsqueeze(2).to_broadcast([P, E, NT]), ALU.add))
                for k in range(TOP_K):
                    link(nc.vector.tensor_tensor(EQ[:, :, :], OH[:, k, :, :],
                                                 SLOT[:, :, :].rearrange("p e t -> p t e"), ALU.mult))
                    link(nc.vector.tensor_reduce(SL[:, k, :], EQ[:, :, :], AX.X, ALU.add))
                link(nc.vector.tensor_copy(slots_u[:, :, :], SL[:, :, :]))
                link(nc.vector.tensor_copy(SLi[:, :, :], SL[:, :, :]))
                flat = SLi[:, :, :].rearrange("p k t -> p (k t)")
                link(nc.vector.tensor_scalar(Ri[:, :], flat, P - 1, None, ALU.bitwise_and))
                link(nc.vector.tensor_scalar(Ti[:, :], flat, P.bit_length() - 1, None, ALU.arith_shift_right))
                link(nc.vector.tensor_copy(RF[:, :], Ri[:, :]))
                link(nc.vector.tensor_copy(TF[:, :], Ti[:, :]))

                jw = [P, NJ, E]
                link(nc.vector.tensor_tensor(GE[:, :, :], row_f[:, 0:NJ].unsqueeze(2).to_broadcast(jw),
                                             CT[:, :].unsqueeze(1).to_broadcast(jw), ALU.is_ge))
                link(nc.vector.tensor_reduce(UF[:, :], GE[:, :, :], AX.X, ALU.add))
                link(nc.vector.tensor_scalar(unit_i[:, :], UF[:, :], float(E - 1), float(NS), ALU.min, ALU.add))

                for g, k in steps(dve, NG, 4):
                    if since(g, 4):
                        dve.wait_ge(tok_done, g - 3)
                    nc.vector.tensor_scalar(RSEL[:, k, :], row_b[:, :], RF[:, ds(g, 1)], None, ALU.is_equal)
                    nc.vector.tensor_scalar(TSEL[:, k, 0:NJ], row_b[:, 0:NJ], TF[:, ds(g, 1)], par_f[:, :],
                                            ALU.is_equal, ALU.mult)
                    nc.vector.tensor_scalar(TSEL[:, k, NJ:2 * NJ], row_b[:, 0:NJ], TF[:, ds(g, 1)],
                                            tile_of[:, ds(g, 1)], ALU.is_equal, ALU.mult).then_inc(onehot, 1)
                dve.wait_ge(tok_done, NG)
                link(nc.vector.tensor_copy(tokf[:, :], ps_tok[:, :]))
                link(nc.vector.scalar_tensor_tensor(tok_u[:, :], tokf[:, NJ:2 * NJ], float(P), tokf[:, 0:NJ],
                                                    ALU.mult, ALU.add))

            @block.tensor
            def _(pe):
                def transpose_x(t, k):
                    pe.wait_ge(xn_ready, t + 1)
                    if since(t, 2):
                        pe.wait_ge(xl_done, t - 1)
                    for c in range(2):
                        last = nc.tensor.transpose(ps_x[k % 2][:, c * P:(c + 1) * P], XN[:, k, c * P:(c + 1) * P],
                                                   ident[:, :])
                    last.then_inc(xT_done, 1)

                pe.wait_ge(gate_w, 1)
                transpose_x(0, 0)
                for t, k in steps(pe, NT, 4):
                    if until(t, 1, NT):
                        transpose_x(t + 1, (k + 1) % 4)
                    pe.wait_ge(xl_done, t + 1)
                    passes = [(a, b, c) for c in range(2) for a, b in ((xh, GWh), (xh, GWl), (xl, GWh))]
                    for i, (a, b, c) in enumerate(passes):
                        last = nc.tensor.matmul(ps_gate[:, ds(t * E, E)], a[:, k % 2, c * P:(c + 1) * P], b[:, c, :],
                                                start=i == 0, stop=i == 5)
                    last.then_inc(gate_done, 1)
                pe.wait_ge(sel_done, 1)
                pe.wait_ge(consts, 6)
                sel = SEL[:, :, :].rearrange("p e t -> p (e t)")
                nc.tensor.matmul(ps_pre[:, :], lower_t[:, :], sel, start=True, stop=True)
                nc.tensor.matmul(ps_tot[:, :], ones_b[:, :], sel, start=True, stop=True).then_inc(pre_done, 1)
                for g in range(NG):
                    pe.wait_ge(onehot, g + 1)
                    nc.tensor.matmul(ps_tok[:, :], RSEL[:, g % 4, :], TSEL[:, g % 4, :], start=g == 0,
                                     stop=g == NG - 1).then_inc(tok_done, 1)

        expert_stage(nc, tag, S, ident, WUh, WUl, WDh, WDl, tok_u, unit_i, xn_dram, y_dram)
        shared_stage(nc, tag, S, X, ST, MV, RSTD, W12, slots_u, ident, WUh, WUl, WDh, WDl, y_dram, out_dram)


def split_passes(n_chunks):
    return [(c, a, b) for c in range(n_chunks) for a, b in ((0, 0), (0, 1), (1, 0))]


def expert_stage(nc, tag, S, ident, WUh, WUl, WDh, WDl, tok_u, unit_i, xn_dram, y_dram):
    D, FF, NU, NJ, TAIL = S.D, S.FF, S.NU, S.NJ, S.TAIL
    with ExitStack() as c2:
        def sb(name, shape, dt=F32):
            return c2.enter_context(nc.sbuf_tensor(f"{tag}2_{name}", shape, dt))

        def ps(name):
            return [c2.enter_context(nc.psum_tensor(f"{tag}2_{name}{i}", [P, 512], F32)) for i in range(2)]

        sem = semaphores(nc, c2, f"{tag}2")

        XG = sb("XG", [P, 4, D])
        xs = [sb("xh", [P, 2, D], F32R), sb("xl", [P, 2, D], F32R)]
        SG = sb("SG", [P, 2, FF])
        H = sb("H", [P, 2, 2 * P])
        hs = [sb("hh", [P, 2, 2 * P], F32R), sb("hl", [P, 2, 2 * P], F32R)]
        YS = sb("YS", [P, 4, D])
        ps_x, ps_u, ps_h, ps_y = ps("ps_x"), ps("ps_u"), ps("ps_h"), ps("ps_y")

        zeroed = sem("zeroed")
        gathered = [sem(f"gathered{i}") for i in range(4)]
        xT_done = sem("xT_done")
        xh_done = sem("xh_done")
        xl_done = sem("xl_done")
        up_done = sem("up_done")
        silu_done = sem("silu_done")
        h_ready = sem("h_ready")
        hT_done = sem("hT_done")
        hh_done = sem("hh_done")
        hl_done = sem("hl_done")
        y_done = sem("y_done")
        y_copied = sem("y_copied")
        y_out = [sem(f"y_out{i}") for i in range(4)]

        block = c2.enter_context(nc.Block())

        @block.gpsimd
        def _(pool):
            for j in range(NJ):
                if j >= 4:
                    pool.wait_ge(xT_done, j - 3)
                nc.gpsimd.indirect_dma_start(
                    out=XG[:, j % 4, :], out_offset=None, in_=xn_dram[:, :],
                    in_offset=bass.IndirectOffsetOnAxis(ap=tok_u[:, j:j + 1], axis=0)
                ).then_inc(gathered[j % 4], 16)

        @block.sync
        def _(sp):
            for j, k in steps(sp, NJ, 4):
                sp.wait_ge(y_copied, j + 1)
                sp.dma_start(y_dram[ds(j * P, P), :], YS[:, k, :]).then_inc(y_out[k], 16)
            for k in range(4):
                sp.wait_ge(y_out[k], 16 * (NJ // 4))

        @block.scalar
        def _(act):
            def y_copy(j, k):
                act.wait_ge(y_done, j + 1)
                if since(j, 4):
                    act.wait_ge(y_out[k], 16 * quarter(j, k))
                nc.scalar.activation(YS[:, k, :], ps_y[k % 2][:, 0:D], ACT.Copy).then_inc(y_copied, 1)

            def x_high(j, k):
                act.wait_ge(xT_done, j + 1)
                if since(j, 2):
                    act.wait_ge(up_done, j - 1)
                nc.scalar.activation(xs[0][:, k % 2, :], ps_x[k % 2][:, 0:D], ACT.Copy).then_inc(xh_done, 1)

            def h_high(j, k):
                act.wait_ge(hT_done, j + 1)
                if since(j, 2):
                    act.wait_ge(y_done, j - 1)
                nc.scalar.activation(hs[0][:, k % 2, :], ps_h[k % 2][:, 0:2 * P], ACT.Copy).then_inc(hh_done, 1)

            x_high(0, 0)
            for j, k in steps(act, NJ, 4):
                if until(j, 1, NJ):
                    x_high(j + 1, (k + 1) % 4)
                act.wait_ge(up_done, j + 1)
                if since(j, 2):
                    act.wait_ge(h_ready, j - 1)
                nc.scalar.activation(SG[:, k % 2, :], ps_u[k % 2][:, 0:FF], ACT.Silu).then_inc(silu_done, 1)
                if since(j, 1):
                    h_high(j - 1, (k - 1) % 4)
                if since(j, 2):
                    y_copy(j - 2, (k - 2) % 4)
            h_high(NJ - 1, 3)
            y_copy(NJ - 2, 2)
            y_copy(NJ - 1, 3)

        @block.vector
        def _(dve):
            nc.vector.memset(H[:, :, FF:2 * P], 0.0).then_inc(zeroed, 1)

            def x_low(j, k):
                dve.wait_ge(xh_done, j + 1)
                nc.vector.tensor_tensor(xs[1][:, k % 2, :], ps_x[k % 2][:, 0:D],
                                        xs[0][:, k % 2, :].bitcast(F32), ALU.subtract).then_inc(xl_done, 1)

            def h_low(j, k):
                dve.wait_ge(hh_done, j + 1)
                nc.vector.tensor_tensor(hs[1][:, k % 2, :], ps_h[k % 2][:, 0:2 * P],
                                        hs[0][:, k % 2, :].bitcast(F32), ALU.subtract).then_inc(hl_done, 1)

            x_low(0, 0)
            for j, k in steps(dve, NJ, 4):
                if until(j, 1, NJ):
                    x_low(j + 1, (k + 1) % 4)
                dve.wait_ge(silu_done, j + 1)
                if since(j, 2):
                    dve.wait_ge(hT_done, j - 1)
                nc.vector.tensor_tensor(H[:, k % 2, 0:FF], SG[:, k % 2, :], ps_u[k % 2][:, FF:2 * FF],
                                        ALU.mult).then_inc(h_ready, 1)
                if since(j, 1):
                    h_low(j - 1, (k - 1) % 4)
            h_low(NJ - 1, 3)

        @block.tensor
        def _(pe):
            W_up, W_down = (WUh, WUl), (WDh, WDl)

            def transpose_x(j, k):
                pe.wait_ge(gathered[k], 16 * (quarter(j, k) + 1))
                if since(j, 2):
                    pe.wait_ge(xl_done, j - 1)
                for c in range(2):
                    last = nc.tensor.transpose(ps_x[k % 2][:, c * P:(c + 1) * P], XG[:, k, c * P:(c + 1) * P],
                                               ident[:, :])
                last.then_inc(xT_done, 1)

            def up(j, k):
                unit = pe.value_load(unit_i[0:1, ds(j, 1)], min_val=0, max_val=NU - 1)
                pe.wait_ge(xl_done, j + 1)
                if since(j, 2):
                    pe.wait_ge(h_ready, j - 1)
                plan = split_passes(2)
                for i, (c, a, b) in enumerate(plan):
                    last = nc.tensor.matmul(ps_u[k % 2][:, 0:2 * FF], xs[a][:, k % 2, c * P:(c + 1) * P],
                                            W_up[b][:, c, ds(unit * (2 * FF), 2 * FF)],
                                            start=i == 0, stop=i == len(plan) - 1)
                last.then_inc(up_done, 1)

            def transpose_h(j, k):
                if isinstance(j, int) and j == 0:
                    pe.wait_ge(zeroed, 1)
                pe.wait_ge(h_ready, j + 1)
                if since(j, 2):
                    pe.wait_ge(hl_done, j - 1)
                for c in range(2):
                    last = nc.tensor.transpose(ps_h[k % 2][:, c * P:(c + 1) * P], H[:, k % 2, c * P:(c + 1) * P],
                                               ident[:, :])
                last.then_inc(hT_done, 1)

            def down(j, k):
                unit = pe.value_load(unit_i[0:1, ds(j, 1)], min_val=0, max_val=NU - 1)
                pe.wait_ge(hl_done, j + 1)
                if since(j, 2):
                    pe.wait_ge(y_copied, j - 1)
                plan = split_passes(2)
                for i, (c, a, b) in enumerate(plan):
                    rows = P if c == 0 else TAIL
                    last = nc.tensor.matmul(ps_y[k % 2][:, 0:D], hs[a][0:rows, k % 2, c * P:(c + 1) * P],
                                            W_down[b][c][:, ds(unit * D, D)],
                                            start=i == 0, stop=i == len(plan) - 1)
                last.then_inc(y_done, 1)

            transpose_x(0, 0)
            for j, k in steps(pe, NJ, 4):
                if until(j, 1, NJ):
                    transpose_x(j + 1, (k + 1) % 4)
                up(j, k)
                if since(j, 1):
                    transpose_h(j - 1, (k - 1) % 4)
                if since(j, 2):
                    down(j - 2, (k - 2) % 4)
            transpose_h(NJ - 1, 3)
            down(NJ - 2, 2)
            down(NJ - 1, 3)


def quarter(n, k):
    return n // 4 if isinstance(n, int) else (n - k) // 4


def shared_stage(nc, tag, S, X, ST, MV, RSTD, W12, slots_u, ident, WUh, WUl, WDh, WDl, y_dram, out_dram):
    D, FF, NT, NS, TAIL = S.D, S.FF, S.NT, S.NS, S.TAIL
    with ExitStack() as c3:
        def sb(name, shape, dt=F32):
            return c3.enter_context(nc.sbuf_tensor(f"{tag}3_{name}", shape, dt))

        def ps(name):
            return [c3.enter_context(nc.psum_tensor(f"{tag}3_{name}{i}", [P, 512], F32)) for i in range(2)]

        sem = semaphores(nc, c3, f"{tag}3")

        XN = sb("XN", [P, 2, D])
        xs = [sb("xh", [P, 2, D], F32R), sb("xl", [P, 2, D], F32R)]
        SG = sb("SG", [P, 2, FF])
        H = sb("H", [P, 2, 2 * P])
        hs = [sb("hh", [P, 2, 2 * P], F32R), sb("hl", [P, 2, 2 * P], F32R)]
        YG = sb("YG", [P, 4, TOP_K, D])
        ST2 = ST[:, :, :].rearrange("p t s -> p (t s)")
        ps_x, ps_u, ps_h, ps_y = ps("ps_x"), ps("ps_u"), ps("ps_h"), ps("ps_y")
        X2 = X[:, :, :].rearrange("p t d -> p (t d)")
        MV2 = MV[:, :, :].rearrange("p t s -> p (t s)")
        W2 = W12[:, :, :].rearrange("p k t -> p (k t)")

        zeroed = sem("zeroed")
        gathered = [sem(f"gathered{i}") for i in range(4)]
        xn_ready = sem("xn_ready")
        xT_done = sem("xT_done")
        xh_done = sem("xh_done")
        xl_done = sem("xl_done")
        up_done = sem("up_done")
        silu_done = sem("silu_done")
        h_ready = sem("h_ready")
        hT_done = sem("hT_done")
        hh_done = sem("hh_done")
        hl_done = sem("hl_done")
        y_done = sem("y_done")
        added = sem("added")
        mixed = sem("mixed")
        x_done = sem("x_done")
        stats = sem("stats")
        stored = sem("stored")

        block = c3.enter_context(nc.Block())

        @block.gpsimd
        def _(pool):
            for t in range(NT):
                if t >= 4:
                    pool.wait_ge(x_done, t - 3)
                for c in range(TOP_K):
                    nc.gpsimd.indirect_dma_start(
                        out=YG[:, t % 4, c, :], out_offset=None, in_=y_dram[:, :],
                        in_offset=bass.IndirectOffsetOnAxis(ap=slots_u[:, c, t:t + 1], axis=0)
                    ).then_inc(gathered[t % 4], 16)

        @block.sync
        def _(sp):
            if out_dram is not None:
                for t, k in steps(sp, NT, 4):
                    sp.wait_ge(x_done, t + 1)
                    sp.dma_start(out_dram[ds(t * P, P), :], X2[:, ds(t * D, D)]).then_inc(stored, 16)
                sp.wait_ge(stored, 16 * NT)

        @block.scalar
        def _(act):
            def x_high(t, k):
                act.wait_ge(xT_done, t + 1)
                if since(t, 2):
                    act.wait_ge(up_done, 2 * t - 2)
                nc.scalar.activation(xs[0][:, k % 2, :], ps_x[k % 2][:, 0:D], ACT.Copy).then_inc(xh_done, 1)

            def h_high(t, k, s):
                n = 2 * t + s
                act.wait_ge(hT_done, n + 1)
                if since(t, 1):
                    act.wait_ge(y_done, t)
                nc.scalar.activation(hs[0][:, s, :], ps_h[s][:, 0:2 * P], ACT.Copy).then_inc(hh_done, 1)

            x_high(0, 0)
            for t, k in steps(act, NT, 4):
                for s in range(NS):
                    act.wait_ge(up_done, 2 * t + s + 1)
                    if since(t, 1):
                        act.wait_ge(h_ready, 2 * t + s - 1)
                    nc.scalar.activation(SG[:, s, :], ps_u[s][:, 0:FF], ACT.Silu).then_inc(silu_done, 1)
                    if s == 0 and until(t, 1, NT):
                        x_high(t + 1, (k + 1) % 4)
                for s in range(NS):
                    h_high(t, k, s)

        @block.vector
        def _(dve):
            nc.vector.memset(H[:, :, FF:2 * P], 0.0).then_inc(zeroed, 1)

            def normalise(t, k):
                if since(t, 2):
                    dve.wait_ge(xT_done, t - 1)
                nc.vector.tensor_scalar(XN[:, k % 2, :], X2[:, ds(t * D, D)], MV2[:, ds(2 * t, 1)],
                                        RSTD[:, ds(t, 1)], ALU.subtract, ALU.mult).then_inc(xn_ready, 1)

            def x_low(t, k):
                dve.wait_ge(xh_done, t + 1)
                nc.vector.tensor_tensor(xs[1][:, k % 2, :], ps_x[k % 2][:, 0:D],
                                        xs[0][:, k % 2, :].bitcast(F32), ALU.subtract).then_inc(xl_done, 1)

            def h_low(t, s):
                dve.wait_ge(hh_done, 2 * t + s + 1)
                nc.vector.tensor_tensor(hs[1][:, s, :], ps_h[s][:, 0:2 * P],
                                        hs[0][:, s, :].bitcast(F32), ALU.subtract).then_inc(hl_done, 1)

            def finish(t, k):
                x_t = X2[:, ds(t * D, D)]
                dve.wait_ge(gathered[k], 32 * (quarter(t, k) + 1))
                if out_dram is None and since(t, 1):
                    dve.wait_ge(x_done, t)
                nc.vector.scalar_tensor_tensor(x_t, YG[:, k, 0, :], W2[:, ds(t, 1)], x_t,
                                               ALU.mult, ALU.add).then_inc(mixed, 1)
                if out_dram is None and since(t, 1):
                    statistics(t - 1)
                dve.wait_ge(mixed, 2 * t + 1)
                nc.vector.scalar_tensor_tensor(x_t, YG[:, k, 1, :], W2[:, ds(t + NT, 1)], x_t,
                                               ALU.mult, ALU.add).then_inc(mixed, 1)
                dve.wait_ge(mixed, 2 * t + 2)
                dve.wait_ge(y_done, t + 1)
                nc.vector.scalar_tensor_tensor(x_t, ps_y[k % 2][:, 0:D], HALF, x_t,
                                               ALU.mult, ALU.add).then_inc(x_done, 1)

            def statistics(t):
                nc.vector.bn_stats(ST2[:, ds(6 * t, 6)], X2[:, ds(t * D, D)]).then_inc(stats, 1)

            normalise(0, 0)
            x_low(0, 0)
            for t, k in steps(dve, NT, 4):
                if until(t, 1, NT):
                    normalise(t + 1, (k + 1) % 4)
                for s in range(NS):
                    dve.wait_ge(silu_done, 2 * t + s + 1)
                    if since(t, 1):
                        dve.wait_ge(hT_done, 2 * t + s - 1)
                    nc.vector.tensor_tensor(H[:, s, 0:FF], SG[:, s, :], ps_u[s][:, FF:2 * FF],
                                            ALU.mult).then_inc(h_ready, 1)
                    if s == 0 and until(t, 1, NT):
                        x_low(t + 1, (k + 1) % 4)
                for s in range(NS):
                    h_low(t, s)
                if since(t, 1):
                    finish(t - 1, (k - 1) % 4)
            finish(NT - 1, 3)
            if out_dram is None:
                dve.wait_ge(x_done, NT)
                statistics(NT - 1)

        @block.tensor
        def _(pe):
            W_up, W_down = (WUh, WUl), (WDh, WDl)

            def transpose_x(t, k):
                pe.wait_ge(xn_ready, t + 1)
                if since(t, 2):
                    pe.wait_ge(xl_done, t - 1)
                for c in range(2):
                    last = nc.tensor.transpose(ps_x[k % 2][:, c * P:(c + 1) * P],
                                               XN[:, k % 2, c * P:(c + 1) * P], ident[:, :])
                last.then_inc(xT_done, 1)

            def up(t, k, s):
                pe.wait_ge(xl_done, t + 1)
                if since(t, 1):
                    pe.wait_ge(h_ready, 2 * t + s - 1)
                plan = split_passes(2)
                for i, (c, a, b) in enumerate(plan):
                    last = nc.tensor.matmul(ps_u[s][:, 0:2 * FF], xs[a][:, k % 2, c * P:(c + 1) * P],
                                            W_up[b][:, c, s * 2 * FF:(s + 1) * 2 * FF],
                                            start=i == 0, stop=i == len(plan) - 1)
                last.then_inc(up_done, 1)

            def transpose_h(t, s):
                pe.wait_ge(h_ready, 2 * t + s + 1)
                if since(t, 1):
                    pe.wait_ge(hl_done, 2 * t + s - 1)
                for c in range(2):
                    last = nc.tensor.transpose(ps_h[s][:, c * P:(c + 1) * P], H[:, s, c * P:(c + 1) * P],
                                               ident[:, :])
                last.then_inc(hT_done, 1)

            def down(t, k):
                if since(t, 2):
                    pe.wait_ge(x_done, t - 1)
                plan = [(s, *one) for s in range(NS) for one in split_passes(2)]
                for i, (s, c, a, b) in enumerate(plan):
                    if i % 6 == 0:
                        pe.wait_ge(hl_done, 2 * t + s + 1)
                    rows = P if c == 0 else TAIL
                    last = nc.tensor.matmul(ps_y[k % 2][:, 0:D], hs[a][0:rows, s, c * P:(c + 1) * P],
                                            W_down[b][c][:, s * D:(s + 1) * D],
                                            start=i == 0, stop=i == len(plan) - 1)
                last.then_inc(y_done, 1)

            transpose_x(0, 0)
            pe.wait_ge(zeroed, 1)
            for t, k in steps(pe, NT, 4):
                up(t, k, 0)
                if until(t, 1, NT):
                    transpose_x(t + 1, (k + 1) % 4)
                up(t, k, 1)
                if since(t, 1):
                    down(t - 1, (k - 1) % 4)
                transpose_h(t, 0)
                transpose_h(t, 1)
            down(NT - 1, 3)


def attention(nc, S, X, ST, MV, ident, w_qkv, b_qk, b_v, w_out, b_out, out_dram, first):
    with ExitStack() as ctx:
        V = ctx.enter_context(nc.sbuf_tensor("V", [P, S.NT, S.HEADS, S.HD + 1], F32))
        qk_dram = nc.dram_tensor("qk_scratch", (S.B, S.G, P, S.L), F32, kind="Internal").ap()
        project_stage(nc, S, X, ST, MV, ident, w_qkv, b_qk, b_v, V, qk_dram, first)
        ATT = ctx.enter_context(nc.sbuf_tensor("ATT", [P, S.NT, S.D], F32))
        softmax_stage(nc, S, ident, V, ATT, qk_dram)
        output_stage(nc, S, X, ST, MV, ident, ATT, w_out, b_out, out_dram)


def project_stage(nc, S, X, ST, MV, ident, w_qkv, b_qk, b_v, V, qk_dram, first):
    D, NT, HD, HEADS, G, L = S.D, S.NT, S.HD, S.HEADS, S.G, S.L
    GF = D // G
    W = 4 * P
    NW = S.T // W
    with ExitStack() as c:
        def sb(name, shape, dt=F32):
            return c.enter_context(nc.sbuf_tensor(f"p_{name}", shape, dt))

        def ps(name, n=2):
            return [c.enter_context(nc.psum_tensor(f"p_{name}{i}", [P, 512], F32)) for i in range(n)]

        sem = semaphores(nc, c, "p")

        WR = sb("WR", [P, 2, 3 * D])
        Wh = sb("Wh", [P, 2, 3 * D], F32R)
        Wl = sb("Wl", [P, 2, 3 * D], F32R)
        BQK = sb("BQK", [P, G])
        BV = sb("BV", [P, D])
        RSTD = sb("RSTD", [P, NT])
        XN = sb("XN", [P, 4, D])
        xs = [sb("xh", [P, 2, 2, W], F32R), sb("xl", [P, 2, 2, W], F32R)]
        QK = sb("QK", [P, 2, W])
        ps_x, ps_qk, ps_v = ps("ps_x"), ps("ps_qk"), ps("ps_v")
        X2 = X[:, :, :].rearrange("p t d -> p (t d)")
        MV2 = MV[:, :, :].rearrange("p t s -> p (t s)")
        V2 = V[:, :, :, :].rearrange("p t h e -> p (t h e)")

        weights_in = sem("weights_in")
        weights = sem("weights")
        weights_hi = sem("weights_hi")
        ones = sem("ones")
        chain = sem("chain")
        rstd_in = sem("rstd_in")
        rstd_out = sem("rstd_out")
        xn_ready = sem("xn_ready")
        xT_done = sem("xT_done")
        xh_done = sem("xh_done")
        xl_done = sem("xl_done")
        qk_done = sem("qk_done")
        qk_copied = sem("qk_copied")
        qk_out = [sem("qk_out0"), sem("qk_out1")]
        v_done = sem("v_done")
        v_copied = sem("v_copied")

        block = c.enter_context(nc.Block())

        @block.sync
        def _(sp):
            sp.dma_start(WR[:, :, :], w_qkv.rearrange("(c p) f -> p c f", p=P)).then_inc(weights_in, 16)
            sp.dma_start(BQK[:, :], b_qk).then_inc(weights_in, 16)
            sp.dma_start(BV[:, :], b_v.rearrange("(a f) -> a f", a=1)
                         .to_broadcast([P, D])).then_inc(weights_in, 16)
            for n in range(NW * G):
                w, g = n // G, n % G
                sp.wait_ge(qk_copied, n + 1)
                sp.dma_start(qk_dram[w // 2, g, :, w % 2 * W:(w % 2 + 1) * W], QK[:, g % 2, :]).then_inc(qk_out[g % 2], 16)
            for i in range(2):
                sp.wait_ge(qk_out[i], 16 * NW * G // 2)

        @block.gpsimd
        def _(pool):
            nc.gpsimd.memset(V[:, :, :, HD:HD + 1], 1.0).then_inc(ones, 1)
            pool.wait_ge(weights_in, 48)
            nc.gpsimd.tensor_copy(Wh[:, :, :], WR[:, :, :]).then_inc(weights_hi, 1)
            pool.wait_ge(weights_hi, 1)
            nc.gpsimd.tensor_tensor(Wl[:, :, :], WR[:, :, :], Wh[:, :, :].bitcast(F32),
                                    ALU.subtract).then_inc(weights, 1)

        @block.scalar
        def _(act):
            act.wait_ge(rstd_in, 1)
            nc.scalar.activation(RSTD[:, :], RSTD[:, :], ACT.Sqrt).then_inc(rstd_out, 1)
            act.wait_ge(weights_in, 48)

            def x_high(w, k):
                for i in range(4):
                    act.wait_ge(xT_done, 4 * w + i + 1)
                    if i == 0 and since(w, 2):
                        act.wait_ge(v_done, 4 * w - 4)
                    nc.scalar.activation(xs[0][:, k, :, i * P:(i + 1) * P],
                                         ps_x[i % 2][:, 0:D].rearrange("p (c n) -> p c n", c=2),
                                         ACT.Copy).then_inc(xh_done, 1)

            x_high(0, 0)
            for w, k in steps(act, NW, 2):
                for g in range(G):
                    act.wait_ge(qk_done, G * w + g + 1)
                    if g >= 2 or since(w, 1):
                        act.wait_ge(qk_out[g % 2], 16 * (2 * w + g // 2))
                    nc.scalar.activation(QK[:, g % 2, :], ps_qk[g % 2][:, :], ACT.Identity,
                                         bias=BQK[:, g:g + 1]).then_inc(qk_copied, 1)
                if until(w, 1, NW):
                    x_high(w + 1, 1 - k)

        @block.vector
        def _(dve):
            count = [0]

            def link(ins):
                count[0] += 1
                ins.then_inc(chain, 1)
                dve.wait_ge(chain, count[0])

            if first:
                for t in range(NT):
                    last = nc.vector.bn_stats(ST[:, t, :], X[:, t, :])
                link(last)
            for t in range(NT):
                last = nc.vector.bn_aggr(MV[:, t, :], ST[:, t, :])
            link(last)
            nc.vector.tensor_scalar(RSTD[:, :], MV[:, :, 1], EPS, None, ALU.add).then_inc(rstd_in, 1)
            dve.wait_ge(rstd_out, 1)
            link(nc.vector.reciprocal(RSTD[:, :], RSTD[:, :]))
            dve.wait_ge(weights_in, 48)
            dve.wait_ge(ones, 1)

            def x_parts(w, k):
                for i in range(5):
                    if i < 4:
                        if since(w, 1):
                            dve.wait_ge(xT_done, 4 * w + i - 3)
                        t = 4 * w + i
                        nc.vector.tensor_scalar(XN[:, i, :], X2[:, ds(t * D, D)], MV2[:, ds(2 * t, 1)],
                                                RSTD[:, ds(t, 1)], ALU.subtract, ALU.mult).then_inc(xn_ready, 1)
                    if i > 0:
                        j = i - 1
                        dve.wait_ge(xh_done, 4 * w + j + 1)
                        nc.vector.tensor_tensor(xs[1][:, k, :, j * P:(j + 1) * P],
                                                ps_x[j % 2][:, 0:D].rearrange("p (c n) -> p c n", c=2),
                                                xs[0][:, k, :, j * P:(j + 1) * P].bitcast(F32),
                                                ALU.subtract).then_inc(xl_done, 1)

            x_parts(0, 0)
            for w, k in steps(dve, NW, 2):
                if until(w, 1, NW):
                    x_parts(w + 1, 1 - k)
                for i in range(4):
                    t = 4 * w + i
                    dve.wait_ge(v_done, t + 1)
                    nc.vector.tensor_tensor(
                        V2[:, ds(t * (HEADS * (HD + 1)), HEADS * (HD + 1))]
                        .rearrange("p (h e) -> p h e", h=HEADS)[:, :, 0:HD],
                        ps_v[i % 2][:, 0:D].rearrange("p (h e) -> p h e", h=HEADS),
                        BV[:, :].rearrange("p (h e) -> p h e", h=HEADS), ALU.add).then_inc(v_copied, 1)

        @block.tensor
        def _(pe):
            Ws = (Wh, Wl)

            def transpose_x(w, k):
                for i in range(4):
                    pe.wait_ge(xn_ready, 4 * w + i + 1)
                    if i >= 2 or since(w, 1):
                        pe.wait_ge(xl_done, 4 * w + i - 1)
                    for c in range(2):
                        last = nc.tensor.transpose(ps_x[i % 2][:, c * P:(c + 1) * P],
                                                   XN[:, i, c * P:(c + 1) * P], ident[:, :])
                    last.then_inc(xT_done, 1)

            transpose_x(0, 0)
            pe.wait_ge(weights, 1)
            for w, k in steps(pe, NW, 2):
                pe.wait_ge(xl_done, 4 * w + 4)
                for g in range(G):
                    if g >= 2 or since(w, 1):
                        pe.wait_ge(qk_copied, G * w + g - 1)
                    for i, (c, a, b) in enumerate(split_passes(2)):
                        wt = Ws[a][:, c, 2 * g * GF:2 * (g + 1) * GF]
                        last = nc.tensor.matmul(ps_qk[g % 2][:, :], wt, xs[b][:, k, c, :], start=i == 0, stop=i == 5)
                    last.then_inc(qk_done, 1)
                if until(w, 1, NW):
                    transpose_x(w + 1, 1 - k)
                for t in range(4):
                    if t >= 2 or since(w, 1):
                        pe.wait_ge(v_copied, 4 * w + t - 1)
                    for i, (c, a, b) in enumerate(split_passes(2)):
                        last = nc.tensor.matmul(ps_v[t % 2][:, 0:D], xs[a][:, k, c, t * P:(t + 1) * P],
                                                Ws[b][:, c, 2 * D:3 * D], start=i == 0, stop=i == 5)
                    last.then_inc(v_done, 1)


def softmax_stage(nc, S, ident, V, ATT, qk_dram):
    D, NT, HD, HEADS, G, L = S.D, S.NT, S.HD, S.HEADS, S.G, S.L
    NG = S.B * G
    NQ = L // P
    W = 512
    GH = HEADS // G
    GF = D // G
    V1 = HD + 1
    R = 3 * HD
    RM = R + 2
    SCALE = float(HD) ** -0.5
    NEG = -1e30
    B_STEPS = [(hf, i) for hf in range(2) for i in range(4 * hf + 4)]
    NB = len(B_STEPS)
    DIAGONAL = [n for n, (hf, i) in enumerate(B_STEPS) if i >= 4 * hf]
    A_UNITS = [(i, s, h) for i in range(NQ) for s in range(1 + i // 4) for h in range(GH)]
    NA = len(A_UNITS)
    AHEAD = NA // 2
    PER = NA // NB
    MAX_T = AHEAD // PER + 1
    SPREAD = 6 * GH * 16
    PLACE = 2 * GH * 16
    assert GH == 4 and D // G == 64 and PER * NB == NA and AHEAD % PER == 0
    with ExitStack() as c:
        def sb(name, shape, dt=F32):
            return c.enter_context(nc.sbuf_tensor(f"s_{name}", shape, dt))

        def ps(name, shape):
            return c.enter_context(nc.psum_tensor(f"s_{name}", shape, F32))

        sem = semaphores(nc, c, "s")

        def ring(name, n):
            return [sem(f"{name}{i}") for i in range(n)]

        QKR = sb("QKR", [P, L])
        QKh = sb("QKh", [P, L], F32R)
        QKl = sb("QKl", [P, L], F32R)
        QO = [sb(f"QO{i}", [P, 2, L], F32R) for i in range(4)]
        KO = [sb(f"KO{i}", [P, 2, L], F32R) for i in range(4)]
        VG = [sb(f"VG{i}", [P, NQ, GH * V1]) for i in range(4)]
        PR = sb("PR", [P, 4, 2, W])
        MX = sb("MX", [P, GH, NQ, 2])
        NM = sb("NM", [P, GH * NQ])
        NMh = sb("NMh", [GH * NQ, P], F32R)
        NMl = sb("NMl", [GH * NQ, P], F32R)
        OS = sb("OS", [P, W])
        RC = sb("RC", [P, 4, GH])
        identb = sb("identb", [P, P], BF16)
        zero_b = sb("zero_b", [P, P], BF16)
        neg = sb("neg", [P, P], BF16)
        ps_a = [ps(f"ps_a{i}", [P, W]) for i in range(2)]
        ps_b = [ps(f"ps_b{i}", [P, 2, W]) for i in range(2)]
        ps_o = ps("ps_o", [P, W])
        ps_t = ps("ps_t", [P, W])
        ATT2 = ATT[:, :, :].rearrange("p t d -> p (t d)")
        V2 = V[:, :, :, :].rearrange("p t h e -> p t (h e)")

        consts = sem("consts")
        presets = sem("presets")
        raw_in = sem("raw_in")
        hi_done = sem("hi_done")
        split = sem("split")
        values = sem("values")
        operands = ring("operands", 4)
        a_done = sem("a_done")
        a_read = sem("a_read")
        max_ready = sem("max_ready")
        maxT_done = sem("maxT_done")
        maxh_done = sem("maxh_done")
        maxl_done = sem("maxl_done")
        max_rows = ring("max_rows", 4)
        b_done = sem("b_done")
        exp_done = sem("exp_done")
        masked = sem("masked")
        pv_done = sem("pv_done")
        o_copied = sem("o_copied")
        oT_done = sem("oT_done")
        recip = sem("recip")
        att_done = sem("att_done")

        block = c.enter_context(nc.Block())

        def turn(g, k, back):
            return g - back, (k - back) % 4

        @block.sync
        def _(sp):
            def spread(g, k):
                sp.wait_ge(split, g + 1)
                for dst, first_row, parts in ((QO, 0, (QKh, QKh, QKl)), (KO, GF, (QKh, QKl, QKh))):
                    for r, src in enumerate(parts):
                        for h in range(GH):
                            at, to = first_row + h * HD, 64 * (h % 2) + r * HD
                            sp.dma_start(dst[k][to:to + HD, h // 2, :].bitcast(F32),
                                         src[at:at + HD, :].bitcast(F32))\
                                .then_inc(operands[k], 16)

            def place_max(g, k):
                sp.wait_ge(maxh_done, g + 1)
                sp.wait_ge(maxl_done, g + 1)
                for r, src in enumerate((NMh, NMl)):
                    for h in range(GH):
                        to = 64 * (h % 2) + R + r
                        sp.dma_start(QO[k][to:to + 1, h // 2, :].bitcast(F32),
                                         src[h * NQ:(h + 1) * NQ, :].bitcast(F32))\
                            .then_inc(max_rows[k], 16)

            sp.wait_ge(presets, 1)
            for g in range(3):
                spread(g, g)
            place_max(0, 0)
            for g, k in steps(sp, NG, 4):
                if until(g, 1, NG):
                    place_max(g + 1, (k + 1) % 4)
                if until(g, 3, NG):
                    spread(g + 3, (k + 3) % 4)

        @block.gpsimd
        def _(pool):
            nc.gpsimd.memset(zero_b[:, :], 0.0).then_inc(consts, 1)
            pool.wait_ge(consts, 1)
            nc.gpsimd.affine_select(out=neg[:, :], in_=zero_b[:, :], compare_op=ALU.is_ge, fill=NEG, base=0,
                                    pattern=[[-1, P]], channel_multiplier=1).then_inc(consts, 1)
            nc.gpsimd.tensor_copy(identb[:, :], ident[:, :]).then_inc(consts, 1)

            def load(g):
                pool.dma_start(QKR[:, :], qk_dram[g // G, g % G, :, :]).then_inc(raw_in, 16)

            def prepare(g, k):
                pool.wait_ge(raw_in, 16 * (g + 1))
                if since(g, 1):
                    p, pk = turn(g, k, 1)
                    pool.wait_ge(operands[pk], SPREAD * (quarter(p, pk) + 1))
                if g >= 4:
                    pool.wait_ge(pv_done, NB * (g - 3))
                nc.gpsimd.tensor_copy(QKh[:, :], QKR[:, :]).then_inc(hi_done, 1)
                pool.wait_ge(hi_done, g + 1)
                nc.gpsimd.tensor_tensor(QKl[:, :], QKR[:, :], QKh[:, :].bitcast(F32), ALU.subtract).then_inc(split, 1)
                if g + 1 < NG:
                    pool.wait_ge(split, g + 1)
                    load(g + 1)
                batch = V2[:, ds(quarter(g, k) * NQ, NQ), k * GH * V1:(k + 1) * GH * V1]
                nc.gpsimd.tensor_copy(VG[k][:, :, :], batch).then_inc(values, 1)

            load(0)
            for g in range(3):
                prepare(g, g)
            for g in range(NG):
                k = g % 4
                for n in range(NB):
                    if n in DIAGONAL:
                        for pair in range(2):
                            u = 2 * n + pair
                            pool.wait_ge(exp_done, 2 * NB * g + u + 1)
                            tile = PR[:, u % 4, :, 0:P]
                            nc.gpsimd.affine_select(out=tile, in_=tile, compare_op=ALU.is_ge, fill=0.0, base=0,
                                                    pattern=[[0, 2], [1, P]], channel_multiplier=-1)\
                                .then_inc(masked, 1)
                    if n == 3 and until(g, 3, NG):
                        prepare(g + 3, (k + 3) % 4)

        @block.scalar
        def _(act):
            def max_high(g, k):
                act.wait_ge(maxT_done, g + 1)
                if since(g, 1):
                    p, pk = turn(g, k, 1)
                    act.wait_ge(max_rows[pk], PLACE * (quarter(p, pk) + 1))
                nc.scalar.activation(NMh[:, :], ps_t[0:GH * NQ, 0:P], ACT.Copy).then_inc(maxh_done, 1)

            def copy_output(g, hf):
                act.wait_ge(pv_done, NB * g + (4 if hf == 0 else NB))
                if hf == 1 or since(g, 1):
                    act.wait_ge(oT_done, 2 * g + hf)
                nc.scalar.activation(OS[:, :], ps_o[:, :], ACT.Copy).then_inc(o_copied, 1)

            max_high(0, 0)
            for g, k in steps(act, NG, 4):
                for n, (hf, i) in enumerate(B_STEPS):
                    lo = max(0, i * P - hf * W)
                    for pair in range(2):
                        u = 2 * n + pair
                        act.wait_ge(b_done, 2 * NB * g + u + 1)
                        if n >= 2 or since(g, 1):
                            act.wait_ge(pv_done, NB * g + n - 1)
                        nc.scalar.activation(PR[:, u % 4, :, 0:W - lo], ps_b[u % 2][:, :, lo:W], ACT.Exp,
                                             scale=SCALE).then_inc(exp_done, 1)
                    if n == 4:
                        copy_output(g, 0)
                    if n == MAX_T and until(g, 1, NG):
                        max_high(g + 1, (k + 1) % 4)
                copy_output(g, 1)

        @block.vector
        def _(dve):
            for k in range(4):
                for r in (32, 96):
                    nc.vector.memset(KO[k][r:r + 32, :, :].bitcast(F32), 1.0)
            nc.vector.memset(ps_o[:, :], 0.0)
            nc.vector.memset(MX[:, :, :, :], -3e38).then_inc(presets, 1)
            dve.wait_ge(presets, 1)

            def a_units(g, units):
                for v in units:
                    i, s, h = A_UNITS[v]
                    if v == 0 and since(g, 1):
                        dve.wait_ge(max_ready, g)
                    dve.wait_ge(a_done, NA * g + v + 1)
                    keys = min((i + 1) * P - s * W, W)
                    nc.vector.tensor_reduce(MX[:, h, i, s:s + 1], ps_a[v % 2][:, 0:keys], AX.X,
                                            ALU.max).then_inc(a_read, 1)

            def combine(g):
                dve.wait_ge(a_read, NA * (g + 1))
                if since(g, 1):
                    dve.wait_ge(maxT_done, g)
                nc.vector.tensor_reduce(NM[:, :].rearrange("p (h i) -> p h i", h=GH), MX[:, :, :, :], AX.X,
                                        ALU.max, negate=True).then_inc(max_ready, 1)

            def max_low(g):
                dve.wait_ge(maxh_done, g + 1)
                nc.vector.tensor_tensor(NMl[:, :], ps_t[0:GH * NQ, 0:P], NMh[:, :].bitcast(F32),
                                        ALU.subtract).then_inc(maxl_done, 1)

            def normalise(g, k, hf):
                turned = ps_t[:, :].rearrange("p (j h r) -> p j h r", j=4, h=GH)
                dve.wait_ge(oT_done, 2 * g + hf + 1)
                if hf == 1 or since(g, 1):
                    dve.wait_ge(att_done, 2 * g + hf)
                nc.vector.reciprocal(RC[:, :, :], turned[:, :, :, HD]).then_inc(recip, 1)
                dve.wait_ge(recip, 2 * g + hf + 1)
                half_rows = ATT2[:, ds((quarter(g, k) * NQ + 4 * hf) * D, 4 * D)].rearrange("p (j d) -> p j d", j=4)
                nc.vector.tensor_tensor(
                    half_rows[:, :, k * GF:(k + 1) * GF].rearrange("p j (h e) -> p j h e", h=GH),
                    turned[:, :, :, 0:HD], RC[:, :, :].unsqueeze(3).to_broadcast([P, 4, GH, HD]),
                    ALU.mult).then_inc(att_done, 1)

            a_units(0, range(NA))
            combine(0)
            max_low(0)
            a_units(1, range(AHEAD))
            for g, k in steps(dve, NG, 4):
                for n in range(NB):
                    first = n * PER
                    if first < NA - AHEAD:
                        if until(g, 1, NG):
                            a_units(g + 1, range(AHEAD + first, AHEAD + first + PER))
                            if first + PER == NA - AHEAD:
                                combine(g + 1)
                    elif until(g, 2, NG):
                        a_units(g + 2, range(first - NA + AHEAD, first - NA + AHEAD + PER))
                    if n == 1 and since(g, 1):
                        normalise(*turn(g, k, 1), 1)
                    if n == MAX_T - 1:
                        normalise(g, k, 0)
                    if n == MAX_T and until(g, 1, NG):
                        max_low(g + 1)
            normalise(NG - 1, 3, 1)

        @block.tensor
        def _(pe):
            def a_units(g, k, units):
                for v in range(units[0], units[-1] + 1, 2):
                    i, s, _ = A_UNITS[v]
                    keys = min((i + 1) * P - s * W, W)
                    diagonal = s == i // 4
                    if v == 0:
                        pe.wait_ge(operands[k], SPREAD * (quarter(g, k) + 1))
                    for w in (v, v + 1):
                        if w >= 2 or since(g, 1):
                            pe.wait_ge(a_read, NA * g + w - 1)
                        if diagonal:
                            nc.tensor.matmul(ps_a[w % 2][:, keys - P:keys], identb[:, :], neg[:, :], start=True,
                                             stop=False, skip_group_check=True)
                    for w in (v, v + 1):
                        h = A_UNITS[w][2]
                        r = 64 * (h % 2)
                        nc.tensor.matmul(ps_a[w % 2][:, 0:keys], QO[k][r:r + R, h // 2, i * P:(i + 1) * P],
                                         KO[k][r:r + R, h // 2, s * W:s * W + keys], start=not diagonal, stop=True,
                                         skip_group_check=True).then_inc(a_done, 1)

            def turn_max(g):
                pe.wait_ge(max_ready, g + 1)
                if since(g, 1):
                    pe.wait_ge(att_done, 2 * g - 1)
                nc.tensor.transpose(ps_t[0:GH * NQ, 0:P], NM[:, :], ident[:, :]).then_inc(maxT_done, 1)

            def b_step(g, k, n):
                hf, i = B_STEPS[n]
                lo = max(0, i * P - hf * W)
                if n == 0:
                    pe.wait_ge(operands[k], SPREAD * (quarter(g, k) + 1))
                    pe.wait_ge(max_rows[k], PLACE * (quarter(g, k) + 1))
                for pair in range(2):
                    u = 2 * n + pair
                    if u >= 2 or since(g, 1):
                        pe.wait_ge(exp_done, 2 * NB * g + u - 1)
                    for h in range(2):
                        last = nc.tensor.matmul(ps_b[pair][:, h, lo:W], KO[k][64 * h:64 * h + RM, pair, i * P:(i + 1) * P],
                                                QO[k][64 * h:64 * h + RM, pair, hf * W + lo:(hf + 1) * W],
                                                start=True, stop=True)
                    last.then_inc(b_done, 1)

            def pv_step(g, k, n):
                hf, i = B_STEPS[n]
                lo = max(0, i * P - hf * W)
                if n == 0:
                    pe.wait_ge(values, g + 1)
                if i == 0 and (n > 0 or since(g, 1)):
                    pe.wait_ge(o_copied, 2 * g + hf)
                pe.wait_ge(exp_done, 2 * NB * g + 2 * n + 2)
                if n in DIAGONAL:
                    pe.wait_ge(masked, 2 * len(DIAGONAL) * g + 2 * DIAGONAL.index(n) + 2)
                for h in range(GH):
                    last = nc.tensor.matmul(ps_o[32 * h:32 * h + V1, lo:W], VG[k][:, i, h * V1:(h + 1) * V1],
                                            PR[:, (2 * n + h // 2) % 4, h % 2, 0:W - lo],
                                            start=i == 0, stop=i == 4 * hf + 3, skip_group_check=True)
                last.then_inc(pv_done, 1)

            def turn_output(g, hf):
                pe.wait_ge(o_copied, 2 * g + hf + 1)
                if hf == 1:
                    if until(g, 1, NG):
                        pe.wait_ge(maxl_done, g + 2)
                    else:
                        pe.wait_ge(att_done, 2 * g + 1)
                elif since(g, 1):
                    pe.wait_ge(att_done, 2 * g)
                else:
                    pe.wait_ge(maxl_done, 1)
                for j in range(4):
                    last = nc.tensor.transpose(ps_t[:, j * P:(j + 1) * P], OS[:, j * P:(j + 1) * P], ident[:, :])
                last.then_inc(oT_done, 1)

            pe.wait_ge(consts, 3)
            pe.wait_ge(presets, 1)
            a_units(0, 0, range(NA))
            turn_max(0)
            a_units(1, 1, range(AHEAD))
            for g, k in steps(pe, NG, 4):
                for n in range(NB):
                    b_step(g, k, n)
                    first = n * PER
                    if first < NA - AHEAD:
                        if until(g, 1, NG):
                            a_units(g + 1, (k + 1) % 4, range(AHEAD + first, AHEAD + first + PER))
                    elif until(g, 2, NG):
                        a_units(g + 2, (k + 2) % 4, range(first - NA + AHEAD, first - NA + AHEAD + PER))
                    if n >= 1:
                        pv_step(g, k, n - 1)
                    if n == 1 and since(g, 1):
                        turn_output(g - 1, 1)
                    if n == MAX_T - 1:
                        turn_output(g, 0)
                    if n == MAX_T and until(g, 1, NG):
                        turn_max(g + 1)
                pv_step(g, k, NB - 1)
            turn_output(NG - 1, 1)


def output_stage(nc, S, X, ST, MV, ident, ATT, w_out, b_out, out_dram):
    D, NT = S.D, S.NT
    with ExitStack() as c:
        def sb(name, shape, dt=F32):
            return c.enter_context(nc.sbuf_tensor(f"o_{name}", shape, dt))

        def ps(name):
            return [c.enter_context(nc.psum_tensor(f"o_{name}{i}", [P, 512], F32)) for i in range(2)]

        sem = semaphores(nc, c, "o")

        WR = sb("WR", [P, 2, D])
        Ws = [sb("Wh", [P, 2, D], F32R), sb("Wl", [P, 2, D], F32R)]
        BO = sb("BO", [P, D])
        AT = sb("AT", [P, 2, D])
        xs = [sb("ah", [P, 2, D], F32R), sb("al", [P, 2, D], F32R)]
        ST2 = ST[:, :, :].rearrange("p t s -> p (t s)")
        ps_x, ps_y = ps("ps_x"), ps("ps_y")
        X2 = X[:, :, :].rearrange("p t d -> p (t d)")
        ATT2 = ATT[:, :, :].rearrange("p t d -> p (t d)")

        weights_in = sem("weights_in")
        weights = sem("weights")
        row_ready = sem("row_ready")
        biased = sem("biased")
        xT_done = sem("xT_done")
        xh_done = sem("xh_done")
        xl_done = sem("xl_done")
        y_done = sem("y_done")
        x_done = sem("x_done")
        stats = sem("stats")
        stored = sem("stored")

        block = c.enter_context(nc.Block())

        @block.sync
        def _(sp):
            sp.dma_start(WR[:, :, :], w_out.rearrange("(c p) f -> p c f", p=P)).then_inc(weights_in, 16)
            sp.dma_start(BO[:, :], b_out.rearrange("(a f) -> a f", a=1).to_broadcast([P, D])).then_inc(weights_in, 16)
            if out_dram is not None:
                for t, k in steps(sp, NT, 4):
                    sp.wait_ge(x_done, t + 1)
                    sp.dma_start(out_dram[ds(t * P, P), :], X2[:, ds(t * D, D)]).then_inc(stored, 16)
                sp.wait_ge(stored, 16 * NT)

        @block.gpsimd
        def _(pool):
            pool.wait_ge(weights_in, 32)
            for t, k in steps(pool, NT, 4):
                x_t = X2[:, ds(t * D, D)]
                nc.gpsimd.tensor_tensor(x_t, x_t, BO[:, :], ALU.add).then_inc(biased, 1)

        @block.scalar
        def _(act):
            def fix_rows(t, k):
                if since(t, 2):
                    act.wait_ge(xT_done, t - 1)
                nc.scalar.activation(AT[:, k % 2, :], ATT2[:, ds(t * D, D)], ACT.Copy).then_inc(row_ready, 1)

            fix_rows(0, 0)
            fix_rows(1, 1)
            for t, k in steps(act, NT, 4):
                if until(t, 2, NT):
                    fix_rows(t + 2, (k + 2) % 4)
                act.wait_ge(xT_done, t + 1)
                if since(t, 2):
                    act.wait_ge(y_done, t - 1)
                nc.scalar.activation(xs[0][:, k % 2, :], ps_x[k % 2][:, 0:D], ACT.Copy).then_inc(xh_done, 1)

        @block.vector
        def _(dve):
            dve.wait_ge(weights_in, 32)
            nc.vector.tensor_copy(Ws[0][:, :, :], WR[:, :, :]).then_inc(weights, 1)
            dve.wait_ge(weights, 1)
            nc.vector.tensor_tensor(Ws[1][:, :, :], WR[:, :, :], Ws[0][:, :, :].bitcast(F32),
                                    ALU.subtract).then_inc(weights, 1)

            def x_low(t, k):
                dve.wait_ge(xh_done, t + 1)
                nc.vector.tensor_tensor(xs[1][:, k % 2, :], ps_x[k % 2][:, 0:D],
                                        xs[0][:, k % 2, :].bitcast(F32), ALU.subtract).then_inc(xl_done, 1)

            def statistics(t):
                nc.vector.bn_stats(ST2[:, ds(6 * t, 6)], X2[:, ds(t * D, D)]).then_inc(stats, 1)

            x_low(0, 0)
            for t, k in steps(dve, NT, 4):
                if until(t, 1, NT):
                    x_low(t + 1, (k + 1) % 4)
                x_t = X2[:, ds(t * D, D)]
                dve.wait_ge(y_done, t + 1)
                dve.wait_ge(biased, t + 1)
                if since(t, 1):
                    dve.wait_ge(x_done, t)
                nc.vector.tensor_tensor(x_t, ps_y[k % 2][:, 0:D], x_t, ALU.add).then_inc(x_done, 1)
                if out_dram is None and since(t, 1):
                    statistics(t - 1)
            if out_dram is None:
                dve.wait_ge(x_done, NT)
                statistics(NT - 1)

        @block.tensor
        def _(pe):
            def transpose_x(t, k):
                pe.wait_ge(row_ready, t + 1)
                if since(t, 2):
                    pe.wait_ge(xl_done, t - 1)
                for c in range(2):
                    last = nc.tensor.transpose(ps_x[k % 2][:, c * P:(c + 1) * P], AT[:, k % 2, c * P:(c + 1) * P],
                                               ident[:, :])
                last.then_inc(xT_done, 1)

            transpose_x(0, 0)
            pe.wait_ge(weights, 2)
            for t, k in steps(pe, NT, 4):
                if until(t, 1, NT):
                    transpose_x(t + 1, (k + 1) % 4)
                pe.wait_ge(xl_done, t + 1)
                if since(t, 2):
                    pe.wait_ge(x_done, t - 1)
                for i, (c, a, b) in enumerate(split_passes(2)):
                    last = nc.tensor.matmul(ps_y[k % 2][:, 0:D], xs[a][:, k % 2, c * P:(c + 1) * P],
                                            Ws[b][:, c, :], start=i == 0, stop=i == 5)
                last.then_inc(y_done, 1)


def macaron(nc, PARTS, x, w_up, w_down, gate, w_qkv, b_qk, b_v, w_out, b_out, out):
    S = Shapes(x, w_up, w_down, gate)
    x_rows = x.rearrange("b l d -> (b l) d")
    out_rows = out.rearrange("b l d -> (b l) d")
    with ExitStack() as ctx:
        xn_dram = nc.dram_tensor("xn_scratch", (S.T, S.D), F32, kind="Internal").ap()
        y_dram = nc.dram_tensor("y_scratch", (S.NJ * P, S.D), F32, kind="Internal").ap()
        X = ctx.enter_context(nc.sbuf_tensor("X", [P, S.NT, S.D], F32))
        ST = ctx.enter_context(nc.sbuf_tensor("ST", [P, S.NT, 6], F32))
        MV = ctx.enter_context(nc.sbuf_tensor("MV", [P, S.NT, 2], F32))
        ident = ctx.enter_context(nc.sbuf_tensor("ident", [P, P], F32))
        x_in = nc.alloc_semaphore("x_in")
        ident_done = nc.alloc_semaphore("ident_done")
        with nc.Block() as block:
            @block.sync
            def _(sp):
                sp.dma_start(X[:, :, :], x_rows.rearrange("(t p) d -> p t d", p=P)).then_inc(x_in, 16)
                sp.wait_ge(x_in, 16)

            @block.gpsimd
            def _(pool):
                nc.gpsimd.memset(ident[:, :], 0.0).then_inc(ident_done, 1)
                pool.wait_ge(ident_done, 1)
                nc.gpsimd.affine_select(out=ident[:, :], in_=ident[:, :], compare_op=ALU.not_equal, fill=1.0,
                                        base=0, pattern=[[-1, P]], channel_multiplier=1).then_inc(ident_done, 1)
                pool.wait_ge(ident_done, 2)
        if "1" in PARTS:
            feed_forward(nc, "f1", S, X, ST, MV, ident, w_up, w_down, gate, xn_dram, y_dram,
                         out_rows if PARTS == "1" else None, True)
        if "a" in PARTS:
            attention(nc, S, X, ST, MV, ident, w_qkv, b_qk, b_v, w_out, b_out, out_rows if PARTS == "a" else None,
                      PARTS == "a")
        if "2" in PARTS:
            feed_forward(nc, "f2", S, X, ST, MV, ident, w_up, w_down, gate, xn_dram, y_dram, out_rows, False)


def kernel(**inputs):
    import numpy as np
    import concourse.bacc as _bacc
    from concourse.bass_utils import run_bass_kernel_spmd as _run

    a = {k[3:]: np.asarray(v) for k, v in inputs.items()}
    ff = a["ffn_exp_wg"].shape[1]
    d = a["attn_W_out"].shape[0]
    units = range(a["ffn_shared_wg"].shape[0] // ff)
    gates = [a["ffn_shared_wg"][s * ff:(s + 1) * ff] for s in units] + list(a["ffn_exp_wg"])
    ups = [a["ffn_shared_wu"][s * ff:(s + 1) * ff] for s in units] + list(a["ffn_exp_wu"])
    downs = [a["ffn_shared_wd"][:, s * ff:(s + 1) * ff] for s in units] + list(a["ffn_exp_wd"])
    laid = {
        "x": a["attn_x"],
        "w_up": np.stack([np.concatenate([g, u]).T for g, u in zip(gates, ups)], axis=1),
        "w_down": np.stack([d.T for d in downs]),
        "gate": a["ffn_gate_w"].T,
        "w_qkv": np.concatenate([a["attn_W_qkv"][:2 * d].reshape(2, 4, -1, d).transpose(1, 0, 2, 3).reshape(2 * d, d),
                                 a["attn_W_qkv"][2 * d:]]).T,
        "b_qk": a["attn_b_qkv"].reshape(3, 4, -1)[:2].transpose(0, 2, 1).reshape(-1, 4),
        "b_v": a["attn_b_qkv"].reshape(3, -1)[2],
        "w_out": a["attn_W_out"].T,
        "b_out": a["attn_b_out"],
    }
    nc = _bacc.Bacc("TRN2", target_bir_lowering=False, num_devices=1)
    arrays, args = {}, []
    for name, v in laid.items():
        arrays[f"in_{name}"] = np.ascontiguousarray(v)
        args.append(nc.dram_tensor(f"in_{name}", v.shape, mybir.dt.from_np(v.dtype), kind="ExternalInput").ap())
    shape = a["attn_x"].shape
    args.append(nc.dram_tensor("out", shape, F32, kind="ExternalOutput").ap())
    macaron(nc, "1a2", *args)
    r = _run(nc, [arrays], core_ids=[0])
    return r.results[0]["out"]
```

```python
from contextlib import ExitStack

import concourse.bass as bass
from concourse import mybir

ALU = mybir.AluOpType
ACT = mybir.ActivationFunctionType
AX = mybir.AxisListType
F32 = mybir.dt.float32
F32R = mybir.dt.float32r
BF16 = mybir.dt.bfloat16
I32 = mybir.dt.int32
U32 = mybir.dt.uint32
ds = bass.ds

P = 128
TOP_K = 2
ROUTED_SCALE = 2.5
HALF = 0.5
EPS = 1e-5


def steps(eng, total, unroll):
    for n in range(unroll):
        yield n, n
    with eng.Fori(1, total // unroll - 1) as i:
        for k in range(unroll):
            yield i * unroll + k, k
    for n in range(total - unroll, total):
        yield n, n % unroll


def since(n, k):
    return not isinstance(n, int) or n >= k


def until(n, k, total):
    return not isinstance(n, int) or n + k < total


def half(n, k):
    return n // 2 if isinstance(n, int) else (n - k % 2) // 2


def semaphores(nc, stack, tag):
    made = []

    def clear():
        nc.clear_and_free_semaphores(made)
        nc.all_engine_barrier()

    def sem(name):
        made.append(nc.alloc_semaphore(f"{tag}_{name}"))
        return made[-1]

    stack.callback(clear)
    return sem


class Shapes:
    def __init__(self, x, w_up, w_down, gate):
        self.B, self.L, self.D = x.shape
        self.T = self.B * self.L
        self.NT = self.T // P
        self.NC = self.D // P
        self.NU = w_up.shape[1]
        self.E = gate.shape[1]
        self.NS = self.NU - self.E
        self.FF = w_up.shape[2] // 2
        self.NJ = self.T * TOP_K // P + self.E
        self.TAIL = self.FF - P
        self.HD = 16
        self.HEADS = self.D // self.HD
        self.G = self.HEADS // 4
        assert self.NS == 2 and self.NC == 2 and 0 < self.TAIL < P and self.NT % 4 == 0 and self.NJ % 4 == 0


def feed_forward(nc, tag, S, X, ST, MV, ident, w_up, w_down, gate, xn_dram, y_dram, out_dram, first):
    D, NT, NU, NS, FF, E, NJ, TAIL = S.D, S.NT, S.NU, S.NS, S.FF, S.E, S.NJ, S.TAIL
    NG = NT * TOP_K
    with ExitStack() as ctx:
        def sb(name, shape, dt=F32):
            return ctx.enter_context(nc.sbuf_tensor(f"{tag}_{name}", shape, dt))

        WUh = sb("WUh", [P, 2, NU * 2 * FF], F32R)
        WUl = sb("WUl", [P, 2, NU * 2 * FF], F32R)
        WDh = [sb("WDh0", [P, NU * D], F32R), sb("WDh1", [TAIL, NU * D], F32R)]
        WDl = [sb("WDl0", [P, NU * D], F32R), sb("WDl1", [TAIL, NU * D], F32R)]
        RSTD = sb("RSTD", [P, NT])
        W12 = sb("W12", [P, TOP_K, NT])
        slots_u = sb("slots_u", [P, TOP_K, NT], U32)
        tok_u = sb("tok_u", [P, NJ], U32)
        unit_i = sb("unit_i", [P, NJ], I32)
        X2 = X[:, :, :].rearrange("p t d -> p (t d)")
        MV2 = MV[:, :, :].rearrange("p t s -> p (t s)")

        with ExitStack() as c1:
            sem = semaphores(nc, c1, f"{tag}1")

            def sb1(name, shape, dt=F32):
                return c1.enter_context(nc.sbuf_tensor(f"{tag}1_{name}", shape, dt))

            def ps1(name, shape):
                return c1.enter_context(nc.psum_tensor(f"{tag}1_{name}", shape, F32))

            XN = sb1("XN", [P, 4, D])
            xh = sb1("xh", [P, 2, D], F32R)
            xl = sb1("xl", [P, 2, D], F32R)
            GW = sb1("GW", [P, 2, E])
            GWh = sb1("GWh", [P, 2, E], F32R)
            GWl = sb1("GWl", [P, 2, E], F32R)
            stage = sb1("stage", [P, 2, 4 * FF])
            stageD = sb1("stageD", [P, 2, 2, D])
            ps_x = [ps1(f"ps_x{i}", [P, D]) for i in range(2)]
            ps_gate = ps1("ps_gate", [P, NT * E])
            ps_pre = ps1("ps_pre", [P, E * NT])
            ps_tot = ps1("ps_tot", [P, E * NT])
            ps_tok = ps1("ps_tok", [P, 2 * NJ])
            SC = sb1("SC", [P, NT, E])
            SC2 = sb1("SC2", [P, NT, E])
            EQ = sb1("EQ", [P, NT, E])
            PR = sb1("PR", [P, NT, E])
            OH = sb1("OH", [P, TOP_K, NT, E])
            SEL = sb1("SEL", [P, E, NT], BF16)
            M12 = sb1("M12", [P, TOP_K, NT])
            PMAX = sb1("PMAX", [P, NT])
            DEN = sb1("DEN", [P, NT])
            prio_i = sb1("prio_i", [P, E], I32)
            prio = sb1("prio", [P, E])
            lower_t = sb1("lower_t", [P, P], BF16)
            ones_b = sb1("ones_b", [P, P], BF16)
            ones_f = sb1("ones_f", [P, E * NT])
            CUM = sb1("CUM", [P, E, NT])
            EXC = sb1("EXC", [P, E, NT])
            SLOT = sb1("SLOT", [P, E, NT])
            CNT = sb1("CNT", [P, E])
            CNTi = sb1("CNTi", [P, E], I32)
            NTI = sb1("NTI", [P, E])
            CT = sb1("CT", [P, E])
            BASE = sb1("BASE", [P, E])
            SL = sb1("SL", [P, TOP_K, NT])
            SLi = sb1("SLi", [P, TOP_K, NT], I32)
            Ri = sb1("Ri", [P, NG], I32)
            Ti = sb1("Ti", [P, NG], I32)
            RF = sb1("RF", [P, NG])
            TF = sb1("TF", [P, NG])
            row_i = sb1("row_i", [P, P], I32)
            row_f = sb1("row_f", [P, P])
            row_b = sb1("row_b", [P, P], BF16)
            par_i = sb1("par_i", [P, 1], I32)
            par_f = sb1("par_f", [P, 1])
            GE = sb1("GE", [P, NJ, E])
            UF = sb1("UF", [P, NJ])
            tile_of = sb1("tile_of", [P, NG])
            RSEL = sb1("RSEL", [P, 4, P], BF16)
            TSEL = sb1("TSEL", [P, 4, 2 * NJ], BF16)
            tokf = sb1("tokf", [P, 2 * NJ])

            raw_in = [sem("raw_in0"), sem("raw_in1")]
            gate_in = sem("gate_in")
            consts = sem("consts")
            chain = sem("chain")
            chain_pool = sem("chain_pool")
            split_w = sem("split_w")
            rstd_in = sem("rstd_in")
            rstd_out = sem("rstd_out")
            stats_done = sem("stats_done")
            xn_ready = sem("xn_ready")
            xn_out = [sem(f"xn_out{i}") for i in range(4)]
            xT_done = sem("xT_done")
            xh_done = sem("xh_done")
            xl_done = sem("xl_done")
            gate_w = sem("gate_w")
            gate_done = sem("gate_done")
            sig_done = sem("sig_done")
            sel_done = sem("sel_done")
            pre_done = sem("pre_done")
            pre_copied = sem("pre_copied")
            onehot = sem("onehot")
            tok_done = sem("tok_done")

            PRE = sb1("PRE", [P, E * NT])
            TOT = sb1("TOT", [P, E * NT])

            block = c1.enter_context(nc.Block())

            @block.sync
            def _(sp):
                sp.dma_start(GW[:, :, :], gate.rearrange("(c p) e -> p c e", p=P)).then_inc(gate_in, 16)
                def load_unit(u):
                    b = u % 2
                    if u >= 2:
                        sp.wait_ge(split_w, u - 1)
                    sp.dma_start(stage[:, b, :].rearrange("p (c f) -> p c f", c=2),
                                 w_up[:, u, :].rearrange("(c p) f -> p c f", p=P)).then_inc(raw_in[b], 16)
                    sp.dma_start(stageD[:, b, 0, :], w_down[u, 0:P, :]).then_inc(raw_in[b], 16)
                    sp.dma_start(stageD[0:TAIL, b, 1, :], w_down[u, P:FF, :]).then_inc(raw_in[b], 16)
                load_unit(0)
                load_unit(1)
                for u in range(2, NU):
                    load_unit(u)
                for k in range(4):
                    sp.wait_ge(xn_out[k], 16 * (NT // 4))

            @block.gpsimd
            def _(pool):
                nc.gpsimd.iota(prio_i[:, :], pattern=[[-1, E]], base=E, channel_multiplier=0).then_inc(consts, 1)
                nc.gpsimd.iota(row_i[:, :], pattern=[[1, P]], base=0, channel_multiplier=0).then_inc(consts, 1)
                nc.gpsimd.iota(par_i[:, :], pattern=[[0, 1]], base=0, channel_multiplier=1).then_inc(consts, 1)
                nc.gpsimd.memset(ones_b[:, :], 1.0).then_inc(consts, 1)
                nc.gpsimd.memset(ones_f[:, :], 1.0).then_inc(consts, 1)
                pool.wait_ge(consts, 5)
                nc.gpsimd.affine_select(out=lower_t[:, :], in_=ones_b[:, :], compare_op=ALU.is_gt, fill=0.0,
                                        base=0, pattern=[[1, P]], channel_multiplier=-1).then_inc(consts, 1)
                for u in range(NU):
                    b = u % 2
                    pool.wait_ge(raw_in[b], 48 * (u // 2 + 1))
                    up = stage[:, b, :].rearrange("p (c f) -> p c f", c=2)
                    wu = slice(u * 2 * FF, (u + 1) * 2 * FF)
                    wd = slice(u * D, (u + 1) * D)
                    nc.gpsimd.tensor_copy(WUh[:, :, wu], up).then_inc(chain_pool, 1)
                    nc.gpsimd.tensor_copy(WDh[0][:, wd], stageD[:, b, 0, :]).then_inc(chain_pool, 1)
                    nc.gpsimd.tensor_copy(WDh[1][:, wd], stageD[0:TAIL, b, 1, :]).then_inc(chain_pool, 1)
                    pool.wait_ge(chain_pool, 3 * (u + 1))
                    nc.gpsimd.tensor_tensor(WUl[:, :, wu], up, WUh[:, :, wu].bitcast(F32), ALU.subtract)
                    nc.gpsimd.tensor_tensor(WDl[0][:, wd], stageD[:, b, 0, :], WDh[0][:, wd].bitcast(F32), ALU.subtract)
                    nc.gpsimd.tensor_tensor(WDl[1][:, wd], stageD[0:TAIL, b, 1, :], WDh[1][:, wd].bitcast(F32),
                                            ALU.subtract).then_inc(split_w, 1)

            @block.scalar
            def _(act):
                act.wait_ge(rstd_in, 1)
                nc.scalar.activation(RSTD[:, :], RSTD[:, :], ACT.Sqrt).then_inc(rstd_out, 1)
                for t, k in steps(act, NT, 4):
                    act.wait_ge(xT_done, t + 1)
                    if since(t, 2):
                        act.wait_ge(gate_done, t - 1)
                    nc.scalar.activation(xh[:, k % 2, :], ps_x[k % 2][:, :], ACT.Copy).then_inc(xh_done, 1)
                    act.wait_ge(xn_ready, t + 1)
                    act.dma_start(xn_dram[ds(t * P, P), :], XN[:, k, :]).then_inc(xn_out[k], 16)
                act.wait_ge(gate_done, NT)
                nc.scalar.activation(SC[:, :, :].rearrange("p t e -> p (t e)"), ps_gate[:, :],
                                     ACT.Sigmoid).then_inc(sig_done, 1)
                act.wait_ge(pre_done, 1)
                nc.scalar.activation(PRE[:, :], ps_pre[:, :], ACT.Copy).then_inc(pre_copied, 1)
                nc.scalar.activation(TOT[:, :], ps_tot[:, :], ACT.Copy).then_inc(pre_copied, 1)

            @block.vector
            def _(dve):
                count = [0]

                def link(ins):
                    count[0] += 1
                    ins.then_inc(chain, 1)
                    dve.wait_ge(chain, count[0])

                dve.wait_ge(gate_in, 16)
                link(nc.vector.tensor_copy(GWh[:, :, :], GW[:, :, :]))
                nc.vector.tensor_tensor(GWl[:, :, :], GW[:, :, :], GWh[:, :, :].bitcast(F32),
                                        ALU.subtract).then_inc(gate_w, 1)
                if first:
                    for t in range(NT):
                        last = nc.vector.bn_stats(ST[:, t, :], X[:, t, :])
                    link(last)
                for t in range(NT):
                    last = nc.vector.bn_aggr(MV[:, t, :], ST[:, t, :])
                link(last)
                nc.vector.tensor_scalar(RSTD[:, :], MV[:, :, 1], EPS, None, ALU.add).then_inc(rstd_in, 1)
                dve.wait_ge(rstd_out, 1)
                link(nc.vector.reciprocal(RSTD[:, :], RSTD[:, :]))

                def normalise(t, k):
                    if since(t, 4):
                        dve.wait_ge(xT_done, t - 3)
                        dve.wait_ge(xn_out[k], 16 * quarter(t, k))
                    nc.vector.tensor_scalar(XN[:, k, :], X2[:, ds(t * D, D)], MV2[:, ds(2 * t, 1)],
                                            RSTD[:, ds(t, 1)], ALU.subtract, ALU.mult).then_inc(xn_ready, 1)

                def quarter(t, k):
                    return t // 4 if isinstance(t, int) else (t - k) // 4

                normalise(0, 0)
                for t, k in steps(dve, NT, 4):
                    if until(t, 1, NT):
                        normalise(t + 1, (k + 1) % 4)
                    dve.wait_ge(xh_done, t + 1)
                    nc.vector.tensor_tensor(xl[:, k % 2, :], ps_x[k % 2][:, :], xh[:, k % 2, :].bitcast(F32),
                                            ALU.subtract).then_inc(xl_done, 1)

                dve.wait_ge(consts, 6)
                link(nc.vector.tensor_copy(prio[:, :], prio_i[:, :]))
                link(nc.vector.tensor_copy(row_f[:, :], row_i[:, :]))
                link(nc.vector.tensor_copy(row_b[:, :], row_i[:, :]))
                link(nc.vector.tensor_copy(par_f[:, :], par_i[:, :]))
                for k in range(TOP_K):
                    link(nc.vector.tensor_copy(tile_of[:, k * NT:(k + 1) * NT], row_i[:, 0:NT]))
                dve.wait_ge(sig_done, 1)
                src = SC
                wide = [P, NT, E]
                for k in range(TOP_K):
                    link(nc.vector.tensor_reduce(M12[:, k, :], src[:, :, :], AX.X, ALU.max))
                    link(nc.vector.tensor_tensor(EQ[:, :, :], src[:, :, :],
                                                 M12[:, k, :].unsqueeze(2).to_broadcast(wide), ALU.is_equal))
                    link(nc.vector.tensor_tensor(PR[:, :, :], EQ[:, :, :],
                                                 prio[:, :].unsqueeze(1).to_broadcast(wide), ALU.mult))
                    link(nc.vector.tensor_reduce(PMAX[:, :], PR[:, :, :], AX.X, ALU.max))
                    link(nc.vector.tensor_tensor(OH[:, k, :, :], PR[:, :, :],
                                                 PMAX[:, :].unsqueeze(2).to_broadcast(wide), ALU.is_equal))
                    if k == 0:
                        link(nc.vector.scalar_tensor_tensor(SC2[:, :, :], OH[:, 0, :, :], -4.0, SC[:, :, :],
                                                            ALU.mult, ALU.add))
                        src = SC2
                nc.vector.tensor_tensor(SEL[:, :, :].rearrange("p e t -> p t e"), OH[:, 0, :, :],
                                        OH[:, 1, :, :], ALU.add).then_inc(sel_done, 1)
                link(nc.vector.tensor_tensor(DEN[:, :], M12[:, 0, :], M12[:, 1, :], ALU.add))
                link(nc.vector.tensor_scalar(DEN[:, :], DEN[:, :], 1e-20, None, ALU.add))
                link(nc.vector.reciprocal(DEN[:, :], DEN[:, :]))
                for k in range(TOP_K):
                    link(nc.vector.scalar_tensor_tensor(W12[:, k, :], M12[:, k, :], ROUTED_SCALE * HALF, DEN[:, :],
                                                        ALU.mult, ALU.mult))

                dve.wait_ge(pre_copied, 2)
                CUMf = CUM[:, :, :].rearrange("p e t -> p (e t)")
                EXCf = EXC[:, :, :].rearrange("p e t -> p (e t)")
                SLOTf = SLOT[:, :, :].rearrange("p e t -> p (e t)")
                link(nc.vector.tensor_tensor_scan(CUMf, ones_f[:, :], TOT[:, :], 0.0, ALU.mult, ALU.add))
                link(nc.vector.tensor_tensor(EXCf, CUMf, TOT[:, :], ALU.subtract))
                link(nc.vector.tensor_tensor(CNT[:, :], CUM[:, :, NT - 1], EXC[:, :, 0], ALU.subtract))
                link(nc.vector.tensor_scalar(CNTi[:, :], CNT[:, :], float(P - 1), None, ALU.add))
                link(nc.vector.tensor_scalar(CNTi[:, :], CNTi[:, :], P.bit_length() - 1, None,
                                             ALU.arith_shift_right))
                link(nc.vector.tensor_copy(NTI[:, :], CNTi[:, :]))
                link(nc.vector.tensor_tensor_scan(CT[:, :], ones_f[:, 0:E], NTI[:, :], 0.0, ALU.mult, ALU.add))
                link(nc.vector.tensor_tensor(BASE[:, :], CT[:, :], NTI[:, :], ALU.subtract))
                link(nc.vector.scalar_tensor_tensor(BASE[:, :], BASE[:, :], float(P), EXC[:, :, 0],
                                                    ALU.mult, ALU.subtract))
                link(nc.vector.tensor_tensor(SLOTf, EXCf, PRE[:, :], ALU.add))
                link(nc.vector.tensor_tensor(SLOT[:, :, :], SLOT[:, :, :],
                                             BASE[:, :].unsqueeze(2).to_broadcast([P, E, NT]), ALU.add))
                for k in range(TOP_K):
                    link(nc.vector.tensor_tensor(EQ[:, :, :], OH[:, k, :, :],
                                                 SLOT[:, :, :].rearrange("p e t -> p t e"), ALU.mult))
                    link(nc.vector.tensor_reduce(SL[:, k, :], EQ[:, :, :], AX.X, ALU.add))
                link(nc.vector.tensor_copy(slots_u[:, :, :], SL[:, :, :]))
                link(nc.vector.tensor_copy(SLi[:, :, :], SL[:, :, :]))
                flat = SLi[:, :, :].rearrange("p k t -> p (k t)")
                link(nc.vector.tensor_scalar(Ri[:, :], flat, P - 1, None, ALU.bitwise_and))
                link(nc.vector.tensor_scalar(Ti[:, :], flat, P.bit_length() - 1, None, ALU.arith_shift_right))
                link(nc.vector.tensor_copy(RF[:, :], Ri[:, :]))
                link(nc.vector.tensor_copy(TF[:, :], Ti[:, :]))

                jw = [P, NJ, E]
                link(nc.vector.tensor_tensor(GE[:, :, :], row_f[:, 0:NJ].unsqueeze(2).to_broadcast(jw),
                                             CT[:, :].unsqueeze(1).to_broadcast(jw), ALU.is_ge))
                link(nc.vector.tensor_reduce(UF[:, :], GE[:, :, :], AX.X, ALU.add))
                link(nc.vector.tensor_scalar(unit_i[:, :], UF[:, :], float(E - 1), float(NS), ALU.min, ALU.add))

                for g, k in steps(dve, NG, 4):
                    if since(g, 4):
                        dve.wait_ge(tok_done, g - 3)
                    nc.vector.tensor_scalar(RSEL[:, k, :], row_b[:, :], RF[:, ds(g, 1)], None, ALU.is_equal)
                    nc.vector.tensor_scalar(TSEL[:, k, 0:NJ], row_b[:, 0:NJ], TF[:, ds(g, 1)], par_f[:, :],
                                            ALU.is_equal, ALU.mult)
                    nc.vector.tensor_scalar(TSEL[:, k, NJ:2 * NJ], row_b[:, 0:NJ], TF[:, ds(g, 1)],
                                            tile_of[:, ds(g, 1)], ALU.is_equal, ALU.mult).then_inc(onehot, 1)
                dve.wait_ge(tok_done, NG)
                link(nc.vector.tensor_copy(tokf[:, :], ps_tok[:, :]))
                link(nc.vector.scalar_tensor_tensor(tok_u[:, :], tokf[:, NJ:2 * NJ], float(P), tokf[:, 0:NJ],
                                                    ALU.mult, ALU.add))

            @block.tensor
            def _(pe):
                def transpose_x(t, k):
                    pe.wait_ge(xn_ready, t + 1)
                    if since(t, 2):
                        pe.wait_ge(xl_done, t - 1)
                    for c in range(2):
                        last = nc.tensor.transpose(ps_x[k % 2][:, c * P:(c + 1) * P], XN[:, k, c * P:(c + 1) * P],
                                                   ident[:, :])
                    last.then_inc(xT_done, 1)

                pe.wait_ge(gate_w, 1)
                transpose_x(0, 0)
                for t, k in steps(pe, NT, 4):
                    if until(t, 1, NT):
                        transpose_x(t + 1, (k + 1) % 4)
                    pe.wait_ge(xl_done, t + 1)
                    passes = [(a, b, c) for c in range(2) for a, b in ((xh, GWh), (xh, GWl), (xl, GWh))]
                    for i, (a, b, c) in enumerate(passes):
                        last = nc.tensor.matmul(ps_gate[:, ds(t * E, E)], a[:, k % 2, c * P:(c + 1) * P], b[:, c, :],
                                                start=i == 0, stop=i == 5)
                    last.then_inc(gate_done, 1)
                pe.wait_ge(sel_done, 1)
                pe.wait_ge(consts, 6)
                sel = SEL[:, :, :].rearrange("p e t -> p (e t)")
                nc.tensor.matmul(ps_pre[:, :], lower_t[:, :], sel, start=True, stop=True)
                nc.tensor.matmul(ps_tot[:, :], ones_b[:, :], sel, start=True, stop=True).then_inc(pre_done, 1)
                for g in range(NG):
                    pe.wait_ge(onehot, g + 1)
                    nc.tensor.matmul(ps_tok[:, :], RSEL[:, g % 4, :], TSEL[:, g % 4, :], start=g == 0,
                                     stop=g == NG - 1).then_inc(tok_done, 1)

        expert_stage(nc, tag, S, ident, WUh, WUl, WDh, WDl, tok_u, unit_i, xn_dram, y_dram)
        shared_stage(nc, tag, S, X, ST, MV, RSTD, W12, slots_u, ident, WUh, WUl, WDh, WDl, y_dram, out_dram)


def split_passes(n_chunks):
    return [(c, a, b) for c in range(n_chunks) for a, b in ((0, 0), (0, 1), (1, 0))]


def expert_stage(nc, tag, S, ident, WUh, WUl, WDh, WDl, tok_u, unit_i, xn_dram, y_dram):
    D, FF, NU, NJ, TAIL = S.D, S.FF, S.NU, S.NJ, S.TAIL
    with ExitStack() as c2:
        def sb(name, shape, dt=F32):
            return c2.enter_context(nc.sbuf_tensor(f"{tag}2_{name}", shape, dt))

        def ps(name):
            return [c2.enter_context(nc.psum_tensor(f"{tag}2_{name}{i}", [P, 512], F32)) for i in range(2)]

        sem = semaphores(nc, c2, f"{tag}2")

        XG = sb("XG", [P, 4, D])
        xs = [sb("xh", [P, 2, D], F32R), sb("xl", [P, 2, D], F32R)]
        SG = sb("SG", [P, 2, FF])
        H = sb("H", [P, 2, 2 * P])
        hs = [sb("hh", [P, 2, 2 * P], F32R), sb("hl", [P, 2, 2 * P], F32R)]
        YS = sb("YS", [P, 4, D])
        ps_x, ps_u, ps_h, ps_y = ps("ps_x"), ps("ps_u"), ps("ps_h"), ps("ps_y")

        zeroed = sem("zeroed")
        gathered = [sem(f"gathered{i}") for i in range(4)]
        xT_done = sem("xT_done")
        xh_done = sem("xh_done")
        xl_done = sem("xl_done")
        up_done = sem("up_done")
        silu_done = sem("silu_done")
        h_ready = sem("h_ready")
        hT_done = sem("hT_done")
        hh_done = sem("hh_done")
        hl_done = sem("hl_done")
        y_done = sem("y_done")
        y_copied = sem("y_copied")
        y_out = [sem(f"y_out{i}") for i in range(4)]

        block = c2.enter_context(nc.Block())

        @block.gpsimd
        def _(pool):
            for j in range(NJ):
                if j >= 4:
                    pool.wait_ge(xT_done, j - 3)
                nc.gpsimd.indirect_dma_start(
                    out=XG[:, j % 4, :], out_offset=None, in_=xn_dram[:, :],
                    in_offset=bass.IndirectOffsetOnAxis(ap=tok_u[:, j:j + 1], axis=0)
                ).then_inc(gathered[j % 4], 16)

        @block.sync
        def _(sp):
            for j, k in steps(sp, NJ, 4):
                sp.wait_ge(y_copied, j + 1)
                sp.dma_start(y_dram[ds(j * P, P), :], YS[:, k, :]).then_inc(y_out[k], 16)
            for k in range(4):
                sp.wait_ge(y_out[k], 16 * (NJ // 4))

        @block.scalar
        def _(act):
            def y_copy(j, k):
                act.wait_ge(y_done, j + 1)
                if since(j, 4):
                    act.wait_ge(y_out[k], 16 * quarter(j, k))
                nc.scalar.activation(YS[:, k, :], ps_y[k % 2][:, 0:D], ACT.Copy).then_inc(y_copied, 1)

            def x_high(j, k):
                act.wait_ge(xT_done, j + 1)
                if since(j, 2):
                    act.wait_ge(up_done, j - 1)
                nc.scalar.activation(xs[0][:, k % 2, :], ps_x[k % 2][:, 0:D], ACT.Copy).then_inc(xh_done, 1)

            def h_high(j, k):
                act.wait_ge(hT_done, j + 1)
                if since(j, 2):
                    act.wait_ge(y_done, j - 1)
                nc.scalar.activation(hs[0][:, k % 2, :], ps_h[k % 2][:, 0:2 * P], ACT.Copy).then_inc(hh_done, 1)

            x_high(0, 0)
            for j, k in steps(act, NJ, 4):
                if until(j, 1, NJ):
                    x_high(j + 1, (k + 1) % 4)
                act.wait_ge(up_done, j + 1)
                if since(j, 2):
                    act.wait_ge(h_ready, j - 1)
                nc.scalar.activation(SG[:, k % 2, :], ps_u[k % 2][:, 0:FF], ACT.Silu).then_inc(silu_done, 1)
                if since(j, 1):
                    h_high(j - 1, (k - 1) % 4)
                if since(j, 2):
                    y_copy(j - 2, (k - 2) % 4)
            h_high(NJ - 1, 3)
            y_copy(NJ - 2, 2)
            y_copy(NJ - 1, 3)

        @block.vector
        def _(dve):
            nc.vector.memset(H[:, :, FF:2 * P], 0.0).then_inc(zeroed, 1)

            def x_low(j, k):
                dve.wait_ge(xh_done, j + 1)
                nc.vector.tensor_tensor(xs[1][:, k % 2, :], ps_x[k % 2][:, 0:D],
                                        xs[0][:, k % 2, :].bitcast(F32), ALU.subtract).then_inc(xl_done, 1)

            def h_low(j, k):
                dve.wait_ge(hh_done, j + 1)
                nc.vector.tensor_tensor(hs[1][:, k % 2, :], ps_h[k % 2][:, 0:2 * P],
                                        hs[0][:, k % 2, :].bitcast(F32), ALU.subtract).then_inc(hl_done, 1)

            x_low(0, 0)
            for j, k in steps(dve, NJ, 4):
                if until(j, 1, NJ):
                    x_low(j + 1, (k + 1) % 4)
                dve.wait_ge(silu_done, j + 1)
                if since(j, 2):
                    dve.wait_ge(hT_done, j - 1)
                nc.vector.tensor_tensor(H[:, k % 2, 0:FF], SG[:, k % 2, :], ps_u[k % 2][:, FF:2 * FF],
                                        ALU.mult).then_inc(h_ready, 1)
                if since(j, 1):
                    h_low(j - 1, (k - 1) % 4)
            h_low(NJ - 1, 3)

        @block.tensor
        def _(pe):
            W_up, W_down = (WUh, WUl), (WDh, WDl)
            units = {}

            def unit_of(j, k, turn=0):
                if (turn, k) not in units:
                    units[turn, k] = pe.value_load(unit_i[0:1, ds(j, 1)], min_val=0, max_val=NU - 1)
                return units[turn, k]

            def transpose_x(j, k):
                pe.wait_ge(gathered[k % 4], 16 * (quarter(j, k % 4) + 1))
                for c in range(2):
                    last = nc.tensor.transpose(ps_x[k % 2][:, c * P:(c + 1) * P], XG[:, k % 4, c * P:(c + 1) * P],
                                               ident[:, :])
                last.then_inc(xT_done, 1)

            def up(j, k):
                unit = unit_of(j, k)
                pe.wait_ge(xl_done, j + 1)
                plan = split_passes(2)
                for i, (c, a, b) in enumerate(plan):
                    last = nc.tensor.matmul(ps_u[k % 2][:, 0:2 * FF], xs[a][:, k % 2, c * P:(c + 1) * P],
                                            W_up[b][:, c, ds(unit * (2 * FF), 2 * FF)],
                                            start=i == 0, stop=i == len(plan) - 1)
                last.then_inc(up_done, 1)

            def transpose_h(j, k):
                if isinstance(j, int) and j == 0:
                    pe.wait_ge(zeroed, 1)
                pe.wait_ge(h_ready, j + 1)
                for c in range(2):
                    last = nc.tensor.transpose(ps_h[k % 2][:, c * P:(c + 1) * P], H[:, k % 2, c * P:(c + 1) * P],
                                               ident[:, :])
                last.then_inc(hT_done, 1)

            def down(j, k, turn=0):
                unit = unit_of(j, k, turn)
                pe.wait_ge(hl_done, j + 1)
                if since(j, 2):
                    pe.wait_ge(y_copied, j - 1)
                plan = split_passes(2)
                for i, (c, a, b) in enumerate(plan):
                    rows = P if c == 0 else TAIL
                    last = nc.tensor.matmul(ps_y[k % 2][:, 0:D], hs[a][0:rows, k % 2, c * P:(c + 1) * P],
                                            W_down[b][c][:, ds(unit * D, D)],
                                            start=i == 0, stop=i == len(plan) - 1)
                last.then_inc(y_done, 1)

            U = 8
            transpose_x(0, 0)
            for j, k in steps(pe, NJ, U):
                if k == 0:
                    units.clear()
                if until(j, 1, NJ):
                    transpose_x(j + 1, (k + 1) % U)
                up(j, k)
                if since(j, 1):
                    transpose_h(j - 1, (k - 1) % U)
                if since(j, 2):
                    down(j - 2, (k - 2) % U, -1 if k < 2 else 0)
            transpose_h(NJ - 1, U - 1)
            down(NJ - 2, U - 2)
            down(NJ - 1, U - 1)


def quarter(n, k):
    return n // 4 if isinstance(n, int) else (n - k) // 4


def shared_stage(nc, tag, S, X, ST, MV, RSTD, W12, slots_u, ident, WUh, WUl, WDh, WDl, y_dram, out_dram):
    D, FF, NT, NS, TAIL = S.D, S.FF, S.NT, S.NS, S.TAIL
    with ExitStack() as c3:
        def sb(name, shape, dt=F32):
            return c3.enter_context(nc.sbuf_tensor(f"{tag}3_{name}", shape, dt))

        def ps(name):
            return [c3.enter_context(nc.psum_tensor(f"{tag}3_{name}{i}", [P, 512], F32)) for i in range(2)]

        sem = semaphores(nc, c3, f"{tag}3")

        XN = sb("XN", [P, 2, D])
        xs = [sb("xh", [P, 2, D], F32R), sb("xl", [P, 2, D], F32R)]
        SG = sb("SG", [P, 2, FF])
        H = sb("H", [P, 2, 2 * P])
        hs = [sb("hh", [P, 2, 2 * P], F32R), sb("hl", [P, 2, 2 * P], F32R)]
        YG = sb("YG", [P, 4, TOP_K, D])
        ST2 = ST[:, :, :].rearrange("p t s -> p (t s)")
        ps_x, ps_u, ps_h, ps_y = ps("ps_x"), ps("ps_u"), ps("ps_h"), ps("ps_y")
        X2 = X[:, :, :].rearrange("p t d -> p (t d)")
        MV2 = MV[:, :, :].rearrange("p t s -> p (t s)")
        W2 = W12[:, :, :].rearrange("p k t -> p (k t)")

        zeroed = sem("zeroed")
        gathered = [sem(f"gathered{i}") for i in range(4)]
        xn_ready = sem("xn_ready")
        xT_done = sem("xT_done")
        xh_done = sem("xh_done")
        xl_done = sem("xl_done")
        up_done = sem("up_done")
        silu_done = sem("silu_done")
        h_ready = sem("h_ready")
        hT_done = sem("hT_done")
        hh_done = sem("hh_done")
        hl_done = sem("hl_done")
        y_done = sem("y_done")
        added = sem("added")
        mixed = sem("mixed")
        x_done = sem("x_done")
        stats = sem("stats")
        stored = sem("stored")

        block = c3.enter_context(nc.Block())

        @block.gpsimd
        def _(pool):
            for t in range(NT):
                if t >= 4:
                    pool.wait_ge(x_done, t - 3)
                for c in range(TOP_K):
                    nc.gpsimd.indirect_dma_start(
                        out=YG[:, t % 4, c, :], out_offset=None, in_=y_dram[:, :],
                        in_offset=bass.IndirectOffsetOnAxis(ap=slots_u[:, c, t:t + 1], axis=0)
                    ).then_inc(gathered[t % 4], 16)

        @block.sync
        def _(sp):
            if out_dram is not None:
                for t, k in steps(sp, NT, 4):
                    sp.wait_ge(x_done, t + 1)
                    sp.dma_start(out_dram[ds(t * P, P), :], X2[:, ds(t * D, D)]).then_inc(stored, 16)
                sp.wait_ge(stored, 16 * NT)

        @block.scalar
        def _(act):
            def x_high(t, k):
                act.wait_ge(xT_done, t + 1)
                if since(t, 2):
                    act.wait_ge(up_done, 2 * t - 2)
                nc.scalar.activation(xs[0][:, k % 2, :], ps_x[k % 2][:, 0:D], ACT.Copy).then_inc(xh_done, 1)

            def h_high(t, k, s):
                n = 2 * t + s
                act.wait_ge(hT_done, n + 1)
                if since(t, 1):
                    act.wait_ge(y_done, t)
                nc.scalar.activation(hs[0][:, s, :], ps_h[s][:, 0:2 * P], ACT.Copy).then_inc(hh_done, 1)

            x_high(0, 0)
            for t, k in steps(act, NT, 4):
                for s in range(NS):
                    act.wait_ge(up_done, 2 * t + s + 1)
                    if since(t, 1):
                        act.wait_ge(h_ready, 2 * t + s - 1)
                    nc.scalar.activation(SG[:, s, :], ps_u[s][:, 0:FF], ACT.Silu).then_inc(silu_done, 1)
                    if s == 0 and until(t, 1, NT):
                        x_high(t + 1, (k + 1) % 4)
                for s in range(NS):
                    h_high(t, k, s)

        @block.vector
        def _(dve):
            nc.vector.memset(H[:, :, FF:2 * P], 0.0).then_inc(zeroed, 1)

            def normalise(t, k):
                if since(t, 2):
                    dve.wait_ge(xT_done, t - 1)
                nc.vector.tensor_scalar(XN[:, k % 2, :], X2[:, ds(t * D, D)], MV2[:, ds(2 * t, 1)],
                                        RSTD[:, ds(t, 1)], ALU.subtract, ALU.mult).then_inc(xn_ready, 1)

            def x_low(t, k):
                dve.wait_ge(xh_done, t + 1)
                nc.vector.tensor_tensor(xs[1][:, k % 2, :], ps_x[k % 2][:, 0:D],
                                        xs[0][:, k % 2, :].bitcast(F32), ALU.subtract).then_inc(xl_done, 1)

            def h_low(t, s):
                dve.wait_ge(hh_done, 2 * t + s + 1)
                nc.vector.tensor_tensor(hs[1][:, s, :], ps_h[s][:, 0:2 * P],
                                        hs[0][:, s, :].bitcast(F32), ALU.subtract).then_inc(hl_done, 1)

            def add_expert(t, k, c):
                x_t = X2[:, ds(t * D, D)]
                if c == 0:
                    dve.wait_ge(gathered[k], 32 * (quarter(t, k) + 1))
                else:
                    dve.wait_ge(mixed, 2 * t + 1)
                nc.vector.scalar_tensor_tensor(x_t, YG[:, k, c, :], W2[:, ds(t + c * NT, 1)], x_t,
                                               ALU.mult, ALU.add).then_inc(mixed, 1)

            def add_shared(t, k):
                x_t = X2[:, ds(t * D, D)]
                dve.wait_ge(mixed, 2 * t + 2)
                dve.wait_ge(y_done, t + 1)
                nc.vector.scalar_tensor_tensor(x_t, ps_y[k % 2][:, 0:D], HALF, x_t,
                                               ALU.mult, ALU.add).then_inc(x_done, 1)

            def statistics(t):
                if out_dram is None:
                    dve.wait_ge(x_done, t + 1)
                    nc.vector.bn_stats(ST2[:, ds(6 * t, 6)], X2[:, ds(t * D, D)]).then_inc(stats, 1)

            def gated(t, s):
                dve.wait_ge(silu_done, 2 * t + s + 1)
                if since(t, 1):
                    dve.wait_ge(hT_done, 2 * t + s - 1)
                nc.vector.tensor_tensor(H[:, s, 0:FF], SG[:, s, :], ps_u[s][:, FF:2 * FF],
                                        ALU.mult).then_inc(h_ready, 1)

            normalise(0, 0)
            x_low(0, 0)
            for t, k in steps(dve, NT, 4):
                before = since(t, 1), t - 1, (k - 1) % 4
                if until(t, 1, NT):
                    normalise(t + 1, (k + 1) % 4)
                gated(t, 0)
                if before[0]:
                    add_expert(*before[1:], 0)
                if until(t, 1, NT):
                    x_low(t + 1, (k + 1) % 4)
                gated(t, 1)
                if before[0]:
                    add_expert(*before[1:], 1)
                h_low(t, 0)
                if before[0]:
                    add_shared(*before[1:])
                h_low(t, 1)
                if before[0]:
                    statistics(t - 1)
            add_expert(NT - 1, 3, 0)
            add_expert(NT - 1, 3, 1)
            add_shared(NT - 1, 3)
            statistics(NT - 1)

        @block.tensor
        def _(pe):
            W_up, W_down = (WUh, WUl), (WDh, WDl)

            def transpose_x(t, k):
                pe.wait_ge(xn_ready, t + 1)
                if since(t, 2):
                    pe.wait_ge(xl_done, t - 1)
                for c in range(2):
                    last = nc.tensor.transpose(ps_x[k % 2][:, c * P:(c + 1) * P],
                                               XN[:, k % 2, c * P:(c + 1) * P], ident[:, :])
                last.then_inc(xT_done, 1)

            def up(t, k, s):
                pe.wait_ge(xl_done, t + 1)
                if since(t, 1):
                    pe.wait_ge(h_ready, 2 * t + s - 1)
                plan = split_passes(2)
                for i, (c, a, b) in enumerate(plan):
                    last = nc.tensor.matmul(ps_u[s][:, 0:2 * FF], xs[a][:, k % 2, c * P:(c + 1) * P],
                                            W_up[b][:, c, s * 2 * FF:(s + 1) * 2 * FF],
                                            start=i == 0, stop=i == len(plan) - 1)
                last.then_inc(up_done, 1)

            def transpose_h(t, s):
                pe.wait_ge(h_ready, 2 * t + s + 1)
                if since(t, 1):
                    pe.wait_ge(hl_done, 2 * t + s - 1)
                for c in range(2):
                    last = nc.tensor.transpose(ps_h[s][:, c * P:(c + 1) * P], H[:, s, c * P:(c + 1) * P],
                                               ident[:, :])
                last.then_inc(hT_done, 1)

            def down(t, k):
                if since(t, 2):
                    pe.wait_ge(x_done, t - 1)
                plan = [(s, *one) for s in range(NS) for one in split_passes(2)]
                for i, (s, c, a, b) in enumerate(plan):
                    if i % 6 == 0:
                        pe.wait_ge(hl_done, 2 * t + s + 1)
                    rows = P if c == 0 else TAIL
                    last = nc.tensor.matmul(ps_y[k % 2][:, 0:D], hs[a][0:rows, s, c * P:(c + 1) * P],
                                            W_down[b][c][:, s * D:(s + 1) * D],
                                            start=i == 0, stop=i == len(plan) - 1)
                last.then_inc(y_done, 1)

            transpose_x(0, 0)
            pe.wait_ge(zeroed, 1)
            for t, k in steps(pe, NT, 4):
                up(t, k, 0)
                if until(t, 1, NT):
                    transpose_x(t + 1, (k + 1) % 4)
                up(t, k, 1)
                if since(t, 1):
                    down(t - 1, (k - 1) % 4)
                transpose_h(t, 0)
                transpose_h(t, 1)
            down(NT - 1, 3)


def attention(nc, S, X, ST, MV, ident, w_qkv, b_qk, b_v, w_out, b_out, out_dram, first):
    with ExitStack() as ctx:
        V = ctx.enter_context(nc.sbuf_tensor("V", [P, S.NT, S.HEADS, S.HD + 1], F32))
        qk_dram = nc.dram_tensor("qk_scratch", (S.B, S.G, 2, P, S.L), F32, kind="Internal").ap()
        x_dram = nc.dram_tensor("x_scratch", (S.T, S.D), F32, kind="Internal").ap()
        project_stage(nc, S, X, ST, MV, ident, w_qkv, b_qk, b_v, V, qk_dram, x_dram, first)
        softmax_stage(nc, S, ident, V, X, qk_dram)
        output_stage(nc, S, X, ST, MV, ident, w_out, b_out, x_dram, out_dram)


def project_stage(nc, S, X, ST, MV, ident, w_qkv, b_qk, b_v, V, qk_dram, x_dram, first):
    D, NT, HD, HEADS, G, L = S.D, S.NT, S.HD, S.HEADS, S.G, S.L
    GF = D // G
    W = 4 * P
    assert G == 4
    NW = S.T // W
    with ExitStack() as c:
        def sb(name, shape, dt=F32):
            return c.enter_context(nc.sbuf_tensor(f"p_{name}", shape, dt))

        def ps(name, n=2):
            return [c.enter_context(nc.psum_tensor(f"p_{name}{i}", [P, 512], F32)) for i in range(n)]

        sem = semaphores(nc, c, "p")

        WR = sb("WR", [P, 2, 3 * D])
        Wh = sb("Wh", [P, 2, 3 * D], F32R)
        Wl = sb("Wl", [P, 2, 3 * D], F32R)
        BQK = sb("BQK", [P, G])
        BV = sb("BV", [P, D])
        RSTD = sb("RSTD", [P, NT])
        XN = sb("XN", [P, 4, D])
        xs = [sb("xh", [P, 2, 2, W], F32R), sb("xl", [P, 2, 2, W], F32R)]
        QKh = sb("QKh", [P, G, W], F32R)
        QKl = sb("QKl", [P, G, W], F32R)
        ps_x, ps_qk, ps_v = ps("ps_x"), ps("ps_qk"), ps("ps_v")
        X2 = X[:, :, :].rearrange("p t d -> p (t d)")
        MV2 = MV[:, :, :].rearrange("p t s -> p (t s)")
        V2 = V[:, :, :, :].rearrange("p t h e -> p (t h e)")

        weights_in = sem("weights_in")
        weights = sem("weights")
        weights_hi = sem("weights_hi")
        ones = sem("ones")
        chain = sem("chain")
        rstd_in = sem("rstd_in")
        rstd_out = sem("rstd_out")
        xn_ready = sem("xn_ready")
        xT_done = sem("xT_done")
        xh_done = sem("xh_done")
        xl_done = sem("xl_done")
        qk_done = sem("qk_done")
        qkh_done = sem("qkh_done")
        qkl_done = sem("qkl_done")
        x_out = sem("x_out")
        qk_out = [sem(f"qk_out{i}") for i in range(G)]
        v_done = sem("v_done")
        v_copied = sem("v_copied")

        block = c.enter_context(nc.Block())

        @block.sync
        def _(sp):
            sp.dma_start(WR[:, :, :], w_qkv.rearrange("(c p) f -> p c f", p=P)).then_inc(weights_in, 16)
            sp.dma_start(BQK[:, :], b_qk).then_inc(weights_in, 16)
            sp.dma_start(BV[:, :], b_v.rearrange("(a f) -> a f", a=1)
                         .to_broadcast([P, D])).then_inc(weights_in, 16)
            sp.dma_start(x_dram.rearrange("(t p) d -> p t d", p=P), X[:, :, :]).then_inc(x_out, 16)
            for n in range(NW * G):
                w, g = n // G, n % G
                cols = slice(w % 2 * W, (w % 2 + 1) * W)
                sp.wait_ge(qkh_done, n + 1)
                sp.dma_start(qk_dram[w // 2, g, 0, :, cols], QKh[:, g, :].bitcast(F32)).then_inc(qk_out[g], 16)
                sp.wait_ge(qkl_done, n + 1)
                sp.dma_start(qk_dram[w // 2, g, 1, :, cols], QKl[:, g, :].bitcast(F32)).then_inc(qk_out[g], 16)
            for i in range(G):
                sp.wait_ge(qk_out[i], 32 * NW)
            sp.wait_ge(x_out, 16)

        @block.gpsimd
        def _(pool):
            nc.gpsimd.memset(V[:, :, :, HD:HD + 1], 1.0).then_inc(ones, 1)
            pool.wait_ge(weights_in, 48)
            nc.gpsimd.tensor_copy(Wh[:, :, :], WR[:, :, :]).then_inc(weights_hi, 1)
            pool.wait_ge(weights_hi, 1)
            nc.gpsimd.tensor_tensor(Wl[:, :, :], WR[:, :, :], Wh[:, :, :].bitcast(F32),
                                    ALU.subtract).then_inc(weights, 1)

        @block.scalar
        def _(act):
            act.wait_ge(rstd_in, 1)
            nc.scalar.activation(RSTD[:, :], RSTD[:, :], ACT.Sqrt).then_inc(rstd_out, 1)
            act.wait_ge(weights_in, 48)

            def x_high(w, k, i):
                act.wait_ge(xT_done, 4 * w + i + 1)
                if i == 0 and since(w, 2):
                    act.wait_ge(v_done, 4 * w - 4)
                nc.scalar.activation(xs[0][:, k, :, i * P:(i + 1) * P],
                                     ps_x[i % 2][:, 0:D].rearrange("p (c n) -> p c n", c=2),
                                     ACT.Copy).then_inc(xh_done, 1)

            for i in range(4):
                x_high(0, 0, i)
            for w, k in steps(act, NW, 2):
                for g in range(G):
                    act.wait_ge(qk_done, G * w + g + 1)
                    if since(w, 1):
                        act.wait_ge(qk_out[g], 32 * w)
                    nc.scalar.activation(QKh[:, g, :], ps_qk[g % 2][:, :], ACT.Identity,
                                         bias=BQK[:, g:g + 1]).then_inc(qkh_done, 1)
                    if until(w, 1, NW):
                        x_high(w + 1, 1 - k, g)

        @block.vector
        def _(dve):
            count = [0]

            def link(ins):
                count[0] += 1
                ins.then_inc(chain, 1)
                dve.wait_ge(chain, count[0])

            if first:
                for t in range(NT):
                    last = nc.vector.bn_stats(ST[:, t, :], X[:, t, :])
                link(last)
            for t in range(NT):
                last = nc.vector.bn_aggr(MV[:, t, :], ST[:, t, :])
            link(last)
            nc.vector.tensor_scalar(RSTD[:, :], MV[:, :, 1], EPS, None, ALU.add).then_inc(rstd_in, 1)
            dve.wait_ge(rstd_out, 1)
            link(nc.vector.reciprocal(RSTD[:, :], RSTD[:, :]))
            dve.wait_ge(weights_in, 48)
            dve.wait_ge(ones, 1)

            def normalise(w, i):
                if since(w, 1):
                    dve.wait_ge(xT_done, 4 * w + i - 3)
                t = 4 * w + i
                nc.vector.tensor_scalar(XN[:, i, :], X2[:, ds(t * D, D)], MV2[:, ds(2 * t, 1)],
                                        RSTD[:, ds(t, 1)], ALU.subtract, ALU.mult).then_inc(xn_ready, 1)

            def x_low(w, k, i):
                dve.wait_ge(xh_done, 4 * w + i + 1)
                nc.vector.tensor_tensor(xs[1][:, k, :, i * P:(i + 1) * P],
                                        ps_x[i % 2][:, 0:D].rearrange("p (c n) -> p c n", c=2),
                                        xs[0][:, k, :, i * P:(i + 1) * P].bitcast(F32),
                                        ALU.subtract).then_inc(xl_done, 1)

            for i in range(4):
                normalise(0, i)
            for i in range(4):
                x_low(0, 0, i)
            for w, k in steps(dve, NW, 2):
                for g in range(G):
                    if until(w, 1, NW):
                        normalise(w + 1, g)
                    dve.wait_ge(qkh_done, G * w + g + 1)
                    nc.vector.scalar_tensor_tensor(QKl[:, g, :], ps_qk[g % 2][:, :], BQK[:, g:g + 1],
                                                   QKh[:, g, :].bitcast(F32), ALU.add,
                                                   ALU.subtract).then_inc(qkl_done, 1)
                    t = 4 * w + g
                    dve.wait_ge(v_done, t + 1)
                    nc.vector.tensor_tensor(
                        V2[:, ds(t * (HEADS * (HD + 1)), HEADS * (HD + 1))]
                        .rearrange("p (h e) -> p h e", h=HEADS)[:, :, 0:HD],
                        ps_v[g % 2][:, 0:D].rearrange("p (h e) -> p h e", h=HEADS),
                        BV[:, :].rearrange("p (h e) -> p h e", h=HEADS), ALU.add).then_inc(v_copied, 1)
                    if until(w, 1, NW):
                        x_low(w + 1, 1 - k, g)

        @block.tensor
        def _(pe):
            Ws = (Wh, Wl)

            def transpose_x(w, i):
                pe.wait_ge(xn_ready, 4 * w + i + 1)
                if i >= 2 or since(w, 1):
                    pe.wait_ge(xl_done, 4 * w + i - 1)
                for c in range(2):
                    last = nc.tensor.transpose(ps_x[i % 2][:, c * P:(c + 1) * P],
                                               XN[:, i, c * P:(c + 1) * P], ident[:, :])
                last.then_inc(xT_done, 1)

            for i in range(4):
                transpose_x(0, i)
            pe.wait_ge(weights, 1)
            for w, k in steps(pe, NW, 2):
                pe.wait_ge(xl_done, 4 * w + 4)
                for g in range(G):
                    if g >= 2 or since(w, 1):
                        pe.wait_ge(qkl_done, G * w + g - 1)
                    for i, (c, a, b) in enumerate(split_passes(2)):
                        wt = Ws[a][:, c, 2 * g * GF:2 * (g + 1) * GF]
                        last = nc.tensor.matmul(ps_qk[g % 2][:, :], wt, xs[b][:, k, c, :], start=i == 0, stop=i == 5)
                    last.then_inc(qk_done, 1)
                    if g >= 2 or since(w, 1):
                        pe.wait_ge(v_copied, 4 * w + g - 1)
                    for i, (c, a, b) in enumerate(split_passes(2)):
                        last = nc.tensor.matmul(ps_v[g % 2][:, 0:D], xs[a][:, k, c, g * P:(g + 1) * P],
                                                Ws[b][:, c, 2 * D:3 * D], start=i == 0, stop=i == 5)
                    last.then_inc(v_done, 1)
                    if until(w, 1, NW):
                        transpose_x(w + 1, g)


def softmax_stage(nc, S, ident, V, ATT, qk_dram):
    D, NT, HD, HEADS, G, L = S.D, S.NT, S.HD, S.HEADS, S.G, S.L
    NG = S.B * G
    NQ = L // P
    W = 512
    GH = HEADS // G
    GF = D // G
    V1 = HD + 1
    PH = 2 * HD
    R = 3 * PH
    RM = R + 2
    SCALE = float(HD) ** -0.5
    NEG = -1e30
    B_STEPS = [(hf, i) for hf in range(2) for i in range(4 * hf + 4)]
    NB = len(B_STEPS)
    DIAGONAL = [n for n, (hf, i) in enumerate(B_STEPS) if i >= 4 * hf]
    A_UNITS = []
    for i in range(NQ):
        for s in range(1 + i // 4):
            keys = min((i + 1) * P - s * W, W)
            wide = W // keys
            starts = range(0, GH, wide)
            A_UNITS += [(i, s, h, min(wide, GH - h), keys) for h in starts]
    RING = 3
    while len(A_UNITS) % RING:
        at = max(n for n, unit in enumerate(A_UNITS) if unit[3] > 1)
        i, s, h, heads, keys = A_UNITS[at]
        A_UNITS[at:at + 1] = [(i, s, h, 1, keys), (i, s, h + 1, heads - 1, keys)]
    NA = len(A_UNITS)
    a_cost = [heads * keys + 64 for _, _, _, heads, keys in A_UNITS]
    AHEAD = next(v for v in range(NA) if sum(a_cost[:v]) * 3 >= sum(a_cost))
    beside = [(1, v) for v in range(AHEAD, NA)] + [(2, v) for v in range(AHEAD)]
    b_cost = [GH * (min(W, (hf + 1) * W - i * P)) for hf, i in B_STEPS]
    A_BESIDE = [[] for _ in B_STEPS]
    gone = 0
    for one in beside:
        step = next(n for n in range(NB) if gone * sum(b_cost) < sum(b_cost[:n + 1]) * sum(a_cost))
        A_BESIDE[step].append(one)
        gone += a_cost[one[1]]
    MAX_T = 1 + max(n for n in range(NB) if (1, NA - 1) in A_BESIDE[n])
    SLOTS = 6
    LOAD = 9 * 16
    PLACE = 2 * 16
    assert GH == 4 and D // G == 64 and GH * NB % RING == 0 and NB * 2 % SLOTS == 0 and MAX_T < NB
    with ExitStack() as c:
        def sb(name, shape, dt=F32):
            return c.enter_context(nc.sbuf_tensor(f"s_{name}", shape, dt))

        def ps(name, shape):
            return c.enter_context(nc.psum_tensor(f"s_{name}", shape, F32))

        sem = semaphores(nc, c, "s")

        def ring(name, n):
            return [sem(f"{name}{i}") for i in range(n)]

        QO = [sb(f"QO{i}", [P, GH, L], F32R) for i in range(4)]
        KO = [sb(f"KO{i}", [P, 2, L], F32R) for i in range(4)]
        VG = [sb(f"VG{i}", [P, NQ, GH * V1]) for i in range(4)]
        PR = sb("PR", [P, SLOTS, 2, W])
        MX = sb("MX", [P, GH, NQ, 2])
        NM = sb("NM", [P, GH * NQ])
        NMh = sb("NMh", [GH * NQ, P], F32R)
        NMl = sb("NMl", [GH * NQ, P], F32R)
        OS = sb("OS", [P, W])
        RC = sb("RC", [P, 4, GH])
        identb = sb("identb", [P, P], BF16)
        zero_b = sb("zero_b", [P, P], BF16)
        neg = sb("neg", [P, P], BF16)
        ps_a = [ps(f"ps_a{i}", [P, W]) for i in range(RING)]
        ps_b = [ps(f"ps_b{i}", [P, W]) for i in range(RING)]
        ps_o = ps("ps_o", [P, W])
        ps_t = ps("ps_t", [P, W])
        ATT2 = ATT[:, :, :].rearrange("p t d -> p (t d)")
        V2 = V[:, :, :, :].rearrange("p t h e -> p t (h e)")

        consts = sem("consts")
        presets = sem("presets")
        values = sem("values")
        operands = ring("operands", 4)
        a_done = sem("a_done")
        a_read = sem("a_read")
        max_ready = sem("max_ready")
        maxT_done = sem("maxT_done")
        maxh_done = sem("maxh_done")
        maxl_done = sem("maxl_done")
        max_rows = ring("max_rows", 4)
        b_done = sem("b_done")
        exp_done = sem("exp_done")
        masked = sem("masked")
        pv_done = sem("pv_done")
        o_copied = sem("o_copied")
        oT_done = sem("oT_done")
        recip = sem("recip")
        att_done = sem("att_done")

        block = c.enter_context(nc.Block())

        def turn(g, k, back):
            return g - back, (k - back) % 4

        @block.sync
        def _(sp):
            def load(g):
                k = g % 4
                if g >= 4:
                    sp.wait_ge(pv_done, NB * (g - 3))
                for part, (q, kk) in enumerate(((0, 0), (0, 1), (1, 0))):
                    at = part * PH
                    keys = qk_dram[g // G, g % G, kk, GF:2 * GF, :].rearrange("(r c) l -> r c l", c=2)
                    sp.dma_start(KO[k][at:at + PH, :, :].bitcast(F32), keys).then_inc(operands[k], 16)
                    for hp in range(2):
                        rows = slice(at + hp * HD, at + (hp + 1) * HD)
                        queries = qk_dram[g // G, g % G, q, hp * PH:(hp + 1) * PH, :]\
                            .rearrange("(r c) l -> r c l", c=2)
                        sp.dma_start(QO[k][rows, 2 * hp:2 * hp + 2, :].bitcast(F32), queries)\
                            .then_inc(operands[k], 16)

            def place_max(g):
                k = g % 4
                sp.wait_ge(maxh_done, g + 1)
                sp.wait_ge(maxl_done, g + 1)
                for r, src in enumerate((NMh, NMl)):
                    sp.dma_start(QO[k][R + r:R + r + 1, :, :].bitcast(F32), src[:, :].bitcast(F32))\
                        .then_inc(max_rows[k], 16)

            sp.wait_ge(presets, 2)
            for g in range(4):
                load(g)
            place_max(0)
            for g in range(NG):
                if g + 1 < NG:
                    place_max(g + 1)
                if g + 4 < NG:
                    load(g + 4)

        @block.gpsimd
        def _(pool):
            nc.gpsimd.memset(zero_b[:, :], 0.0).then_inc(consts, 1)
            pool.wait_ge(consts, 1)
            nc.gpsimd.affine_select(out=neg[:, :], in_=zero_b[:, :], compare_op=ALU.is_ge, fill=NEG, base=0,
                                    pattern=[[-1, P]], channel_multiplier=1).then_inc(consts, 1)
            nc.gpsimd.tensor_copy(identb[:, :], ident[:, :]).then_inc(consts, 1)

            for k in range(2, 4):
                last = nc.gpsimd.memset(QO[k][:, :, :].bitcast(F32), 0.0)
            last.then_inc(presets, 1)

            def prepare(g):
                if g >= 4:
                    pool.wait_ge(pv_done, NB * (g - 3))
                batch = V2[:, ds(g // G * NQ, NQ), g % G * GH * V1:(g % G + 1) * GH * V1]
                nc.gpsimd.tensor_copy(VG[g % 4][:, :, :], batch).then_inc(values, 1)

            for g in range(3):
                prepare(g)
            for g in range(NG):
                k = g % 4
                for n in range(NB):
                    if n in DIAGONAL:
                        for pair in range(2):
                            u = 2 * n + pair
                            pool.wait_ge(exp_done, GH * NB * g + 2 * u + 2)
                            tile = PR[:, u % SLOTS, :, 0:P]
                            nc.gpsimd.affine_select(out=tile, in_=tile, compare_op=ALU.is_ge, fill=0.0, base=0,
                                                    pattern=[[0, 2], [1, P]], channel_multiplier=-1)\
                                .then_inc(masked, 1)
                    if n == 3 and until(g, 3, NG):
                        prepare(g + 3)

        @block.scalar
        def _(act):
            def max_high(g, k):
                act.wait_ge(maxT_done, g + 1)
                if since(g, 1):
                    p, pk = turn(g, k, 1)
                    act.wait_ge(max_rows[pk], PLACE * (quarter(p, pk) + 1))
                nc.scalar.activation(NMh[:, :], ps_t[0:GH * NQ, 0:P], ACT.Copy).then_inc(maxh_done, 1)

            def copy_output(g, hf):
                act.wait_ge(pv_done, NB * g + (4 if hf == 0 else NB))
                if hf == 1 or since(g, 1):
                    act.wait_ge(oT_done, 2 * g + hf)
                nc.scalar.activation(OS[:, :], ps_o[:, :], ACT.Copy).then_inc(o_copied, 1)

            max_high(0, 0)
            for g, k in steps(act, NG, 4):
                for n, (hf, i) in enumerate(B_STEPS):
                    lo = max(0, i * P - hf * W)
                    for h in range(GH):
                        u = GH * n + h
                        act.wait_ge(b_done, GH * NB * g + u + 1)
                        if h == 0 and (n >= SLOTS // 2 or since(g, 1)):
                            act.wait_ge(pv_done, NB * g + n + 1 - SLOTS // 2)
                        nc.scalar.activation(PR[:, u // 2 % SLOTS, u % 2, 0:W - lo], ps_b[u % RING][:, lo:W], ACT.Exp,
                                             scale=SCALE).then_inc(exp_done, 1)
                    if n == 4:
                        copy_output(g, 0)
                    if n == MAX_T and until(g, 1, NG):
                        max_high(g + 1, (k + 1) % 4)
                copy_output(g, 1)

        @block.vector
        def _(dve):
            for k in range(4):
                nc.vector.memset(KO[k][R:P, :, :].bitcast(F32), 1.0)
            for k in range(2):
                nc.vector.memset(QO[k][:, :, :].bitcast(F32), 0.0)
            nc.vector.memset(ps_o[:, :], 0.0)
            nc.vector.memset(MX[:, :, :, :], -3e38).then_inc(presets, 1)
            dve.wait_ge(presets, 1)

            def a_units(g, units):
                for v in units:
                    i, s, h, heads, keys = A_UNITS[v]
                    if v == 0 and since(g, 1):
                        dve.wait_ge(max_ready, g)
                    dve.wait_ge(a_done, NA * g + v + 1)
                    nc.vector.tensor_reduce(MX[:, h:h + heads, i, s],
                                            ps_a[v % RING][:, 0:heads * keys].rearrange("p (h n) -> p h n", h=heads),
                                            AX.X, ALU.max).then_inc(a_read, 1)

            def combine(g):
                dve.wait_ge(a_read, NA * (g + 1))
                if since(g, 1):
                    dve.wait_ge(maxT_done, g)
                nc.vector.tensor_reduce(NM[:, :].rearrange("p (h i) -> p h i", h=GH), MX[:, :, :, :], AX.X,
                                        ALU.max, negate=True).then_inc(max_ready, 1)

            def max_low(g):
                dve.wait_ge(maxh_done, g + 1)
                nc.vector.tensor_tensor(NMl[:, :], ps_t[0:GH * NQ, 0:P], NMh[:, :].bitcast(F32),
                                        ALU.subtract).then_inc(maxl_done, 1)

            def normalise(g, k, hf):
                turned = ps_t[:, :].rearrange("p (j h r) -> p j h r", j=4, h=GH)
                dve.wait_ge(oT_done, 2 * g + hf + 1)
                if hf == 1 or since(g, 1):
                    dve.wait_ge(att_done, 2 * g + hf)
                nc.vector.reciprocal(RC[:, :, :], turned[:, :, :, HD]).then_inc(recip, 1)
                dve.wait_ge(recip, 2 * g + hf + 1)
                half_rows = ATT2[:, ds((quarter(g, k) * NQ + 4 * hf) * D, 4 * D)].rearrange("p (j d) -> p j d", j=4)
                nc.vector.tensor_tensor(
                    half_rows[:, :, k * GF:(k + 1) * GF].rearrange("p j (h e) -> p j h e", h=GH),
                    turned[:, :, :, 0:HD], RC[:, :, :].unsqueeze(3).to_broadcast([P, 4, GH, HD]),
                    ALU.mult).then_inc(att_done, 1)

            a_units(0, range(NA))
            combine(0)
            max_low(0)
            a_units(1, range(AHEAD))
            for g, k in steps(dve, NG, 4):
                for n in range(NB):
                    for groups, v in A_BESIDE[n]:
                        if until(g, groups, NG):
                            a_units(g + groups, [v])
                            if v == NA - 1:
                                combine(g + 1)
                    if n == 1 and since(g, 1):
                        normalise(*turn(g, k, 1), 1)
                    if n == MAX_T - 1:
                        normalise(g, k, 0)
                    if n == MAX_T and until(g, 1, NG):
                        max_low(g + 1)
            normalise(NG - 1, 3, 1)

        @block.tensor
        def _(pe):
            def a_units(g, k, units):
                for v in units:
                    i, s, h0, heads, keys = A_UNITS[v]
                    diagonal = s == i // 4
                    if v == 0:
                        pe.wait_ge(operands[k], LOAD * (quarter(g, k) + 1))
                    if v >= RING or since(g, 1):
                        pe.wait_ge(a_read, NA * g + v + 1 - RING)
                    for h in range(h0, h0 + heads):
                        at = (h - h0) * keys
                        last = nc.tensor.matmul(ps_a[v % RING][:, at:at + keys], QO[k][0:R, h, i * P:(i + 1) * P],
                                                KO[k][0:R, h % 2, s * W:s * W + keys], start=True,
                                                stop=not diagonal, skip_group_check=True)
                        if diagonal:
                            last = nc.tensor.matmul(ps_a[v % RING][:, at + keys - P:at + keys], identb[:, :],
                                                    neg[:, :], start=False, stop=True, skip_group_check=True)
                    last.then_inc(a_done, 1)

            def turn_max(g):
                pe.wait_ge(max_ready, g + 1)
                if since(g, 1):
                    pe.wait_ge(att_done, 2 * g - 1)
                nc.tensor.transpose(ps_t[0:GH * NQ, 0:P], NM[:, :], ident[:, :]).then_inc(maxT_done, 1)

            def b_unit(g, k, n, h):
                hf, i = B_STEPS[n]
                lo = max(0, i * P - hf * W)
                u = GH * n + h
                if u == 0:
                    pe.wait_ge(operands[k], LOAD * (quarter(g, k) + 1))
                    pe.wait_ge(max_rows[k], PLACE * (quarter(g, k) + 1))
                if u >= RING or since(g, 1):
                    pe.wait_ge(exp_done, GH * NB * g + u + 1 - RING)
                nc.tensor.matmul(ps_b[u % RING][:, lo:W], KO[k][0:RM, h % 2, i * P:(i + 1) * P],
                                 QO[k][0:RM, h, hf * W + lo:(hf + 1) * W], start=True, stop=True).then_inc(b_done, 1)

            def pv_step(g, k, n):
                hf, i = B_STEPS[n]
                lo = max(0, i * P - hf * W)
                if n == 0:
                    pe.wait_ge(values, g + 1)
                if i == 0 and (n > 0 or since(g, 1)):
                    pe.wait_ge(o_copied, 2 * g + hf)
                pe.wait_ge(exp_done, GH * NB * g + GH * (n + 1))
                if n in DIAGONAL:
                    pe.wait_ge(masked, 2 * len(DIAGONAL) * g + 2 * DIAGONAL.index(n) + 2)
                for h in range(GH):
                    last = nc.tensor.matmul(ps_o[32 * h:32 * h + V1, lo:W], VG[k][:, i, h * V1:(h + 1) * V1],
                                            PR[:, (2 * n + h // 2) % SLOTS, h % 2, 0:W - lo],
                                            start=i == 0, stop=i == 4 * hf + 3, skip_group_check=True)
                last.then_inc(pv_done, 1)

            def turn_output(g, hf):
                pe.wait_ge(o_copied, 2 * g + hf + 1)
                if hf == 1:
                    if until(g, 1, NG):
                        pe.wait_ge(maxl_done, g + 2)
                    else:
                        pe.wait_ge(att_done, 2 * g + 1)
                elif since(g, 1):
                    pe.wait_ge(att_done, 2 * g)
                else:
                    pe.wait_ge(maxl_done, 1)
                for j in range(4):
                    last = nc.tensor.transpose(ps_t[:, j * P:(j + 1) * P], OS[:, j * P:(j + 1) * P], ident[:, :])
                last.then_inc(oT_done, 1)

            pe.wait_ge(consts, 3)
            pe.wait_ge(presets, 1)
            a_units(0, 0, range(NA))
            turn_max(0)
            a_units(1, 1, range(AHEAD))
            for g, k in steps(pe, NG, 4):
                for n in range(NB):
                    turns = list(A_BESIDE[n])
                    for h in range(GH):
                        b_unit(g, k, n, h)
                        if h == GH - 1:
                            if n >= 1:
                                pv_step(g, k, n - 1)
                            if n == 1 and since(g, 1):
                                turn_output(g - 1, 1)
                            if n == MAX_T - 1:
                                turn_output(g, 0)
                            if n == MAX_T and until(g, 1, NG):
                                turn_max(g + 1)
                        for _ in range(-(-len(turns) // (GH - h))):
                            groups, v = turns.pop(0)
                            if until(g, groups, NG):
                                a_units(g + groups, (k + groups) % 4, [v])
                pv_step(g, k, NB - 1)
            turn_output(NG - 1, 1)


def output_stage(nc, S, X, ST, MV, ident, w_out, b_out, x_dram, out_dram):
    D, NT = S.D, S.NT
    with ExitStack() as c:
        def sb(name, shape, dt=F32):
            return c.enter_context(nc.sbuf_tensor(f"o_{name}", shape, dt))

        def ps(name):
            return [c.enter_context(nc.psum_tensor(f"o_{name}{i}", [P, 512], F32)) for i in range(2)]

        sem = semaphores(nc, c, "o")

        WR = sb("WR", [P, 2, D])
        Ws = [sb("Wh", [P, 2, D], F32R), sb("Wl", [P, 2, D], F32R)]
        BO = sb("BO", [P, D])
        AT = sb("AT", [P, 2, D])
        xs = [sb("ah", [P, 2, D], F32R), sb("al", [P, 2, D], F32R)]
        ST2 = ST[:, :, :].rearrange("p t s -> p (t s)")
        ps_x, ps_y = ps("ps_x"), ps("ps_y")
        X2 = X[:, :, :].rearrange("p t d -> p (t d)")
        XI = sb("XI", [P, 4, D])
        x_in = [sem(f"x_in{i}") for i in range(4)]

        weights_in = sem("weights_in")
        weights = sem("weights")
        row_ready = sem("row_ready")
        biased = sem("biased")
        xT_done = sem("xT_done")
        xh_done = sem("xh_done")
        xl_done = sem("xl_done")
        y_done = sem("y_done")
        x_done = sem("x_done")
        stats = sem("stats")
        stored = sem("stored")

        block = c.enter_context(nc.Block())

        @block.sync
        def _(sp):
            sp.dma_start(WR[:, :, :], w_out.rearrange("(c p) f -> p c f", p=P)).then_inc(weights_in, 16)
            sp.dma_start(BO[:, :], b_out.rearrange("(a f) -> a f", a=1).to_broadcast([P, D])).then_inc(weights_in, 16)
            for t in range(4):
                sp.dma_start(XI[:, t, :], x_dram[t * P:(t + 1) * P, :]).then_inc(x_in[t], 16)
            for t, k in steps(sp, NT, 4):
                sp.wait_ge(x_done, t + 1)
                if until(t, 4, NT):
                    sp.dma_start(XI[:, k, :], x_dram[ds(t * P + 4 * P, P), :]).then_inc(x_in[k], 16)
                if out_dram is not None:
                    sp.dma_start(out_dram[ds(t * P, P), :], X2[:, ds(t * D, D)]).then_inc(stored, 16)
            if out_dram is not None:
                sp.wait_ge(stored, 16 * NT)

        @block.gpsimd
        def _(pool):
            pool.wait_ge(weights_in, 32)
            for t, k in steps(pool, NT, 4):
                pool.wait_ge(x_in[k], 16 * (quarter(t, k) + 1))
                nc.gpsimd.tensor_tensor(XI[:, k, :], XI[:, k, :], BO[:, :], ALU.add).then_inc(biased, 1)

        @block.scalar
        def _(act):
            def fix_rows(t, k):
                if since(t, 2):
                    act.wait_ge(xT_done, t - 1)
                nc.scalar.activation(AT[:, k % 2, :], X2[:, ds(t * D, D)], ACT.Copy).then_inc(row_ready, 1)

            fix_rows(0, 0)
            fix_rows(1, 1)
            for t, k in steps(act, NT, 4):
                if until(t, 2, NT):
                    fix_rows(t + 2, (k + 2) % 4)
                act.wait_ge(xT_done, t + 1)
                if since(t, 2):
                    act.wait_ge(y_done, t - 1)
                nc.scalar.activation(xs[0][:, k % 2, :], ps_x[k % 2][:, 0:D], ACT.Copy).then_inc(xh_done, 1)

        @block.vector
        def _(dve):
            dve.wait_ge(weights_in, 32)
            nc.vector.tensor_copy(Ws[0][:, :, :], WR[:, :, :]).then_inc(weights, 1)
            dve.wait_ge(weights, 1)
            nc.vector.tensor_tensor(Ws[1][:, :, :], WR[:, :, :], Ws[0][:, :, :].bitcast(F32),
                                    ALU.subtract).then_inc(weights, 1)

            def x_low(t, k):
                dve.wait_ge(xh_done, t + 1)
                nc.vector.tensor_tensor(xs[1][:, k % 2, :], ps_x[k % 2][:, 0:D],
                                        xs[0][:, k % 2, :].bitcast(F32), ALU.subtract).then_inc(xl_done, 1)

            def statistics(t):
                nc.vector.bn_stats(ST2[:, ds(6 * t, 6)], X2[:, ds(t * D, D)]).then_inc(stats, 1)

            x_low(0, 0)
            for t, k in steps(dve, NT, 4):
                if until(t, 1, NT):
                    x_low(t + 1, (k + 1) % 4)
                x_t = X2[:, ds(t * D, D)]
                dve.wait_ge(y_done, t + 1)
                dve.wait_ge(biased, t + 1)
                if since(t, 1):
                    dve.wait_ge(x_done, t)
                nc.vector.tensor_tensor(x_t, ps_y[k % 2][:, 0:D], XI[:, k, :], ALU.add).then_inc(x_done, 1)
                if out_dram is None and since(t, 1):
                    statistics(t - 1)
            if out_dram is None:
                dve.wait_ge(x_done, NT)
                statistics(NT - 1)

        @block.tensor
        def _(pe):
            def transpose_x(t, k):
                pe.wait_ge(row_ready, t + 1)
                if since(t, 2):
                    pe.wait_ge(xl_done, t - 1)
                for c in range(2):
                    last = nc.tensor.transpose(ps_x[k % 2][:, c * P:(c + 1) * P], AT[:, k % 2, c * P:(c + 1) * P],
                                               ident[:, :])
                last.then_inc(xT_done, 1)

            transpose_x(0, 0)
            pe.wait_ge(weights, 2)
            for t, k in steps(pe, NT, 4):
                if until(t, 1, NT):
                    transpose_x(t + 1, (k + 1) % 4)
                pe.wait_ge(xl_done, t + 1)
                if since(t, 2):
                    pe.wait_ge(x_done, t - 1)
                for i, (c, a, b) in enumerate(split_passes(2)):
                    last = nc.tensor.matmul(ps_y[k % 2][:, 0:D], xs[a][:, k % 2, c * P:(c + 1) * P],
                                            Ws[b][:, c, :], start=i == 0, stop=i == 5)
                last.then_inc(y_done, 1)


def macaron(nc, PARTS, x, w_up, w_down, gate, w_qkv, b_qk, b_v, w_out, b_out, out):
    S = Shapes(x, w_up, w_down, gate)
    x_rows = x.rearrange("b l d -> (b l) d")
    out_rows = out.rearrange("b l d -> (b l) d")
    with ExitStack() as ctx:
        xn_dram = nc.dram_tensor("xn_scratch", (S.T, S.D), F32, kind="Internal").ap()
        y_dram = nc.dram_tensor("y_scratch", (S.NJ * P, S.D), F32, kind="Internal").ap()
        X = ctx.enter_context(nc.sbuf_tensor("X", [P, S.NT, S.D], F32))
        ST = ctx.enter_context(nc.sbuf_tensor("ST", [P, S.NT, 6], F32))
        MV = ctx.enter_context(nc.sbuf_tensor("MV", [P, S.NT, 2], F32))
        ident = ctx.enter_context(nc.sbuf_tensor("ident", [P, P], F32))
        x_in = nc.alloc_semaphore("x_in")
        ident_done = nc.alloc_semaphore("ident_done")
        with nc.Block() as block:
            @block.sync
            def _(sp):
                sp.dma_start(X[:, :, :], x_rows.rearrange("(t p) d -> p t d", p=P)).then_inc(x_in, 16)
                sp.wait_ge(x_in, 16)

            @block.gpsimd
            def _(pool):
                nc.gpsimd.memset(ident[:, :], 0.0).then_inc(ident_done, 1)
                pool.wait_ge(ident_done, 1)
                nc.gpsimd.affine_select(out=ident[:, :], in_=ident[:, :], compare_op=ALU.not_equal, fill=1.0,
                                        base=0, pattern=[[-1, P]], channel_multiplier=1).then_inc(ident_done, 1)
                pool.wait_ge(ident_done, 2)
        if "1" in PARTS:
            feed_forward(nc, "f1", S, X, ST, MV, ident, w_up, w_down, gate, xn_dram, y_dram,
                         out_rows if PARTS == "1" else None, True)
        if "a" in PARTS:
            attention(nc, S, X, ST, MV, ident, w_qkv, b_qk, b_v, w_out, b_out, out_rows if PARTS == "a" else None,
                      PARTS == "a")
        if "2" in PARTS:
            feed_forward(nc, "f2", S, X, ST, MV, ident, w_up, w_down, gate, xn_dram, y_dram, out_rows, False)


def kernel(**inputs):
    import numpy as np
    import concourse.bacc as _bacc
    from concourse.bass_utils import run_bass_kernel_spmd as _run

    a = {k[3:]: np.asarray(v) for k, v in inputs.items()}
    ff = a["ffn_exp_wg"].shape[1]
    d = a["attn_W_out"].shape[0]
    units = range(a["ffn_shared_wg"].shape[0] // ff)
    gates = [a["ffn_shared_wg"][s * ff:(s + 1) * ff] for s in units] + list(a["ffn_exp_wg"])
    ups = [a["ffn_shared_wu"][s * ff:(s + 1) * ff] for s in units] + list(a["ffn_exp_wu"])
    downs = [a["ffn_shared_wd"][:, s * ff:(s + 1) * ff] for s in units] + list(a["ffn_exp_wd"])
    laid = {
        "x": a["attn_x"],
        "w_up": np.stack([np.concatenate([g, u]).T for g, u in zip(gates, ups)], axis=1),
        "w_down": np.stack([d.T for d in downs]),
        "gate": a["ffn_gate_w"].T,
        "w_qkv": np.concatenate([a["attn_W_qkv"][:2 * d].reshape(2, 4, 2, 2, -1, d).transpose(1, 0, 2, 4, 3, 5)
                                 .reshape(2 * d, d), a["attn_W_qkv"][2 * d:]]).T,
        "b_qk": a["attn_b_qkv"][:2 * d].reshape(2, 4, 2, 2, -1).transpose(0, 2, 4, 3, 1).reshape(-1, 4),
        "b_v": a["attn_b_qkv"].reshape(3, -1)[2],
        "w_out": a["attn_W_out"].T,
        "b_out": a["attn_b_out"],
    }
    nc = _bacc.Bacc("TRN2", target_bir_lowering=False, num_devices=1)
    arrays, args = {}, []
    for name, v in laid.items():
        arrays[f"in_{name}"] = np.ascontiguousarray(v)
        args.append(nc.dram_tensor(f"in_{name}", v.shape, mybir.dt.from_np(v.dtype), kind="ExternalInput").ap())
    shape = a["attn_x"].shape
    args.append(nc.dram_tensor("out", shape, F32, kind="ExternalOutput").ap())
    macaron(nc, "1a2", *args)
    r = _run(nc, [arrays], core_ids=[0])
    return r.results[0]["out"]
```

```python
from contextlib import ExitStack

import concourse.bass as bass
from concourse import mybir

ALU = mybir.AluOpType
ACT = mybir.ActivationFunctionType
AX = mybir.AxisListType
F32 = mybir.dt.float32
F32R = mybir.dt.float32r
BF16 = mybir.dt.bfloat16
I32 = mybir.dt.int32
U32 = mybir.dt.uint32
ds = bass.ds

P = 128
TOP_K = 2
ROUTED_SCALE = 2.5
HALF = 0.5
EPS = 1e-5


def steps(eng, total, unroll):
    for n in range(unroll):
        yield n, n
    with eng.Fori(1, total // unroll - 1) as i:
        for k in range(unroll):
            yield i * unroll + k, k
    for n in range(total - unroll, total):
        yield n, n % unroll


def since(n, k):
    return not isinstance(n, int) or n >= k


def until(n, k, total):
    return not isinstance(n, int) or n + k < total


def half(n, k):
    return n // 2 if isinstance(n, int) else (n - k % 2) // 2


def semaphores(nc, stack, tag):
    made = []

    def clear():
        nc.clear_and_free_semaphores(made)
        nc.all_engine_barrier()

    def sem(name):
        made.append(nc.alloc_semaphore(f"{tag}_{name}"))
        return made[-1]

    stack.callback(clear)
    return sem


class Shapes:
    def __init__(self, x, w_up, w_down, gate):
        self.B, self.L, self.D = x.shape
        self.T = self.B * self.L
        self.NT = self.T // P
        self.NC = self.D // P
        self.NU = w_up.shape[1]
        self.E = gate.shape[1]
        self.NS = self.NU - self.E
        self.FF = w_up.shape[2] // 2
        self.NJ = self.T * TOP_K // P + self.E
        self.TAIL = self.FF - P
        self.HD = 16
        self.HEADS = self.D // self.HD
        self.G = self.HEADS // 4
        assert self.NS == 2 and self.NC == 2 and 0 < self.TAIL < P and self.NT % 4 == 0 and self.NJ % 4 == 0


def feed_forward(nc, tag, S, X, ST, MV, ident, w_up, w_down, w_shared, gate, xn_dram, y_dram, out_dram):
    D, NT, NU, NS, FF, E, NJ, TAIL = S.D, S.NT, S.NU, S.NS, S.FF, S.E, S.NJ, S.TAIL
    NG = NT * TOP_K
    with ExitStack() as ctx:
        def sb(name, shape, dt=F32):
            return ctx.enter_context(nc.sbuf_tensor(f"{tag}_{name}", shape, dt))

        WUh = sb("WUh", [P, 2, NU * 2 * FF], F32R)
        WUl = sb("WUl", [P, 2, NU * 2 * FF], F32R)
        WDh = [sb("WDh0", [P, E * D], F32R), sb("WDh1", [TAIL, E * D], F32R)]
        WDl = [sb("WDl0", [P, E * D], F32R), sb("WDl1", [TAIL, E * D], F32R)]
        WSh = sb("WSh", [P, 3, D], F32R)
        WSl = sb("WSl", [P, 3, D], F32R)
        RSTD = sb("RSTD", [P, NT])
        W12 = sb("W12", [P, TOP_K, NT])
        slots_u = sb("slots_u", [P, TOP_K, NT], U32)
        tok_u = sb("tok_u", [P, NJ], U32)
        unit_i = sb("unit_i", [P, NJ], I32)
        X2 = X[:, :, :].rearrange("p t d -> p (t d)")
        MV2 = MV[:, :, :].rearrange("p t s -> p (t s)")
        NW = NT // 4
        assert NW <= NU <= NW + 2

        with ExitStack() as c1:
            sem = semaphores(nc, c1, f"{tag}1")

            def sb1(name, shape, dt=F32):
                return c1.enter_context(nc.sbuf_tensor(f"{tag}1_{name}", shape, dt))

            def ps1(name, shape):
                return c1.enter_context(nc.psum_tensor(f"{tag}1_{name}", shape, F32))

            XN = sb1("XN", [P, 2, 4, D])
            xh = sb1("xh", [P, 2, 2, 4 * P], F32R)
            xl = sb1("xl", [P, 2, 2, 4 * P], F32R)
            GW = sb1("GW", [P, 2, E])
            GWhl = sb1("GWhl", [P, 2, 2 * E], F32R)
            GWh0 = sb1("GWh0", [P, 2, 2 * E], F32R)
            LT = sb1("LT", [2 * E, 2, 4 * P])
            ADD = sb1("ADD", [2 * E, E])
            stage = sb1("stage", [P, 2, 4 * FF])
            stageD = sb1("stageD", [P, 2, 2, D])
            ps_x = [ps1(f"ps_x{i}", [P, 512]) for i in range(4)]
            ps_gate = ps1("ps_gate", [P, NT * E])
            ps_lt = [ps1(f"ps_lt{i}", [2 * E, 512]) for i in range(2)]
            ps_count = ps1("ps_count", [P, 2, E * NT])
            ps_tok = ps_x[0][:, 0:2 * NJ]
            SC = sb1("SC", [P, NT, E])
            SC2 = sb1("SC2", [P, NT, E])
            EQ = sb1("EQ", [P, NT, E])
            PR = sb1("PR", [P, NT, E])
            OH = sb1("OH", [P, TOP_K, NT, E])
            SEL = sb1("SEL", [P, E, NT], BF16)
            M12 = sb1("M12", [P, TOP_K, NT])
            PMAX = sb1("PMAX", [P, NT])
            DEN = sb1("DEN", [P, NT])
            prio_i = sb1("prio_i", [P, E], I32)
            prio = sb1("prio", [P, E])
            lower_t = sb1("lower_t", [P, P], BF16)
            ones_b = sb1("ones_b", [P, P], BF16)
            ones_f = sb1("ones_f", [P, E * NT])
            CUM = sb1("CUM", [P, E, NT])
            EXC = sb1("EXC", [P, E, NT])
            SLOT = sb1("SLOT", [P, E, NT])
            CNT = sb1("CNT", [P, E])
            CNTi = sb1("CNTi", [P, E], I32)
            NTI = sb1("NTI", [P, E])
            CT = sb1("CT", [P, E])
            BASE = sb1("BASE", [P, E])
            SL = sb1("SL", [P, TOP_K, NT])
            SLi = sb1("SLi", [P, TOP_K, NT], I32)
            Ri = sb1("Ri", [P, NG], I32)
            Ti = sb1("Ti", [P, NG], I32)
            RF = sb1("RF", [P, NG])
            TF = sb1("TF", [P, NG])
            row_i = sb1("row_i", [P, P], I32)
            row_f = sb1("row_f", [P, P])
            row_b = sb1("row_b", [P, P], BF16)
            par_i = sb1("par_i", [P, 1], I32)
            par_f = sb1("par_f", [P, 1])
            GE = sb1("GE", [P, NJ, E])
            UF = sb1("UF", [P, NJ])
            tile_of = sb1("tile_of", [P, NG])
            CH = NG // 8
            RSEL = sb1("RSEL", [P, 2, CH, P], BF16)
            EQT = sb1("EQT", [P, 2, CH, NJ], BF16)
            TSEL = sb1("TSEL", [P, 2, CH, 2, NJ], BF16)
            tokf = sb1("tokf", [P, 2 * NJ])

            raw_in = [sem("raw_in0"), sem("raw_in1")]
            gate_in = sem("gate_in")
            consts = sem("consts")
            chain = sem("chain")
            weights_hi = sem("weights_hi")
            split_w = sem("split_w")
            rstd_in = sem("rstd_in")
            rstd_out = sem("rstd_out")
            xn_ready = sem("xn_ready")
            xn_out = [sem("xn_out0"), sem("xn_out1")]
            xT_done = sem("xT_done")
            xh_done = sem("xh_done")
            xl_done = sem("xl_done")
            gate_w = sem("gate_w")
            lt_done = sem("lt_done")
            lt_copied = sem("lt_copied")
            gate_done = sem("gate_done")
            sig_done = sem("sig_done")
            sel_done = sem("sel_done")
            pre_done = sem("pre_done")
            pre_copied = sem("pre_copied")
            slot_parts = sem("slot_parts")
            onehot = sem("onehot")
            rows = sem("rows")
            par_ids = sem("par_ids")
            tile_ids = sem("tile_ids")
            tok_done = sem("tok_done")

            PRE = sb1("PRE", [P, E * NT])
            TOT = sb1("TOT", [P, E * NT])

            def down_parts(u):
                if u == 0:
                    return [(0, P, 0), (2 * P, NS * FF - 2 * P, 1)]
                if u == 1:
                    return [(P, P, 0)]
                return [(0, P, 0), (P, TAIL, 1)]

            def raw_target(u, b):
                return 48 * (half(u, b) + 1) - 16 * b

            def hi_target(u):
                return 3 * (u + 1) - (u >= 1)

            block = c1.enter_context(nc.Block())

            @block.sync
            def _(sp):
                sp.dma_start(GW[:, :, :], gate.rearrange("(c p) e -> p c e", p=P)).then_inc(gate_in, 16)
                def load_unit(u):
                    b = u % 2
                    if u >= 2:
                        sp.wait_ge(split_w, u - 1)
                    sp.dma_start(stage[:, b, :].rearrange("p (c f) -> p c f", c=2),
                                 w_up[:, u, :].rearrange("(c p) f -> p c f", p=P)).then_inc(raw_in[b], 16)
                    for at, rows, dst in down_parts(u):
                        src = w_shared[at:at + rows, :] if u < NS else w_down[u - NS, at:at + rows, :]
                        sp.dma_start(stageD[0:rows, b, dst, :], src).then_inc(raw_in[b], 16)
                load_unit(0)
                load_unit(1)
                for u in range(2, NU):
                    load_unit(u)
                for k in range(2):
                    sp.wait_ge(xn_out[k], 16 * (NW // 2))

            @block.gpsimd
            def _(pool):
                nc.gpsimd.iota(prio_i[:, :], pattern=[[-1, E]], base=E, channel_multiplier=0).then_inc(consts, 1)
                nc.gpsimd.iota(row_i[:, :], pattern=[[1, P]], base=0, channel_multiplier=0).then_inc(consts, 1)
                nc.gpsimd.iota(par_i[:, :], pattern=[[0, 1]], base=0, channel_multiplier=1).then_inc(consts, 1)
                nc.gpsimd.memset(ones_b[:, :], 1.0).then_inc(consts, 1)
                nc.gpsimd.memset(ones_f[:, :], 1.0).then_inc(consts, 1)
                pool.wait_ge(consts, 5)
                nc.gpsimd.affine_select(out=lower_t[:, :], in_=ones_b[:, :], compare_op=ALU.is_gt, fill=0.0,
                                        base=0, pattern=[[1, P]], channel_multiplier=-1).then_inc(consts, 1)
                for u in range(NU):
                    b = u % 2
                    pool.wait_ge(raw_in[b], raw_target(u, b))
                    up = stage[:, b, :].rearrange("p (c f) -> p c f", c=2)
                    wu = slice(u * 2 * FF, (u + 1) * 2 * FF)
                    pool.wait_ge(weights_hi, hi_target(u))
                    nc.gpsimd.tensor_tensor(WUl[:, :, wu], up, WUh[:, :, wu].bitcast(F32), ALU.subtract)
                    for _, rows, slot in down_parts(u):
                        if u < NS:
                            chunk = 2 if slot == 1 else u
                            hi, lo = WSh[0:rows, chunk, :], WSl[0:rows, chunk, :]
                        else:
                            wd = slice((u - NS) * D, (u - NS + 1) * D)
                            hi, lo = WDh[slot][:, wd], WDl[slot][:, wd]
                        last = nc.gpsimd.tensor_tensor(lo, stageD[0:rows, b, slot, :], hi.bitcast(F32), ALU.subtract)
                    last.then_inc(split_w, 1)

                pool.wait_ge(slot_parts, 1)
                for n in range(8):
                    pool.wait_ge(onehot, n + 1)
                    if n >= 2:
                        pool.wait_ge(tok_done, n - 1)
                    shape = [P, CH, NJ]
                    nc.gpsimd.tensor_tensor(TSEL[:, n % 2, :, 1, :], EQT[:, n % 2, :, :],
                                            tile_of[:, n * CH:(n + 1) * CH].unsqueeze(2).to_broadcast(shape),
                                            ALU.mult).then_inc(tile_ids, 1)

            @block.scalar
            def _(act):
                act.wait_ge(rstd_in, 1)
                nc.scalar.activation(RSTD[:, :], RSTD[:, :], ACT.Sqrt).then_inc(rstd_out, 1)

                def x_high(w, k, i):
                    act.wait_ge(xT_done, 4 * w + i + 1)
                    if i == 0 and since(w, 2):
                        act.wait_ge(lt_done, w - 1)
                    nc.scalar.activation(xh[:, k, :, i * P:(i + 1) * P],
                                         ps_x[i][:, 0:D].rearrange("p (c n) -> p c n", c=2),
                                         ACT.Copy).then_inc(xh_done, 1)

                def weights_high(u, b):
                    act.wait_ge(raw_in[b], raw_target(u, b))
                    nc.scalar.activation(WUh[:, :, ds(u * (2 * FF), 2 * FF)],
                                         stage[:, b, :].rearrange("p (c f) -> p c f", c=2),
                                         ACT.Copy).then_inc(weights_hi, 1)
                    shared = isinstance(u, int) and u < NS
                    for _, rows, slot in down_parts(u if shared else NS):
                        if shared:
                            hi = WSh[0:rows, 2 if slot == 1 else u, :]
                        else:
                            hi = WDh[slot][:, ds((u - NS) * D, D)]
                        nc.scalar.activation(hi, stageD[0:rows, b, slot, :], ACT.Copy).then_inc(weights_hi, 1)

                for i in range(4):
                    x_high(0, 0, i)
                for w, k in steps(act, NW, 2):
                    act.wait_ge(xn_ready, 4 * w + 4)
                    act.dma_start(xn_dram[ds(w * 4 * P, 4 * P), :].rearrange("(i p) d -> p i d", p=P),
                                  XN[:, k, :, :]).then_inc(xn_out[k], 16)
                    if until(w, 1, NW):
                        for i in range(4):
                            x_high(w + 1, 1 - k, i)
                    act.wait_ge(lt_done, w + 1)
                    if since(w, 2):
                        act.wait_ge(gate_done, w - 1)
                    nc.scalar.activation(LT[:, k, :], ps_lt[k][:, :], ACT.Copy).then_inc(lt_copied, 1)
                    weights_high(w, k)
                act.wait_ge(gate_done, NW)
                nc.scalar.activation(SC[:, :, :].rearrange("p t e -> p (t e)"), ps_gate[:, :],
                                     ACT.Sigmoid).then_inc(sig_done, 1)
                weights_high(NW, NW % 2)
                act.wait_ge(pre_done, 1)
                nc.scalar.activation(PRE[:, :], ps_count[:, 0, :], ACT.Copy).then_inc(pre_copied, 1)
                nc.scalar.activation(TOT[:, :], ps_count[:, 1, :], ACT.Copy).then_inc(pre_copied, 1)
                for u in range(NW + 1, NU):
                    weights_high(u, u % 2)
                act.wait_ge(slot_parts, 1)
                for n in range(8):
                    act.wait_ge(onehot, n + 1)
                    if n >= 2:
                        act.wait_ge(tok_done, n - 1)
                    nc.scalar.activation(TSEL[:, n % 2, :, 0, :], EQT[:, n % 2, :, :], ACT.Copy,
                                         scale=par_f[:, :]).then_inc(par_ids, 1)

            @block.vector
            def _(dve):
                count = [0]

                def link(ins):
                    count[0] += 1
                    ins.then_inc(chain, 1)
                    dve.wait_ge(chain, count[0])

                dve.wait_ge(gate_in, 16)
                nc.vector.memset(GWh0[:, :, E:2 * E].bitcast(F32), 0.0)
                nc.vector.tensor_copy(GWh0[:, :, 0:E], GW[:, :, :])
                nc.vector.tensor_tensor(ADD[:, :], ident[0:2 * E, 0:E], ident[0:2 * E, E:2 * E], ALU.add)
                link(nc.vector.tensor_copy(GWhl[:, :, 0:E], GW[:, :, :]))
                nc.vector.tensor_tensor(GWhl[:, :, E:2 * E], GW[:, :, :], GWhl[:, :, 0:E].bitcast(F32),
                                        ALU.subtract).then_inc(gate_w, 1)
                for t in range(NT):
                    last = nc.vector.bn_aggr(MV[:, t, :], ST[:, t, :])
                link(last)
                nc.vector.tensor_scalar(RSTD[:, :], MV[:, :, 1], EPS, None, ALU.add).then_inc(rstd_in, 1)
                dve.wait_ge(rstd_out, 1)
                link(nc.vector.reciprocal(RSTD[:, :], RSTD[:, :]))

                def normalise(w, k, i):
                    if since(w, 2):
                        dve.wait_ge(xT_done, 4 * w + i - 7)
                        if i == 0:
                            dve.wait_ge(xn_out[k], 16 * half(w, k))
                    t = 4 * w + i
                    nc.vector.tensor_scalar(XN[:, k, i, :], X2[:, ds(t * D, D)], MV2[:, ds(2 * t, 1)],
                                            RSTD[:, ds(t, 1)], ALU.subtract, ALU.mult).then_inc(xn_ready, 1)

                def x_low(w, k, i):
                    dve.wait_ge(xh_done, 4 * w + i + 1)
                    nc.vector.tensor_tensor(xl[:, k, :, i * P:(i + 1) * P],
                                            ps_x[i][:, 0:D].rearrange("p (c n) -> p c n", c=2),
                                            xh[:, k, :, i * P:(i + 1) * P].bitcast(F32),
                                            ALU.subtract).then_inc(xl_done, 1)

                for i in range(4):
                    normalise(0, 0, i)
                for w, k in steps(dve, NW, 2):
                    for i in range(4):
                        if until(w, 1, NW):
                            normalise(w + 1, 1 - k, i)
                        x_low(w, k, i)

                dve.wait_ge(consts, 6)
                link(nc.vector.tensor_copy(prio[:, :], prio_i[:, :]))
                link(nc.vector.tensor_copy(row_f[:, :], row_i[:, :]))
                link(nc.vector.tensor_copy(row_b[:, :], row_i[:, :]))
                link(nc.vector.tensor_copy(par_f[:, :], par_i[:, :]))
                for k in range(TOP_K):
                    link(nc.vector.tensor_copy(tile_of[:, k * NT:(k + 1) * NT], row_i[:, 0:NT]))
                dve.wait_ge(sig_done, 1)
                src = SC
                wide = [P, NT, E]
                for k in range(TOP_K):
                    link(nc.vector.tensor_reduce(M12[:, k, :], src[:, :, :], AX.X, ALU.max))
                    link(nc.vector.tensor_tensor(EQ[:, :, :], src[:, :, :],
                                                 M12[:, k, :].unsqueeze(2).to_broadcast(wide), ALU.is_equal))
                    link(nc.vector.tensor_tensor(PR[:, :, :], EQ[:, :, :],
                                                 prio[:, :].unsqueeze(1).to_broadcast(wide), ALU.mult))
                    link(nc.vector.tensor_reduce(PMAX[:, :], PR[:, :, :], AX.X, ALU.max))
                    link(nc.vector.tensor_tensor(OH[:, k, :, :], PR[:, :, :],
                                                 PMAX[:, :].unsqueeze(2).to_broadcast(wide), ALU.is_equal))
                    if k == 0:
                        link(nc.vector.scalar_tensor_tensor(SC2[:, :, :], OH[:, 0, :, :], -4.0, SC[:, :, :],
                                                            ALU.mult, ALU.add))
                        src = SC2
                nc.vector.tensor_tensor(SEL[:, :, :].rearrange("p e t -> p t e"), OH[:, 0, :, :],
                                        OH[:, 1, :, :], ALU.add).then_inc(sel_done, 1)
                link(nc.vector.tensor_tensor(DEN[:, :], M12[:, 0, :], M12[:, 1, :], ALU.add))
                link(nc.vector.tensor_scalar(DEN[:, :], DEN[:, :], 1e-20, None, ALU.add))
                link(nc.vector.reciprocal(DEN[:, :], DEN[:, :]))
                for k in range(TOP_K):
                    link(nc.vector.scalar_tensor_tensor(W12[:, k, :], M12[:, k, :], ROUTED_SCALE * HALF, DEN[:, :],
                                                        ALU.mult, ALU.mult))

                dve.wait_ge(pre_copied, 2)
                CUMf = CUM[:, :, :].rearrange("p e t -> p (e t)")
                EXCf = EXC[:, :, :].rearrange("p e t -> p (e t)")
                SLOTf = SLOT[:, :, :].rearrange("p e t -> p (e t)")
                link(nc.vector.tensor_tensor_scan(CUMf, ones_f[:, :], TOT[:, :], 0.0, ALU.mult, ALU.add))
                link(nc.vector.tensor_tensor(EXCf, CUMf, TOT[:, :], ALU.subtract))
                link(nc.vector.tensor_tensor(CNT[:, :], CUM[:, :, NT - 1], EXC[:, :, 0], ALU.subtract))
                link(nc.vector.tensor_scalar(CNTi[:, :], CNT[:, :], float(P - 1), None, ALU.add))
                link(nc.vector.tensor_scalar(CNTi[:, :], CNTi[:, :], P.bit_length() - 1, None,
                                             ALU.arith_shift_right))
                link(nc.vector.tensor_copy(NTI[:, :], CNTi[:, :]))
                link(nc.vector.tensor_tensor_scan(CT[:, :], ones_f[:, 0:E], NTI[:, :], 0.0, ALU.mult, ALU.add))
                link(nc.vector.tensor_tensor(BASE[:, :], CT[:, :], NTI[:, :], ALU.subtract))
                link(nc.vector.scalar_tensor_tensor(BASE[:, :], BASE[:, :], float(P), EXC[:, :, 0],
                                                    ALU.mult, ALU.subtract))
                link(nc.vector.tensor_tensor(SLOTf, EXCf, PRE[:, :], ALU.add))
                link(nc.vector.tensor_tensor(SLOT[:, :, :], SLOT[:, :, :],
                                             BASE[:, :].unsqueeze(2).to_broadcast([P, E, NT]), ALU.add))
                for k in range(TOP_K):
                    link(nc.vector.tensor_tensor(EQ[:, :, :], OH[:, k, :, :],
                                                 SLOT[:, :, :].rearrange("p e t -> p t e"), ALU.mult))
                    link(nc.vector.tensor_reduce(SL[:, k, :], EQ[:, :, :], AX.X, ALU.add))
                link(nc.vector.tensor_copy(slots_u[:, :, :], SL[:, :, :]))
                link(nc.vector.tensor_copy(SLi[:, :, :], SL[:, :, :]))
                flat = SLi[:, :, :].rearrange("p k t -> p (k t)")
                link(nc.vector.tensor_scalar(Ri[:, :], flat, P - 1, None, ALU.bitwise_and))
                link(nc.vector.tensor_scalar(Ti[:, :], flat, P.bit_length() - 1, None, ALU.arith_shift_right))
                link(nc.vector.tensor_copy(RF[:, :], Ri[:, :]))
                nc.vector.tensor_copy(TF[:, :], Ti[:, :]).then_inc(slot_parts, 1)
                dve.wait_ge(slot_parts, 1)

                jw = [P, NJ, E]
                link(nc.vector.tensor_tensor(GE[:, :, :], row_f[:, 0:NJ].unsqueeze(2).to_broadcast(jw),
                                             CT[:, :].unsqueeze(1).to_broadcast(jw), ALU.is_ge))
                link(nc.vector.tensor_reduce(UF[:, :], GE[:, :, :], AX.X, ALU.add))
                link(nc.vector.tensor_scalar(unit_i[:, :], UF[:, :], float(E - 1), float(NS), ALU.min, ALU.add))

                for n in range(8):
                    if n >= 2:
                        dve.wait_ge(tok_done, n - 1)
                    part = slice(n * CH, (n + 1) * CH)
                    nc.vector.tensor_tensor(EQT[:, n % 2, :, :],
                                            row_f[:, 0:NJ].unsqueeze(1).to_broadcast([P, CH, NJ]),
                                            TF[:, part].unsqueeze(2).to_broadcast([P, CH, NJ]),
                                            ALU.is_equal).then_inc(onehot, 1)
                    nc.vector.tensor_tensor(RSEL[:, n % 2, :, :],
                                            row_f[:, :].unsqueeze(1).to_broadcast([P, CH, P]),
                                            RF[:, part].unsqueeze(2).to_broadcast([P, CH, P]),
                                            ALU.is_equal).then_inc(rows, 1)
                dve.wait_ge(tok_done, 8)
                link(nc.vector.tensor_copy(tokf[:, :], ps_tok))
                link(nc.vector.scalar_tensor_tensor(tok_u[:, :], tokf[:, NJ:2 * NJ], float(P), tokf[:, 0:NJ],
                                                    ALU.mult, ALU.add))

            @block.tensor
            def _(pe):
                def transpose_x(w, k, i):
                    pe.wait_ge(xn_ready, 4 * w + i + 1)
                    if since(w, 1):
                        pe.wait_ge(xl_done, 4 * w + i - 3)
                    for c in range(2):
                        last = nc.tensor.transpose(ps_x[i][:, c * P:(c + 1) * P], XN[:, k, i, c * P:(c + 1) * P],
                                                   ident[:, :])
                    last.then_inc(xT_done, 1)

                def logits(w, k):
                    pe.wait_ge(xl_done, 4 * w + 4)
                    if since(w, 2):
                        pe.wait_ge(lt_copied, w - 1)
                    for n, (x, g, c) in enumerate([(x, g, c) for x, g in ((xh, GWhl), (xl, GWh0)) for c in range(2)]):
                        last = nc.tensor.matmul(ps_lt[k][:, :], g[:, c, :], x[:, k, c, :], start=n == 0, stop=n == 3)
                    last.then_inc(lt_done, 1)

                def turn_logits(w, k):
                    pe.wait_ge(lt_copied, w + 1)
                    for i in range(4):
                        last = nc.tensor.matmul(ps_gate[:, ds((4 * w + i) * E, E)], LT[:, k, i * P:(i + 1) * P],
                                                ADD[:, :], start=True, stop=True)
                    last.then_inc(gate_done, 1)

                pe.wait_ge(gate_w, 1)
                for i in range(4):
                    transpose_x(0, 0, i)
                for w, k in steps(pe, NW, 2):
                    if until(w, 1, NW):
                        for i in range(4):
                            transpose_x(w + 1, 1 - k, i)
                    logits(w, k)
                    if since(w, 1):
                        turn_logits(w - 1, 1 - k)
                turn_logits(NW - 1, 1)
                pe.wait_ge(sel_done, 1)
                pe.wait_ge(consts, 6)
                sel = SEL[:, :, :].rearrange("p e t -> p (e t)")
                nc.tensor.matmul(ps_count[:, 0, :], lower_t[:, :], sel, start=True, stop=True)
                nc.tensor.matmul(ps_count[:, 1, :], ones_b[:, :], sel, start=True, stop=True).then_inc(pre_done, 1)
                for n in range(8):
                    pe.wait_ge(rows, n + 1)
                    pe.wait_ge(par_ids, n + 1)
                    pe.wait_ge(tile_ids, n + 1)
                    for g in range(CH):
                        last = nc.tensor.matmul(ps_tok, RSEL[:, n % 2, g, :],
                                                TSEL[:, n % 2, g, :, :].rearrange("p a j -> p (a j)"),
                                                start=n == 0 and g == 0, stop=n == 7 and g == CH - 1)
                    last.then_inc(tok_done, 1)

        expert_stage(nc, tag, S, ident, WUh, WUl, WDh, WDl, tok_u, unit_i, xn_dram, y_dram)
        shared_stage(nc, tag, S, X, ST, MV, RSTD, W12, slots_u, ident, WUh, WUl, WSh, WSl, y_dram, out_dram)


def split_passes(n_chunks):
    return [(c, a, b) for c in range(n_chunks) for a, b in ((0, 0), (0, 1), (1, 0))]


def expert_stage(nc, tag, S, ident, WUh, WUl, WDh, WDl, tok_u, unit_i, xn_dram, y_dram):
    D, FF, NU, NS, NJ, TAIL = S.D, S.FF, S.NU, S.NS, S.NJ, S.TAIL
    with ExitStack() as c2:
        def sb(name, shape, dt=F32):
            return c2.enter_context(nc.sbuf_tensor(f"{tag}2_{name}", shape, dt))

        def ps(name):
            return [c2.enter_context(nc.psum_tensor(f"{tag}2_{name}{i}", [P, 512], F32)) for i in range(2)]

        sem = semaphores(nc, c2, f"{tag}2")

        XG = sb("XG", [P, 4, D])
        xs = [sb("xh", [P, 2, D], F32R), sb("xl", [P, 2, D], F32R)]
        SG = sb("SG", [P, 2, FF])
        H = sb("H", [P, 2, 2 * P])
        hs = [sb("hh", [P, 2, 2 * P], F32R), sb("hl", [P, 2, 2 * P], F32R)]
        YS = sb("YS", [P, 4, D])
        ps_x, ps_u, ps_h, ps_y = ps("ps_x"), ps("ps_u"), ps("ps_h"), ps("ps_y")

        zeroed = sem("zeroed")
        gathered = [sem(f"gathered{i}") for i in range(4)]
        xT_done = sem("xT_done")
        xh_done = sem("xh_done")
        xl_done = sem("xl_done")
        up_done = sem("up_done")
        silu_done = sem("silu_done")
        h_ready = sem("h_ready")
        hT_done = sem("hT_done")
        hh_done = sem("hh_done")
        hl_done = sem("hl_done")
        y_done = sem("y_done")
        y_copied = sem("y_copied")
        y_out = [sem(f"y_out{i}") for i in range(4)]

        block = c2.enter_context(nc.Block())

        @block.gpsimd
        def _(pool):
            for j in range(NJ):
                if j >= 4:
                    pool.wait_ge(xT_done, j - 3)
                nc.gpsimd.indirect_dma_start(
                    out=XG[:, j % 4, :], out_offset=None, in_=xn_dram[:, :],
                    in_offset=bass.IndirectOffsetOnAxis(ap=tok_u[:, j:j + 1], axis=0)
                ).then_inc(gathered[j % 4], 16)

        @block.sync
        def _(sp):
            for j, k in steps(sp, NJ, 4):
                sp.wait_ge(y_copied, j + 1)
                sp.dma_start(y_dram[ds(j * P, P), :], YS[:, k, :]).then_inc(y_out[k], 16)
            for k in range(4):
                sp.wait_ge(y_out[k], 16 * (NJ // 4))

        @block.scalar
        def _(act):
            def y_copy(j, k):
                act.wait_ge(y_done, j + 1)
                if since(j, 4):
                    act.wait_ge(y_out[k], 16 * quarter(j, k))
                nc.scalar.activation(YS[:, k, :], ps_y[k % 2][:, 0:D], ACT.Copy).then_inc(y_copied, 1)

            def x_high(j, k):
                act.wait_ge(xT_done, j + 1)
                if since(j, 2):
                    act.wait_ge(up_done, j - 1)
                nc.scalar.activation(xs[0][:, k % 2, :], ps_x[k % 2][:, 0:D], ACT.Copy).then_inc(xh_done, 1)

            def h_high(j, k):
                act.wait_ge(hT_done, j + 1)
                if since(j, 2):
                    act.wait_ge(y_done, j - 1)
                nc.scalar.activation(hs[0][:, k % 2, :], ps_h[k % 2][:, 0:2 * P], ACT.Copy).then_inc(hh_done, 1)

            x_high(0, 0)
            for j, k in steps(act, NJ, 4):
                if until(j, 1, NJ):
                    x_high(j + 1, (k + 1) % 4)
                act.wait_ge(up_done, j + 1)
                if since(j, 2):
                    act.wait_ge(h_ready, j - 1)
                nc.scalar.activation(SG[:, k % 2, :], ps_u[k % 2][:, 0:FF], ACT.Silu).then_inc(silu_done, 1)
                if since(j, 1):
                    h_high(j - 1, (k - 1) % 4)
                if since(j, 2):
                    y_copy(j - 2, (k - 2) % 4)
            h_high(NJ - 1, 3)
            y_copy(NJ - 2, 2)
            y_copy(NJ - 1, 3)

        @block.vector
        def _(dve):
            nc.vector.memset(H[:, :, FF:2 * P], 0.0).then_inc(zeroed, 1)

            def x_low(j, k):
                dve.wait_ge(xh_done, j + 1)
                nc.vector.tensor_tensor(xs[1][:, k % 2, :], ps_x[k % 2][:, 0:D],
                                        xs[0][:, k % 2, :].bitcast(F32), ALU.subtract).then_inc(xl_done, 1)

            def h_low(j, k):
                dve.wait_ge(hh_done, j + 1)
                nc.vector.tensor_tensor(hs[1][:, k % 2, :], ps_h[k % 2][:, 0:2 * P],
                                        hs[0][:, k % 2, :].bitcast(F32), ALU.subtract).then_inc(hl_done, 1)

            x_low(0, 0)
            for j, k in steps(dve, NJ, 4):
                if until(j, 1, NJ):
                    x_low(j + 1, (k + 1) % 4)
                dve.wait_ge(silu_done, j + 1)
                if since(j, 2):
                    dve.wait_ge(hT_done, j - 1)
                nc.vector.tensor_tensor(H[:, k % 2, 0:FF], SG[:, k % 2, :], ps_u[k % 2][:, FF:2 * FF],
                                        ALU.mult).then_inc(h_ready, 1)
                if since(j, 1):
                    h_low(j - 1, (k - 1) % 4)
            h_low(NJ - 1, 3)

        @block.tensor
        def _(pe):
            W_up, W_down = (WUh, WUl), (WDh, WDl)
            units = {}

            kept = [pe.alloc_register(f"{tag}_kept_unit{i}") for i in range(2)]

            def unit_of(j, k, turn=0):
                if turn == -1:
                    return bass.RuntimeValue.of_register_unchecked(kept[k - U], min_val=NS, max_val=NU - 1)
                if k not in units:
                    units[k] = pe.value_load(unit_i[0:1, ds(j, 1)], min_val=NS, max_val=NU - 1)
                    if k >= U - 2:
                        pe.reg_mov(kept[k - U], units[k])
                return units[k]

            def transpose_x(j, k):
                pe.wait_ge(gathered[k % 4], 16 * (quarter(j, k % 4) + 1))
                for c in range(2):
                    last = nc.tensor.transpose(ps_x[k % 2][:, c * P:(c + 1) * P], XG[:, k % 4, c * P:(c + 1) * P],
                                               ident[:, :])
                last.then_inc(xT_done, 1)

            def up(j, k):
                unit = unit_of(j, k)
                pe.wait_ge(xl_done, j + 1)
                plan = split_passes(2)
                for i, (c, a, b) in enumerate(plan):
                    last = nc.tensor.matmul(ps_u[k % 2][:, 0:2 * FF], xs[a][:, k % 2, c * P:(c + 1) * P],
                                            W_up[b][:, c, ds(unit * (2 * FF), 2 * FF)],
                                            start=i == 0, stop=i == len(plan) - 1)
                last.then_inc(up_done, 1)

            def transpose_h(j, k):
                if isinstance(j, int) and j == 0:
                    pe.wait_ge(zeroed, 1)
                pe.wait_ge(h_ready, j + 1)
                for c in range(2):
                    last = nc.tensor.transpose(ps_h[k % 2][:, c * P:(c + 1) * P], H[:, k % 2, c * P:(c + 1) * P],
                                               ident[:, :])
                last.then_inc(hT_done, 1)

            def down(j, k, turn=0):
                unit = unit_of(j, k, turn)
                pe.wait_ge(hl_done, j + 1)
                if since(j, 2):
                    pe.wait_ge(y_copied, j - 1)
                plan = split_passes(2)
                for i, (c, a, b) in enumerate(plan):
                    rows = P if c == 0 else TAIL
                    last = nc.tensor.matmul(ps_y[k % 2][:, 0:D], hs[a][0:rows, k % 2, c * P:(c + 1) * P],
                                            W_down[b][c][:, ds((unit - NS) * D, D)],
                                            start=i == 0, stop=i == len(plan) - 1)
                last.then_inc(y_done, 1)

            U = 12
            transpose_x(0, 0)
            for j, k in steps(pe, NJ, U):
                if k == 0:
                    units.clear()
                if until(j, 1, NJ):
                    transpose_x(j + 1, (k + 1) % U)
                up(j, k)
                if since(j, 1):
                    transpose_h(j - 1, (k - 1) % U)
                if since(j, 2):
                    down(j - 2, (k - 2) % U, -1 if k < 2 else 0)
            transpose_h(NJ - 1, U - 1)
            down(NJ - 2, U - 2)
            down(NJ - 1, U - 1)


def quarter(n, k):
    return n // 4 if isinstance(n, int) else (n - k) // 4


def shared_stage(nc, tag, S, X, ST, MV, RSTD, W12, slots_u, ident, WUh, WUl, WSh, WSl, y_dram, out_dram):
    D, FF, NT, NS = S.D, S.FF, S.NT, S.NS
    HC = 3
    HF = NS * FF
    with ExitStack() as c3:
        def sb(name, shape, dt=F32):
            return c3.enter_context(nc.sbuf_tensor(f"{tag}3_{name}", shape, dt))

        def ps(name):
            return [c3.enter_context(nc.psum_tensor(f"{tag}3_{name}{i}", [P, 512], F32)) for i in range(2)]

        sem = semaphores(nc, c3, f"{tag}3")

        XN = sb("XN", [P, 4, D])
        xs = [sb("xh", [P, 2, D], F32R), sb("xl", [P, 2, D], F32R)]
        SG = sb("SG", [P, 2, FF])
        H = sb("H", [P, 2, HC * P])
        hs = [sb("hh", [P, 2, HC * P], F32R), sb("hl", [P, 2, HC * P], F32R)]
        YG = sb("YG", [P, 4, TOP_K, D])
        ST2 = ST[:, :, :].rearrange("p t s -> p (t s)")
        ps_x, ps_u, ps_h, ps_y = ps("ps_x"), ps("ps_u"), ps("ps_h"), ps("ps_y")
        X2 = X[:, :, :].rearrange("p t d -> p (t d)")
        MV2 = MV[:, :, :].rearrange("p t s -> p (t s)")
        W2 = W12[:, :, :].rearrange("p k t -> p (k t)")

        zeroed = sem("zeroed")
        gathered = [sem(f"gathered{i}") for i in range(4)]
        xn_ready = sem("xn_ready")
        xT_done = sem("xT_done")
        xh_done = sem("xh_done")
        xl_done = sem("xl_done")
        up_done = sem("up_done")
        silu_done = sem("silu_done")
        h_ready = sem("h_ready")
        hT_done = sem("hT_done")
        hh_done = sem("hh_done")
        hl_done = sem("hl_done")
        y_done = sem("y_done")
        mixed = sem("mixed")
        x_done = sem("x_done")
        stats = sem("stats")
        stored = sem("stored")

        block = c3.enter_context(nc.Block())

        @block.gpsimd
        def _(pool):
            for t in range(NT):
                if t >= 4:
                    pool.wait_ge(x_done, t - 3)
                for c in range(TOP_K):
                    nc.gpsimd.indirect_dma_start(
                        out=YG[:, t % 4, c, :], out_offset=None, in_=y_dram[:, :],
                        in_offset=bass.IndirectOffsetOnAxis(ap=slots_u[:, c, t:t + 1], axis=0)
                    ).then_inc(gathered[t % 4], 16)

        @block.sync
        def _(sp):
            if out_dram is not None:
                for t, k in steps(sp, NT, 4):
                    sp.wait_ge(x_done, t + 1)
                    sp.dma_start(out_dram[ds(t * P, P), :], X2[:, ds(t * D, D)]).then_inc(stored, 16)
                sp.wait_ge(stored, 16 * NT)

        @block.scalar
        def _(act):
            def x_high(t, k):
                act.wait_ge(xT_done, t + 1)
                if since(t, 2):
                    act.wait_ge(up_done, 2 * t - 2)
                nc.scalar.activation(xs[0][:, k % 2, :], ps_x[k % 2][:, 0:D], ACT.Copy).then_inc(xh_done, 1)

            def h_high(t, k):
                act.wait_ge(hT_done, t + 1)
                if since(t, 2):
                    act.wait_ge(y_done, t - 1)
                nc.scalar.activation(hs[0][:, k % 2, :], ps_h[k % 2][:, 0:HC * P], ACT.Copy).then_inc(hh_done, 1)

            x_high(0, 0)
            for t, k in steps(act, NT, 4):
                for s in range(NS):
                    act.wait_ge(up_done, 2 * t + s + 1)
                    if since(t, 1):
                        act.wait_ge(h_ready, 2 * t + s - 1)
                    nc.scalar.activation(SG[:, s, :], ps_u[s][:, 0:FF], ACT.Silu).then_inc(silu_done, 1)
                    if s == 0 and until(t, 1, NT):
                        x_high(t + 1, (k + 1) % 4)
                    if s == 0 and since(t, 1):
                        h_high(t - 1, (k - 1) % 4)
            h_high(NT - 1, 3)

        @block.vector
        def _(dve):
            nc.vector.memset(H[:, :, HF:HC * P], 0.0).then_inc(zeroed, 1)

            def normalise(t, k):
                if since(t, 4):
                    dve.wait_ge(xT_done, t - 3)
                nc.vector.tensor_scalar(XN[:, k, :], X2[:, ds(t * D, D)], MV2[:, ds(2 * t, 1)],
                                        RSTD[:, ds(t, 1)], ALU.subtract, ALU.mult).then_inc(xn_ready, 1)

            def x_low(t, k):
                dve.wait_ge(xh_done, t + 1)
                nc.vector.tensor_tensor(xs[1][:, k % 2, :], ps_x[k % 2][:, 0:D],
                                        xs[0][:, k % 2, :].bitcast(F32), ALU.subtract).then_inc(xl_done, 1)

            def h_low(t, k):
                dve.wait_ge(hh_done, t + 1)
                nc.vector.tensor_tensor(hs[1][:, k % 2, :], ps_h[k % 2][:, 0:HC * P],
                                        hs[0][:, k % 2, :].bitcast(F32), ALU.subtract).then_inc(hl_done, 1)

            def add_expert(t, k, c):
                x_t = X2[:, ds(t * D, D)]
                if c == 0:
                    dve.wait_ge(gathered[k], 32 * (quarter(t, k) + 1))
                else:
                    dve.wait_ge(mixed, 2 * t + 1)
                nc.vector.scalar_tensor_tensor(x_t, YG[:, k, c, :], W2[:, ds(t + c * NT, 1)], x_t,
                                               ALU.mult, ALU.add).then_inc(mixed, 1)

            def add_shared(t, k):
                x_t = X2[:, ds(t * D, D)]
                dve.wait_ge(mixed, 2 * t + 2)
                dve.wait_ge(y_done, t + 1)
                nc.vector.scalar_tensor_tensor(x_t, ps_y[k % 2][:, 0:D], HALF, x_t,
                                               ALU.mult, ALU.add).then_inc(x_done, 1)

            def statistics(t):
                if out_dram is None:
                    dve.wait_ge(x_done, t + 1)
                    nc.vector.bn_stats(ST2[:, ds(6 * t, 6)], X2[:, ds(t * D, D)]).then_inc(stats, 1)

            def gated(t, k, s):
                dve.wait_ge(silu_done, 2 * t + s + 1)
                if since(t, 2):
                    dve.wait_ge(hT_done, t - 1)
                nc.vector.tensor_tensor(H[:, k % 2, s * FF:(s + 1) * FF], SG[:, s, :], ps_u[s][:, FF:2 * FF],
                                        ALU.mult).then_inc(h_ready, 1)

            normalise(0, 0)
            normalise(1, 1)
            x_low(0, 0)
            for t, k in steps(dve, NT, 4):
                gated(t, k, 0)
                if until(t, 2, NT):
                    normalise(t + 2, (k + 2) % 4)
                if until(t, 1, NT):
                    x_low(t + 1, (k + 1) % 4)
                if since(t, 1):
                    h_low(t - 1, (k - 1) % 4)
                if since(t, 3):
                    add_expert(t - 3, (k - 3) % 4, 0)
                gated(t, k, 1)
                if since(t, 3):
                    add_expert(t - 3, (k - 3) % 4, 1)
                if since(t, 4):
                    statistics(t - 4)
                if since(t, 3):
                    add_shared(t - 3, (k - 3) % 4)
            h_low(NT - 1, 3)
            for t in range(NT - 3, NT):
                add_expert(t, t % 4, 0)
                add_expert(t, t % 4, 1)
                add_shared(t, t % 4)
            for t in range(NT - 4, NT):
                statistics(t)

        @block.tensor
        def _(pe):
            W_up, W_down = (WUh, WUl), (WSh, WSl)

            def transpose_x(t, k):
                pe.wait_ge(xn_ready, t + 1)
                if since(t, 2):
                    pe.wait_ge(xl_done, t - 1)
                for c in range(2):
                    last = nc.tensor.transpose(ps_x[k % 2][:, c * P:(c + 1) * P],
                                               XN[:, k, c * P:(c + 1) * P], ident[:, :])
                last.then_inc(xT_done, 1)

            def up(t, k, s):
                pe.wait_ge(xl_done, t + 1)
                if since(t, 1):
                    pe.wait_ge(h_ready, 2 * t + s - 1)
                plan = split_passes(2)
                for i, (c, a, b) in enumerate(plan):
                    last = nc.tensor.matmul(ps_u[s][:, 0:2 * FF], xs[a][:, k % 2, c * P:(c + 1) * P],
                                            W_up[b][:, c, s * 2 * FF:(s + 1) * 2 * FF],
                                            start=i == 0, stop=i == len(plan) - 1)
                last.then_inc(up_done, 1)

            def transpose_h(t, k):
                pe.wait_ge(h_ready, 2 * t + 2)
                for c in range(HC):
                    last = nc.tensor.transpose(ps_h[k % 2][:, c * P:(c + 1) * P], H[:, k % 2, c * P:(c + 1) * P],
                                               ident[:, :])
                last.then_inc(hT_done, 1)

            def down(t, k):
                if since(t, 2):
                    pe.wait_ge(x_done, t - 1)
                pe.wait_ge(hl_done, t + 1)
                plan = split_passes(HC)
                for i, (c, a, b) in enumerate(plan):
                    rows = min(P, HF - c * P)
                    last = nc.tensor.matmul(ps_y[k % 2][:, 0:D], hs[a][0:rows, k % 2, c * P:(c + 1) * P],
                                            W_down[b][0:rows, c, :], start=i == 0, stop=i == len(plan) - 1)
                last.then_inc(y_done, 1)

            transpose_x(0, 0)
            pe.wait_ge(zeroed, 1)
            for t, k in steps(pe, NT, 4):
                up(t, k, 0)
                if until(t, 1, NT):
                    transpose_x(t + 1, (k + 1) % 4)
                if since(t, 1):
                    transpose_h(t - 1, (k - 1) % 4)
                up(t, k, 1)
                if since(t, 2):
                    down(t - 2, (k - 2) % 4)
            transpose_h(NT - 1, 3)
            down(NT - 2, 2)
            down(NT - 1, 3)


def attention(nc, S, X, ST, MV, ident, w_qkv, b_qk, b_v, w_out, b_out):
    with ExitStack() as ctx:
        V = ctx.enter_context(nc.sbuf_tensor("V", [P, S.NT, S.HEADS, S.HD + 1], F32))
        qk_dram = nc.dram_tensor("qk_scratch", (S.B, S.G, 2, P, S.L), F32, kind="Internal").ap()
        x_dram = nc.dram_tensor("x_scratch", (S.T, S.D), F32, kind="Internal").ap()
        project_stage(nc, S, X, ST, MV, ident, w_qkv, b_qk, b_v, V, qk_dram, x_dram)
        softmax_stage(nc, S, ident, V, X, qk_dram)
        output_stage(nc, S, X, ST, ident, w_out, b_out, x_dram)


def project_stage(nc, S, X, ST, MV, ident, w_qkv, b_qk, b_v, V, qk_dram, x_dram):
    D, NT, HD, HEADS, G, L = S.D, S.NT, S.HD, S.HEADS, S.G, S.L
    GF = D // G
    W = 4 * P
    assert G == 4
    NW = S.T // W
    with ExitStack() as c:
        def sb(name, shape, dt=F32):
            return c.enter_context(nc.sbuf_tensor(f"p_{name}", shape, dt))

        def ps(name, n=2):
            return [c.enter_context(nc.psum_tensor(f"p_{name}{i}", [P, 512], F32)) for i in range(n)]

        sem = semaphores(nc, c, "p")

        WR = sb("WR", [P, 2, 3 * D])
        Wh = sb("Wh", [P, 2, 3 * D], F32R)
        Wl = sb("Wl", [P, 2, 3 * D], F32R)
        BQK = sb("BQK", [P, G])
        BV = sb("BV", [P, D])
        RSTD = sb("RSTD", [P, NT])
        XN = sb("XN", [P, 4, D])
        xs = [sb("xh", [P, 2, 2, W], F32R), sb("xl", [P, 2, 2, W], F32R)]
        QKh = sb("QKh", [P, G, W], F32R)
        QKl = sb("QKl", [P, G, W], F32R)
        ps_x, ps_qk, ps_v = ps("ps_x"), ps("ps_qk"), ps("ps_v")
        X2 = X[:, :, :].rearrange("p t d -> p (t d)")
        MV2 = MV[:, :, :].rearrange("p t s -> p (t s)")
        V2 = V[:, :, :, :].rearrange("p t h e -> p (t h e)")

        weights_in = sem("weights_in")
        weights_hi = sem("weights_hi")
        weights = sem("weights")
        ones = sem("ones")
        chain = sem("chain")
        rstd_in = sem("rstd_in")
        rstd_out = sem("rstd_out")
        xn_ready = sem("xn_ready")
        xT_done = sem("xT_done")
        xh_done = sem("xh_done")
        xl_done = sem("xl_done")
        qk_done = sem("qk_done")
        qkh_done = sem("qkh_done")
        qkl_done = sem("qkl_done")
        x_out = sem("x_out")
        qk_out = [sem(f"qk_out{i}") for i in range(G)]
        v_done = sem("v_done")
        v_copied = sem("v_copied")

        block = c.enter_context(nc.Block())

        @block.sync
        def _(sp):
            sp.dma_start(WR[:, :, :], w_qkv.rearrange("(c p) f -> p c f", p=P)).then_inc(weights_in, 16)
            sp.dma_start(BQK[:, :], b_qk).then_inc(weights_in, 16)
            sp.dma_start(BV[:, :], b_v.rearrange("(a f) -> a f", a=1)
                         .to_broadcast([P, D])).then_inc(weights_in, 16)
            sp.dma_start(x_dram.rearrange("(t p) d -> p t d", p=P), X[:, :, :]).then_inc(x_out, 16)
            for n in range(NW * G):
                w, g = n // G, n % G
                cols = slice(w % 2 * W, (w % 2 + 1) * W)
                sp.wait_ge(qkh_done, n + 1)
                sp.dma_start(qk_dram[w // 2, g, 0, :, cols], QKh[:, g, :].bitcast(F32)).then_inc(qk_out[g], 16)
                sp.wait_ge(qkl_done, n + 1)
                sp.dma_start(qk_dram[w // 2, g, 1, :, cols], QKl[:, g, :].bitcast(F32)).then_inc(qk_out[g], 16)
            for i in range(G):
                sp.wait_ge(qk_out[i], 32 * NW)
            sp.wait_ge(x_out, 16)

        @block.gpsimd
        def _(pool):
            nc.gpsimd.memset(V[:, :, :, HD:HD + 1], 1.0).then_inc(ones, 1)
            pool.wait_ge(weights_hi, 1)
            nc.gpsimd.tensor_tensor(Wl[:, 1, :], WR[:, 1, :], Wh[:, 1, :].bitcast(F32),
                                    ALU.subtract).then_inc(weights, 1)

        @block.scalar
        def _(act):
            act.wait_ge(rstd_in, 1)
            nc.scalar.activation(RSTD[:, :], RSTD[:, :], ACT.Sqrt).then_inc(rstd_out, 1)
            act.wait_ge(weights_in, 48)
            for c in (1, 0):
                nc.scalar.activation(Wh[:, c, :], WR[:, c, :], ACT.Copy).then_inc(weights_hi, 1)

            def x_high(w, k, i):
                act.wait_ge(xT_done, 4 * w + i + 1)
                if i == 0 and since(w, 2):
                    act.wait_ge(v_done, 4 * w - 4)
                nc.scalar.activation(xs[0][:, k, :, i * P:(i + 1) * P],
                                     ps_x[i % 2][:, 0:D].rearrange("p (c n) -> p c n", c=2),
                                     ACT.Copy).then_inc(xh_done, 1)

            for i in range(4):
                x_high(0, 0, i)
            for w, k in steps(act, NW, 2):
                for g in range(G):
                    if until(w, 1, NW):
                        x_high(w + 1, 1 - k, g)
                    act.wait_ge(qk_done, G * w + g + 1)
                    if since(w, 1):
                        act.wait_ge(qk_out[g], 32 * w)
                    nc.scalar.activation(QKh[:, g, :], ps_qk[g % 2][:, :], ACT.Identity,
                                         bias=BQK[:, g:g + 1]).then_inc(qkh_done, 1)

        @block.vector
        def _(dve):
            count = [0]

            def link(ins):
                count[0] += 1
                ins.then_inc(chain, 1)
                dve.wait_ge(chain, count[0])

            for t in range(NT):
                last = nc.vector.bn_aggr(MV[:, t, :], ST[:, t, :])
            link(last)
            nc.vector.tensor_scalar(RSTD[:, :], MV[:, :, 1], EPS, None, ALU.add).then_inc(rstd_in, 1)
            dve.wait_ge(rstd_out, 1)
            link(nc.vector.reciprocal(RSTD[:, :], RSTD[:, :]))
            dve.wait_ge(weights_in, 48)
            dve.wait_ge(ones, 1)

            def normalise(w, i):
                if since(w, 1):
                    dve.wait_ge(xT_done, 4 * w + i - 3)
                t = 4 * w + i
                nc.vector.tensor_scalar(XN[:, i, :], X2[:, ds(t * D, D)], MV2[:, ds(2 * t, 1)],
                                        RSTD[:, ds(t, 1)], ALU.subtract, ALU.mult).then_inc(xn_ready, 1)

            def x_low(w, k, i):
                dve.wait_ge(xh_done, 4 * w + i + 1)
                nc.vector.tensor_tensor(xs[1][:, k, :, i * P:(i + 1) * P],
                                        ps_x[i % 2][:, 0:D].rearrange("p (c n) -> p c n", c=2),
                                        xs[0][:, k, :, i * P:(i + 1) * P].bitcast(F32),
                                        ALU.subtract).then_inc(xl_done, 1)

            for i in range(4):
                normalise(0, i)
            dve.wait_ge(weights_hi, 2)
            nc.vector.tensor_tensor(Wl[:, 0, :], WR[:, 0, :], Wh[:, 0, :].bitcast(F32),
                                    ALU.subtract).then_inc(weights, 1)
            for i in range(4):
                x_low(0, 0, i)
            normalise(1, 0)
            for w, k in steps(dve, NW, 2):
                for g in range(G):
                    if g + 1 < G and until(w, 1, NW):
                        normalise(w + 1, g + 1)
                    if g + 1 == G and until(w, 2, NW):
                        normalise(w + 2, 0)
                    if until(w, 1, NW):
                        x_low(w + 1, 1 - k, g)
                    dve.wait_ge(qkh_done, G * w + g + 1)
                    nc.vector.scalar_tensor_tensor(QKl[:, g, :], ps_qk[g % 2][:, :], BQK[:, g:g + 1],
                                                   QKh[:, g, :].bitcast(F32), ALU.add,
                                                   ALU.subtract).then_inc(qkl_done, 1)
                    t = 4 * w + g
                    dve.wait_ge(v_done, t + 1)
                    nc.vector.tensor_tensor(
                        V2[:, ds(t * (HEADS * (HD + 1)), HEADS * (HD + 1))]
                        .rearrange("p (h e) -> p h e", h=HEADS)[:, :, 0:HD],
                        ps_v[g % 2][:, 0:D].rearrange("p (h e) -> p h e", h=HEADS),
                        BV[:, :].rearrange("p (h e) -> p h e", h=HEADS), ALU.add).then_inc(v_copied, 1)

        @block.tensor
        def _(pe):
            Ws = (Wh, Wl)

            def transpose_x(w, i):
                pe.wait_ge(xn_ready, 4 * w + i + 1)
                if i >= 2 or since(w, 1):
                    pe.wait_ge(xl_done, 4 * w + i - 1)
                for c in range(2):
                    last = nc.tensor.transpose(ps_x[i % 2][:, c * P:(c + 1) * P],
                                               XN[:, i, c * P:(c + 1) * P], ident[:, :])
                last.then_inc(xT_done, 1)

            for i in range(4):
                transpose_x(0, i)
            pe.wait_ge(weights, 2)
            for w, k in steps(pe, NW, 2):
                pe.wait_ge(xl_done, 4 * w + 4)
                for g in range(G):
                    if until(w, 1, NW):
                        transpose_x(w + 1, g)
                    if g >= 2 or since(w, 1):
                        pe.wait_ge(qkl_done, G * w + g - 1)
                    for i, (c, a, b) in enumerate(split_passes(2)):
                        wt = Ws[a][:, c, 2 * g * GF:2 * (g + 1) * GF]
                        last = nc.tensor.matmul(ps_qk[g % 2][:, :], wt, xs[b][:, k, c, :], start=i == 0, stop=i == 5)
                    last.then_inc(qk_done, 1)
                    if g >= 2 or since(w, 1):
                        pe.wait_ge(v_copied, 4 * w + g - 1)
                    for i, (c, a, b) in enumerate(split_passes(2)):
                        last = nc.tensor.matmul(ps_v[g % 2][:, 0:D], xs[a][:, k, c, g * P:(g + 1) * P],
                                                Ws[b][:, c, 2 * D:3 * D], start=i == 0, stop=i == 5)
                    last.then_inc(v_done, 1)


def softmax_stage(nc, S, ident, V, ATT, qk_dram):
    D, NT, HD, HEADS, G, L = S.D, S.NT, S.HD, S.HEADS, S.G, S.L
    NG = S.B * G
    NQ = L // P
    W = 512
    GH = HEADS // G
    GF = D // G
    V1 = HD + 1
    PH = 2 * HD
    R = 3 * PH
    RM = R + 2
    SCALE = float(HD) ** -0.5
    NEG = -1e30
    B_STEPS = [(hf, i) for hf in range(2) for i in range(4 * hf + 4)]
    NB = len(B_STEPS)
    DIAGONAL = [n for n, (hf, i) in enumerate(B_STEPS) if i >= 4 * hf]
    A_UNITS = []
    for i in range(NQ):
        for s in range(1 + i // 4):
            keys = min((i + 1) * P - s * W, W)
            wide = W // keys
            starts = range(0, GH, wide)
            A_UNITS += [(i, s, h, min(wide, GH - h), keys) for h in starts]
    RING = 3
    while len(A_UNITS) % RING:
        at = max(n for n, unit in enumerate(A_UNITS) if unit[3] > 1)
        i, s, h, heads, keys = A_UNITS[at]
        A_UNITS[at:at + 1] = [(i, s, h, 1, keys), (i, s, h + 1, heads - 1, keys)]
    NA = len(A_UNITS)
    a_cost = [heads * keys + 64 for _, _, _, heads, keys in A_UNITS]
    AHEAD = next(v for v in range(NA) if sum(a_cost[:v]) * 3 >= sum(a_cost))
    beside = [(1, v) for v in range(AHEAD, NA)] + [(2, v) for v in range(AHEAD)]
    b_cost = [GH * (min(W, (hf + 1) * W - i * P)) for hf, i in B_STEPS]
    A_BESIDE = [[] for _ in B_STEPS]
    gone = 0
    for one in beside:
        step = next(n for n in range(NB) if gone * sum(b_cost) < sum(b_cost[:n + 1]) * sum(a_cost))
        A_BESIDE[step].append(one)
        gone += a_cost[one[1]]
    MAX_T = 1 + max(n for n in range(NB) if (1, NA - 1) in A_BESIDE[n])
    SLOTS = 6
    LOAD = 9 * 16
    PLACE = 2 * 16
    assert GH == 4 and D // G == 64 and GH * NB % RING == 0 and NB * 2 % SLOTS == 0 and MAX_T < NB
    with ExitStack() as c:
        def sb(name, shape, dt=F32):
            return c.enter_context(nc.sbuf_tensor(f"s_{name}", shape, dt))

        def ps(name, shape):
            return c.enter_context(nc.psum_tensor(f"s_{name}", shape, F32))

        sem = semaphores(nc, c, "s")

        def ring(name, n):
            return [sem(f"{name}{i}") for i in range(n)]

        QO = [sb(f"QO{i}", [P, GH, L], F32R) for i in range(4)]
        KO = [sb(f"KO{i}", [P, 2, L], F32R) for i in range(4)]
        VG = [sb(f"VG{i}", [P, NQ, GH * V1]) for i in range(4)]
        PR = sb("PR", [P, SLOTS, 2, W])
        MX = sb("MX", [P, GH, NQ, 2])
        NM = sb("NM", [P, GH * NQ])
        NMh = sb("NMh", [GH * NQ, P], F32R)
        NMl = sb("NMl", [GH * NQ, P], F32R)
        OS = sb("OS", [P, W])
        RC = sb("RC", [P, 4, GH])
        identb = sb("identb", [P, P], BF16)
        zero_b = sb("zero_b", [P, GH, P], BF16)
        neg = sb("neg", [P, GH, P], BF16)
        ps_a = [ps(f"ps_a{i}", [P, W]) for i in range(RING)]
        ps_b = [ps(f"ps_b{i}", [P, W]) for i in range(RING)]
        ps_o = ps("ps_o", [P, W])
        ps_t = ps("ps_t", [P, W])
        ATT2 = ATT[:, :, :].rearrange("p t d -> p (t d)")
        V2 = V[:, :, :, :].rearrange("p t h e -> p t (h e)")

        consts = sem("consts")
        presets = sem("presets")
        zeros = ring("zeros", 2)
        ones = sem("ones")
        values = sem("values")
        operands = ring("operands", 4)
        a_done = sem("a_done")
        a_read = sem("a_read")
        max_ready = sem("max_ready")
        maxT_done = sem("maxT_done")
        maxh_done = sem("maxh_done")
        maxl_done = sem("maxl_done")
        max_rows = ring("max_rows", 4)
        b_done = sem("b_done")
        exp_done = sem("exp_done")
        masked = sem("masked")
        pv_done = sem("pv_done")
        o_copied = sem("o_copied")
        oT_done = sem("oT_done")
        recip = sem("recip")
        att_done = sem("att_done")

        block = c.enter_context(nc.Block())

        def turn(g, k, back):
            return g - back, (k - back) % 4

        @block.sync
        def _(sp):
            def load(g):
                k = g % 4
                if g >= 4:
                    sp.wait_ge(pv_done, NB * (g - 3))
                for part, (q, kk) in enumerate(((0, 0), (0, 1), (1, 0))):
                    at = part * PH
                    keys = qk_dram[g // G, g % G, kk, GF:2 * GF, :].rearrange("(r c) l -> r c l", c=2)
                    sp.dma_start(KO[k][at:at + PH, :, :].bitcast(F32), keys).then_inc(operands[k], 16)
                    for hp in range(2):
                        rows = slice(at + hp * HD, at + (hp + 1) * HD)
                        queries = qk_dram[g // G, g % G, q, hp * PH:(hp + 1) * PH, :]\
                            .rearrange("(r c) l -> r c l", c=2)
                        sp.dma_start(QO[k][rows, 2 * hp:2 * hp + 2, :].bitcast(F32), queries)\
                            .then_inc(operands[k], 16)

            def place_max(g):
                k = g % 4
                sp.wait_ge(maxh_done, g + 1)
                sp.wait_ge(maxl_done, g + 1)
                for r, src in enumerate((NMh, NMl)):
                    sp.dma_start(QO[k][R + r:R + r + 1, :, :].bitcast(F32), src[:, :].bitcast(F32))\
                        .then_inc(max_rows[k], 16)

            for g in range(4):
                sp.wait_ge(zeros[g % 2], g // 2 + 1)
                sp.wait_ge(ones, g + 1)
                load(g)
            place_max(0)
            for g in range(NG):
                if g + 1 < NG:
                    place_max(g + 1)
                if g + 4 < NG:
                    load(g + 4)

        @block.gpsimd
        def _(pool):
            nc.gpsimd.memset(zero_b[:, :, :], 0.0).then_inc(consts, 1)
            pool.wait_ge(consts, 1)
            nc.gpsimd.affine_select(out=neg[:, :, :], in_=zero_b[:, :, :], compare_op=ALU.is_ge, fill=NEG, base=0,
                                    pattern=[[0, GH], [-1, P]], channel_multiplier=1).then_inc(consts, 1)
            nc.gpsimd.tensor_copy(identb[:, :], ident[:, :]).then_inc(consts, 1)
            for k in (1, 3):
                nc.gpsimd.memset(QO[k][0:RM, :, :].bitcast(F32), 0.0).then_inc(zeros[1], 1)


            def prepare(g):
                if g >= 4:
                    pool.wait_ge(pv_done, NB * (g - 3))
                batch = V2[:, ds(g // G * NQ, NQ), g % G * GH * V1:(g % G + 1) * GH * V1]
                nc.gpsimd.tensor_copy(VG[g % 4][:, :, :], batch).then_inc(values, 1)

            for g in range(3):
                prepare(g)
            for g in range(NG):
                k = g % 4
                for n in range(NB):
                    if n in DIAGONAL:
                        for pair in range(2):
                            u = 2 * n + pair
                            pool.wait_ge(exp_done, GH * NB * g + 2 * u + 2)
                            tile = PR[:, u % SLOTS, :, 0:P]
                            nc.gpsimd.affine_select(out=tile, in_=tile, compare_op=ALU.is_ge, fill=0.0, base=0,
                                                    pattern=[[0, 2], [1, P]], channel_multiplier=-1)\
                                .then_inc(masked, 1)
                    if n == 3 and until(g, 3, NG):
                        prepare(g + 3)

        @block.scalar
        def _(act):
            def max_high(g, k):
                act.wait_ge(maxT_done, g + 1)
                if since(g, 1):
                    p, pk = turn(g, k, 1)
                    act.wait_ge(max_rows[pk], PLACE * (quarter(p, pk) + 1))
                nc.scalar.activation(NMh[:, :], ps_t[0:GH * NQ, 0:P], ACT.Copy).then_inc(maxh_done, 1)

            def copy_output(g, hf):
                act.wait_ge(pv_done, NB * g + (4 if hf == 0 else NB))
                if hf == 1 or since(g, 1):
                    act.wait_ge(oT_done, 2 * g + hf)
                nc.scalar.activation(OS[:, :], ps_o[:, :], ACT.Copy).then_inc(o_copied, 1)

            max_high(0, 0)
            for g, k in steps(act, NG, 4):
                for n, (hf, i) in enumerate(B_STEPS):
                    lo = max(0, i * P - hf * W)
                    for h in range(GH):
                        u = GH * n + h
                        act.wait_ge(b_done, GH * NB * g + u + 1)
                        if h == 0 and (n >= SLOTS // 2 or since(g, 1)):
                            act.wait_ge(pv_done, NB * g + n + 1 - SLOTS // 2)
                        nc.scalar.activation(PR[:, u // 2 % SLOTS, u % 2, 0:W - lo], ps_b[u % RING][:, lo:W], ACT.Exp,
                                             scale=SCALE).then_inc(exp_done, 1)
                    if n == 4:
                        copy_output(g, 0)
                    if n == MAX_T and until(g, 1, NG):
                        max_high(g + 1, (k + 1) % 4)
                copy_output(g, 1)

        @block.vector
        def _(dve):
            nc.vector.memset(QO[0][0:RM, :, :].bitcast(F32), 0.0).then_inc(zeros[0], 1)
            nc.vector.memset(KO[0][R:RM, :, :].bitcast(F32), 1.0).then_inc(ones, 1)
            nc.vector.memset(ps_o[:, :], 0.0)
            nc.vector.memset(MX[:, :, :, :], -3e38).then_inc(presets, 1)
            nc.vector.memset(KO[1][R:RM, :, :].bitcast(F32), 1.0).then_inc(ones, 1)
            nc.vector.memset(QO[2][0:RM, :, :].bitcast(F32), 0.0).then_inc(zeros[0], 1)
            for k in (2, 3):
                nc.vector.memset(KO[k][R:RM, :, :].bitcast(F32), 1.0).then_inc(ones, 1)
            dve.wait_ge(presets, 1)

            def a_units(g, units):
                for v in units:
                    i, s, h, heads, keys = A_UNITS[v]
                    if v == 0 and since(g, 1):
                        dve.wait_ge(max_ready, g)
                    dve.wait_ge(a_done, NA * g + v + 1)
                    nc.vector.tensor_reduce(MX[:, h:h + heads, i, s],
                                            ps_a[v % RING][:, 0:heads * keys].rearrange("p (h n) -> p h n", h=heads),
                                            AX.X, ALU.max).then_inc(a_read, 1)

            def combine(g):
                dve.wait_ge(a_read, NA * (g + 1))
                if since(g, 1):
                    dve.wait_ge(maxT_done, g)
                nc.vector.tensor_reduce(NM[:, :].rearrange("p (h i) -> p h i", h=GH), MX[:, :, :, :], AX.X,
                                        ALU.max, negate=True).then_inc(max_ready, 1)

            def max_low(g):
                dve.wait_ge(maxh_done, g + 1)
                nc.vector.tensor_tensor(NMl[:, :], ps_t[0:GH * NQ, 0:P], NMh[:, :].bitcast(F32),
                                        ALU.subtract).then_inc(maxl_done, 1)

            def normalise(g, k, hf):
                turned = ps_t[:, :].rearrange("p (j h r) -> p j h r", j=4, h=GH)
                dve.wait_ge(oT_done, 2 * g + hf + 1)
                if hf == 1 or since(g, 1):
                    dve.wait_ge(att_done, 2 * g + hf)
                nc.vector.reciprocal(RC[:, :, :], turned[:, :, :, HD]).then_inc(recip, 1)
                dve.wait_ge(recip, 2 * g + hf + 1)
                half_rows = ATT2[:, ds((quarter(g, k) * NQ + 4 * hf) * D, 4 * D)].rearrange("p (j d) -> p j d", j=4)
                nc.vector.tensor_tensor(
                    half_rows[:, :, k * GF:(k + 1) * GF].rearrange("p j (h e) -> p j h e", h=GH),
                    turned[:, :, :, 0:HD], RC[:, :, :].unsqueeze(3).to_broadcast([P, 4, GH, HD]),
                    ALU.mult).then_inc(att_done, 1)

            a_units(0, range(NA))
            combine(0)
            max_low(0)
            a_units(1, range(AHEAD))
            for g, k in steps(dve, NG, 4):
                for n in range(NB):
                    for groups, v in A_BESIDE[n]:
                        if until(g, groups, NG):
                            a_units(g + groups, [v])
                            if v == NA - 1:
                                combine(g + 1)
                    if n == 1 and since(g, 1):
                        normalise(*turn(g, k, 1), 1)
                    if n == MAX_T - 1:
                        normalise(g, k, 0)
                    if n == MAX_T and until(g, 1, NG):
                        max_low(g + 1)
            normalise(NG - 1, 3, 1)

        @block.tensor
        def _(pe):
            def a_units(g, k, units):
                for v in units:
                    i, s, h0, heads, keys = A_UNITS[v]
                    diagonal = s == i // 4
                    if v == 0:
                        pe.wait_ge(operands[k], LOAD * (quarter(g, k) + 1))
                    if v >= RING or since(g, 1):
                        pe.wait_ge(a_read, NA * g + v + 1 - RING)
                    if diagonal:
                        scores = ps_a[v % RING][:, 0:heads * keys].rearrange("p (h n) -> p h n", h=heads)
                        nc.tensor.matmul(scores[:, :, keys - P:keys], identb[:, :], neg[:, 0:heads, :],
                                         start=True, stop=False, skip_group_check=True)
                    for h in range(h0, h0 + heads):
                        at = (h - h0) * keys
                        last = nc.tensor.matmul(ps_a[v % RING][:, at:at + keys], QO[k][0:R, h, i * P:(i + 1) * P],
                                                KO[k][0:R, h % 2, s * W:s * W + keys], start=not diagonal,
                                                stop=True, skip_group_check=True)
                    last.then_inc(a_done, 1)

            def turn_max(g):
                pe.wait_ge(max_ready, g + 1)
                if since(g, 1):
                    pe.wait_ge(att_done, 2 * g - 1)
                nc.tensor.transpose(ps_t[0:GH * NQ, 0:P], NM[:, :], ident[:, :]).then_inc(maxT_done, 1)

            def b_unit(g, k, n, h):
                hf, i = B_STEPS[n]
                lo = max(0, i * P - hf * W)
                u = GH * n + h
                if u == 0:
                    pe.wait_ge(operands[k], LOAD * (quarter(g, k) + 1))
                    pe.wait_ge(max_rows[k], PLACE * (quarter(g, k) + 1))
                if u >= RING or since(g, 1):
                    pe.wait_ge(exp_done, GH * NB * g + u + 1 - RING)
                nc.tensor.matmul(ps_b[u % RING][:, lo:W], KO[k][0:RM, h % 2, i * P:(i + 1) * P],
                                 QO[k][0:RM, h, hf * W + lo:(hf + 1) * W], start=True, stop=True).then_inc(b_done, 1)

            def pv_step(g, k, n):
                hf, i = B_STEPS[n]
                lo = max(0, i * P - hf * W)
                if n == 0:
                    pe.wait_ge(values, g + 1)
                if i == 0 and (n > 0 or since(g, 1)):
                    pe.wait_ge(o_copied, 2 * g + hf)
                pe.wait_ge(exp_done, GH * NB * g + GH * (n + 1))
                if n in DIAGONAL:
                    pe.wait_ge(masked, 2 * len(DIAGONAL) * g + 2 * DIAGONAL.index(n) + 2)
                for h in range(GH):
                    last = nc.tensor.matmul(ps_o[32 * h:32 * h + V1, lo:W], VG[k][:, i, h * V1:(h + 1) * V1],
                                            PR[:, (2 * n + h // 2) % SLOTS, h % 2, 0:W - lo],
                                            start=i == 0, stop=i == 4 * hf + 3, skip_group_check=True)
                last.then_inc(pv_done, 1)

            def turn_output(g, hf):
                pe.wait_ge(o_copied, 2 * g + hf + 1)
                if hf == 1:
                    if until(g, 1, NG):
                        pe.wait_ge(maxl_done, g + 2)
                    else:
                        pe.wait_ge(att_done, 2 * g + 1)
                elif since(g, 1):
                    pe.wait_ge(att_done, 2 * g)
                else:
                    pe.wait_ge(maxl_done, 1)
                for j in range(4):
                    last = nc.tensor.transpose(ps_t[:, j * P:(j + 1) * P], OS[:, j * P:(j + 1) * P], ident[:, :])
                last.then_inc(oT_done, 1)

            pe.wait_ge(consts, 3)
            pe.wait_ge(presets, 1)
            a_units(0, 0, range(NA))
            turn_max(0)
            a_units(1, 1, range(AHEAD))
            for g, k in steps(pe, NG, 4):
                for n in range(NB):
                    turns = list(A_BESIDE[n])
                    for h in range(GH):
                        b_unit(g, k, n, h)
                        if h == GH - 1:
                            if n >= 1:
                                pv_step(g, k, n - 1)
                            if n == 1 and since(g, 1):
                                turn_output(g - 1, 1)
                            if n == MAX_T - 1:
                                turn_output(g, 0)
                            if n == MAX_T and until(g, 1, NG):
                                turn_max(g + 1)
                        for _ in range(-(-len(turns) // (GH - h))):
                            groups, v = turns.pop(0)
                            if until(g, groups, NG):
                                a_units(g + groups, (k + groups) % 4, [v])
                pv_step(g, k, NB - 1)
            turn_output(NG - 1, 1)


def output_stage(nc, S, X, ST, ident, w_out, b_out, x_dram):
    D, NT = S.D, S.NT
    with ExitStack() as c:
        def sb(name, shape, dt=F32):
            return c.enter_context(nc.sbuf_tensor(f"o_{name}", shape, dt))

        def ps(name):
            return [c.enter_context(nc.psum_tensor(f"o_{name}{i}", [P, 512], F32)) for i in range(4)]

        sem = semaphores(nc, c, "o")

        WR = sb("WR", [P, 2, D])
        Ws = [sb("Wh", [P, 2, D], F32R), sb("Wl", [P, 2, D], F32R)]
        BO = sb("BO", [P, D])
        AT = sb("AT", [P, 4, D])
        xs = [sb("ah", [P, 4, D], F32R), sb("al", [P, 4, D], F32R)]
        ST2 = ST[:, :, :].rearrange("p t s -> p (t s)")
        ps_x, ps_y = ps("ps_x"), ps("ps_y")
        X2 = X[:, :, :].rearrange("p t d -> p (t d)")
        XI = sb("XI", [P, NT, D])
        XI2 = XI[:, :, :].rearrange("p t d -> p (t d)")
        x_tiles = x_dram.rearrange("(t p) d -> p t d", p=P)
        NW = NT // 4
        x_in = [sem(f"x_in{i}") for i in range(NW)]

        weights_in = sem("weights_in")
        weights = sem("weights")
        row_ready = sem("row_ready")
        biased = sem("biased")
        xT_done = sem("xT_done")
        xh_done = sem("xh_done")
        xl_done = sem("xl_done")
        y_done = sem("y_done")
        x_done = sem("x_done")
        stats = sem("stats")

        block = c.enter_context(nc.Block())

        @block.sync
        def _(sp):
            sp.dma_start(WR[:, :, :], w_out.rearrange("(c p) f -> p c f", p=P)).then_inc(weights_in, 16)
            sp.dma_start(BO[:, :], b_out.rearrange("(a f) -> a f", a=1).to_broadcast([P, D])).then_inc(weights_in, 16)
            for w in range(NW):
                tiles = slice(4 * w, 4 * w + 4)
                sp.dma_start(XI[:, tiles, :], x_tiles[:, tiles, :]).then_inc(x_in[w], 16)

        @block.gpsimd
        def _(pool):
            pool.wait_ge(weights_in, 32)
            for w in range(NW):
                pool.wait_ge(x_in[w], 16)
                tiles = XI[:, 4 * w:4 * w + 4, :]
                nc.gpsimd.tensor_tensor(tiles, tiles, BO[:, :].unsqueeze(1).to_broadcast([P, 4, D]),
                                        ALU.add).then_inc(biased, 1)

        @block.scalar
        def _(act):
            def fix_rows(t, k):
                if since(t, 4):
                    act.wait_ge(xT_done, t - 3)
                nc.scalar.activation(AT[:, k, :], X2[:, ds(t * D, D)], ACT.Copy).then_inc(row_ready, 1)

            def x_high(t, k):
                act.wait_ge(xT_done, t + 1)
                if since(t, 4):
                    act.wait_ge(y_done, t - 3)
                nc.scalar.activation(xs[0][:, k, :], ps_x[k][:, 0:D], ACT.Copy).then_inc(xh_done, 1)

            for t in range(3):
                fix_rows(t, t)
            x_high(0, 0)
            for t, k in steps(act, NT, 4):
                if until(t, 3, NT):
                    fix_rows(t + 3, (k + 3) % 4)
                if until(t, 1, NT):
                    x_high(t + 1, (k + 1) % 4)

        @block.vector
        def _(dve):
            dve.wait_ge(weights_in, 32)
            nc.vector.tensor_copy(Ws[0][:, :, :], WR[:, :, :]).then_inc(weights, 1)
            dve.wait_ge(weights, 1)
            nc.vector.tensor_tensor(Ws[1][:, :, :], WR[:, :, :], Ws[0][:, :, :].bitcast(F32),
                                    ALU.subtract).then_inc(weights, 1)

            def x_low(t, k):
                dve.wait_ge(xh_done, t + 1)
                nc.vector.tensor_tensor(xs[1][:, k, :], ps_x[k][:, 0:D], xs[0][:, k, :].bitcast(F32),
                                        ALU.subtract).then_inc(xl_done, 1)

            def statistics(t):
                nc.vector.bn_stats(ST2[:, ds(6 * t, 6)], X2[:, ds(t * D, D)]).then_inc(stats, 1)

            x_low(0, 0)
            for t, k in steps(dve, NT, 4):
                if until(t, 1, NT):
                    x_low(t + 1, (k + 1) % 4)
                x_t = X2[:, ds(t * D, D)]
                dve.wait_ge(y_done, t + 1)
                if k == 0:
                    dve.wait_ge(biased, quarter(t, k) + 1)
                if since(t, 1):
                    dve.wait_ge(x_done, t)
                nc.vector.tensor_tensor(x_t, ps_y[k][:, 0:D], XI2[:, ds(t * D, D)], ALU.add).then_inc(x_done, 1)
                if since(t, 1):
                    statistics(t - 1)
            dve.wait_ge(x_done, NT)
            statistics(NT - 1)

        @block.tensor
        def _(pe):
            def transpose_x(t, k):
                pe.wait_ge(row_ready, t + 1)
                for c in range(2):
                    last = nc.tensor.transpose(ps_x[k][:, c * P:(c + 1) * P], AT[:, k, c * P:(c + 1) * P], ident[:, :])
                last.then_inc(xT_done, 1)

            transpose_x(0, 0)
            transpose_x(1, 1)
            pe.wait_ge(weights, 2)
            for t, k in steps(pe, NT, 4):
                if until(t, 2, NT):
                    transpose_x(t + 2, (k + 2) % 4)
                pe.wait_ge(xl_done, t + 1)
                if since(t, 4):
                    pe.wait_ge(x_done, t - 3)
                for i, (c, a, b) in enumerate(split_passes(2)):
                    last = nc.tensor.matmul(ps_y[k][:, 0:D], xs[a][:, k, c * P:(c + 1) * P],
                                            Ws[b][:, c, :], start=i == 0, stop=i == 5)
                last.then_inc(y_done, 1)




def macaron(nc, x, w_up, w_down, w_shared, gate, w_qkv, b_qk, b_v, w_out, b_out, out):
    S = Shapes(x, w_up, w_down, gate)
    x_rows = x.rearrange("b l d -> (b l) d")
    out_rows = out.rearrange("b l d -> (b l) d")
    with ExitStack() as ctx:
        xn_dram = nc.dram_tensor("xn_scratch", (S.T, S.D), F32, kind="Internal").ap()
        y_dram = nc.dram_tensor("y_scratch", (S.NJ * P, S.D), F32, kind="Internal").ap()
        X = ctx.enter_context(nc.sbuf_tensor("X", [P, S.NT, S.D], F32))
        ST = ctx.enter_context(nc.sbuf_tensor("ST", [P, S.NT, 6], F32))
        MV = ctx.enter_context(nc.sbuf_tensor("MV", [P, S.NT, 2], F32))
        ident = ctx.enter_context(nc.sbuf_tensor("ident", [P, P], F32))
        x_tiles = x_rows.rearrange("(t p) d -> p t d", p=P)
        x_in = [nc.alloc_semaphore(f"x_in{n}") for n in range(4)]
        stats = nc.alloc_semaphore("stats")

        def tiles(n):
            return slice(n * S.NT // 4, (n + 1) * S.NT // 4)

        ident_done = nc.alloc_semaphore("ident_done")
        with nc.Block() as block:
            @block.sync
            def _(sp):
                for n in range(4):
                    sp.dma_start(X[:, tiles(n), :], x_tiles[:, tiles(n), :]).then_inc(x_in[n], 16)

            @block.vector
            def _(dve):
                for n in range(4):
                    dve.wait_ge(x_in[n], 16)
                    for t in range(S.NT)[tiles(n)]:
                        last = nc.vector.bn_stats(ST[:, t, :], X[:, t, :])
                last.then_inc(stats, 1)
                dve.wait_ge(stats, 1)

            @block.gpsimd
            def _(pool):
                nc.gpsimd.memset(ident[:, :], 0.0).then_inc(ident_done, 1)
                pool.wait_ge(ident_done, 1)
                nc.gpsimd.affine_select(out=ident[:, :], in_=ident[:, :], compare_op=ALU.not_equal, fill=1.0,
                                        base=0, pattern=[[-1, P]], channel_multiplier=1).then_inc(ident_done, 1)
                pool.wait_ge(ident_done, 2)
        feed_forward(nc, "f1", S, X, ST, MV, ident, w_up, w_down, w_shared, gate, xn_dram, y_dram, None)
        attention(nc, S, X, ST, MV, ident, w_qkv, b_qk, b_v, w_out, b_out)
        feed_forward(nc, "f2", S, X, ST, MV, ident, w_up, w_down, w_shared, gate, xn_dram, y_dram, out_rows)


def kernel(**inputs):
    import numpy as np
    import concourse.bacc as _bacc
    from concourse.bass_utils import run_bass_kernel_spmd as _run

    a = {k[3:]: np.asarray(v) for k, v in inputs.items()}
    ff = a["ffn_exp_wg"].shape[1]
    d = a["attn_W_out"].shape[0]
    units = range(a["ffn_shared_wg"].shape[0] // ff)
    gates = [a["ffn_shared_wg"][s * ff:(s + 1) * ff] for s in units] + list(a["ffn_exp_wg"])
    ups = [a["ffn_shared_wu"][s * ff:(s + 1) * ff] for s in units] + list(a["ffn_exp_wu"])
    laid = {
        "x": a["attn_x"],
        "w_up": np.stack([np.concatenate([g, u]).T for g, u in zip(gates, ups)], axis=1),
        "w_down": a["ffn_exp_wd"].transpose(0, 2, 1),
        "w_shared": a["ffn_shared_wd"].T,
        "gate": a["ffn_gate_w"].T,
        "w_qkv": np.concatenate([a["attn_W_qkv"][:2 * d].reshape(2, 4, 2, 2, -1, d).transpose(1, 0, 2, 4, 3, 5)
                                 .reshape(2 * d, d), a["attn_W_qkv"][2 * d:]]).T,
        "b_qk": a["attn_b_qkv"][:2 * d].reshape(2, 4, 2, 2, -1).transpose(0, 2, 4, 3, 1).reshape(-1, 4),
        "b_v": a["attn_b_qkv"].reshape(3, -1)[2],
        "w_out": a["attn_W_out"].T,
        "b_out": a["attn_b_out"],
    }
    nc = _bacc.Bacc("TRN2", target_bir_lowering=False, num_devices=1)
    arrays, args = {}, []
    for name, v in laid.items():
        arrays[f"in_{name}"] = np.ascontiguousarray(v)
        args.append(nc.dram_tensor(f"in_{name}", v.shape, mybir.dt.from_np(v.dtype), kind="ExternalInput").ap())
    shape = a["attn_x"].shape
    args.append(nc.dram_tensor("out", shape, F32, kind="ExternalOutput").ap())
    macaron(nc, *args)
    r = _run(nc, [arrays], core_ids=[0])
    return r.results[0]["out"]
```
